# Optimizing a Trainium2 kernel written in Bass

```python
import numpy as np
import jax
import jax.numpy as jnp

def _softmax(x, axis=-1):
    return jax.nn.softmax(x, axis=axis)

def _gelu(x):
    return jax.nn.gelu(x, approximate=True)

def _silu(x):
    return jax.nn.silu(x)

def _sigmoid(x):
    return jax.nn.sigmoid(x)

def _layernorm(x, axis=-1, eps=1e-05):
    m = jnp.mean(x, axis=axis, keepdims=True)
    v = jnp.var(x, axis=axis, keepdims=True)
    return (x - m) / jnp.sqrt(v + eps)

def _scatter_add(tgt, idx, src, axis=0):
    return tgt.at[idx].add(src)

def _segment_sum(src, seg, n):
    return jax.ops.segment_sum(src, seg, n)
kernel_name = 'mk_adaln_d1_jaxref_r8_06757f'

def setup_inputs(seed: int=0):
    np.random.seed(seed)
    _w = jnp.asarray

    def _L0_attn_setup():
        import jax, jax.numpy as jnp
        import numpy as np
        HIDDEN_DIM = 256
        HEAD_NUM = 16
        HEAD_DIM = HIDDEN_DIM // HEAD_NUM
        key = jax.random.key(seed)
        ks = jax.random.split(key, 9)
        B, S, H = (2, 256, HIDDEN_DIM)
        scale = 1.0 / np.sqrt(H)
        X = jax.random.normal(ks[0], (B, S, H), dtype=jnp.float32)
        Wq = jax.random.normal(ks[1], (H, H), dtype=jnp.float32) * scale
        bq = jnp.zeros((H,), dtype=jnp.float32)
        Wk = jax.random.normal(ks[2], (H, H), dtype=jnp.float32) * scale
        bk = jnp.zeros((H,), dtype=jnp.float32)
        Wv = jax.random.normal(ks[3], (H, H), dtype=jnp.float32) * scale
        bv = jnp.zeros((H,), dtype=jnp.float32)
        Wo = jax.random.normal(ks[4], (H, H), dtype=jnp.float32) * scale
        bo = jnp.zeros((H,), dtype=jnp.float32)
        return {'X': X, 'Wq': Wq, 'bq': bq, 'Wk': Wk, 'bk': bk, 'Wv': Wv, 'bv': bv, 'Wo': Wo, 'bo': bo}
    _L0_attn_in = _L0_attn_setup()

    def _L0_ffn_setup():
        import jax, jax.numpy as jnp
        import numpy as np
        TOPK = 2
        HID, INTER, E, SHARED_INTER = (256, 176, 14, 352)
        key = jax.random.key(seed)
        ks = jax.random.split(key, 11)
        s = 0.02
        return {'x': jax.random.normal(ks[0], (4, 64, HID), jnp.float32), 'gate_w': jax.random.normal(ks[1], (E, HID), jnp.float32) * s, 'cls_w': jax.random.normal(ks[2], (E, HID), jnp.float32) * s, 'extra_scale': jax.random.normal(ks[3], (E,), jnp.float32) * 0.1, 'extra_bias': jax.random.normal(ks[4], (E,), jnp.float32) * 0.01, 'wg': jax.random.normal(ks[5], (E, INTER, HID), jnp.float32) * s, 'wu': jax.random.normal(ks[6], (E, INTER, HID), jnp.float32) * s, 'wd': jax.random.normal(ks[7], (E, HID, INTER), jnp.float32) * s, 'sg': jax.random.normal(ks[8], (SHARED_INTER, HID), jnp.float32) * s, 'su': jax.random.normal(ks[9], (SHARED_INTER, HID), jnp.float32) * s, 'sd': jax.random.normal(ks[10], (HID, SHARED_INTER), jnp.float32) * s}
    _L0_ffn_in = _L0_ffn_setup()
    _L0_c = _w((lambda *s: np.random.randn(*s).astype(np.float32) * 0.05)(8, 256))
    _L0_wmod = _w((lambda *s: np.random.randn(*s).astype(np.float32) * 0.05)(256, 6 * 256) * 256 ** (-0.5))
    _d = {'L0_attn_X': _L0_attn_in['X'], 'L0_attn_Wq': _L0_attn_in['Wq'], 'L0_attn_bq': _L0_attn_in['bq'], 'L0_attn_Wk': _L0_attn_in['Wk'], 'L0_attn_bk': _L0_attn_in['bk'], 'L0_attn_Wv': _L0_attn_in['Wv'], 'L0_attn_bv': _L0_attn_in['bv'], 'L0_attn_Wo': _L0_attn_in['Wo'], 'L0_attn_bo': _L0_attn_in['bo'], 'L0_ffn_gate_w': _L0_ffn_in['gate_w'], 'L0_ffn_cls_w': _L0_ffn_in['cls_w'], 'L0_ffn_extra_scale': _L0_ffn_in['extra_scale'], 'L0_ffn_extra_bias': _L0_ffn_in['extra_bias'], 'L0_ffn_wg': _L0_ffn_in['wg'], 'L0_ffn_wu': _L0_ffn_in['wu'], 'L0_ffn_wd': _L0_ffn_in['wd'], 'L0_ffn_sg': _L0_ffn_in['sg'], 'L0_ffn_su': _L0_ffn_in['su'], 'L0_ffn_sd': _L0_ffn_in['sd'], 'L0_c': _L0_c, 'L0_wmod': _L0_wmod}
    _x0 = _d['L0_attn_X']
    _d['L0_attn_X'] = jax.random.normal(jax.random.fold_in(jax.random.key(seed), 1), (8, 256, 256), dtype=_x0.dtype)
    del _x0
    return _d

def reference(L0_attn_X, L0_attn_Wq, L0_attn_bq, L0_attn_Wk, L0_attn_bk, L0_attn_Wv, L0_attn_bv, L0_attn_Wo, L0_attn_bo, L0_ffn_gate_w, L0_ffn_cls_w, L0_ffn_extra_scale, L0_ffn_extra_bias, L0_ffn_wg, L0_ffn_wu, L0_ffn_wd, L0_ffn_sg, L0_ffn_su, L0_ffn_sd, L0_c, L0_wmod):

    def _L0_attn_ref(X, Wq, bq, Wk, bk, Wv, bv, Wo, bo):
        import jax, jax.numpy as jnp
        import numpy as np
        HIDDEN_DIM = 256
        HEAD_NUM = 16
        HEAD_DIM = HIDDEN_DIM // HEAD_NUM
        B, S, H = X.shape
        Q = X @ Wq + bq
        K = X @ Wk + bk
        V = X @ Wv + bv
        q = Q.reshape(B, S, HEAD_NUM, HEAD_DIM).transpose(0, 2, 1, 3)
        k = K.reshape(B, S, HEAD_NUM, HEAD_DIM).transpose(0, 2, 1, 3)
        v = V.reshape(B, S, HEAD_NUM, HEAD_DIM).transpose(0, 2, 1, 3)
        scores = jnp.einsum('bhqd,bhkd->bhqk', q, k) / jnp.sqrt(jnp.float32(HEAD_DIM))
        attn = jax.nn.softmax(scores, axis=-1)
        out = jnp.einsum('bhqk,bhkd->bhqd', attn, v)
        out = out.transpose(0, 2, 1, 3).reshape(B, S, H)
        return out @ Wo + bo

    def _L0_ffn_ref(x, gate_w, cls_w, extra_scale, extra_bias, wg, wu, wd, sg, su, sd):
        import jax, jax.numpy as jnp
        import numpy as np
        TOPK = 2
        HID, INTER, E, SHARED_INTER = (256, 176, 14, 352)
        shape = x.shape
        d = shape[-1]
        xf = x.reshape(-1, d)
        T = xf.shape[0]
        n_exp = gate_w.shape[0]
        logits = xf @ cls_w.T * jax.nn.silu(xf @ gate_w.T)
        scores = jax.nn.softmax(jnp.abs(logits).astype(jnp.float32), axis=-1)
        biased = scores + extra_bias[None, :]
        _, idx = jax.lax.top_k(biased, TOPK)
        orig = 1.0 + scores * extra_scale[None, :]
        w = jnp.take_along_axis(orig, idx, axis=1).astype(x.dtype)
        combine = jnp.zeros((T, n_exp), x.dtype).at[jnp.arange(T)[:, None], idx].add(w)
        g = jax.nn.silu(jnp.einsum('td,efd->etf', xf, wg))
        u = jnp.einsum('td,efd->etf', xf, wu)
        o = jnp.einsum('etf,edf->etd', g * u, wd)
        y = jnp.einsum('etd,te->td', o, combine)
        z = jax.nn.silu(xf @ sg.T) * (xf @ su.T) @ sd.T
        return (y + z).reshape(shape)
    x = L0_attn_X
    mod = (_silu(L0_c) @ L0_wmod).reshape(L0_c.shape[0], 6, 1, -1)
    sa, ca, ga, sb, cb, gb = (mod[:, 0], mod[:, 1], mod[:, 2], mod[:, 3], mod[:, 4], mod[:, 5])
    ga = (2 * (ga >= 0) - 1) * jnp.maximum(jnp.abs(ga), 0.25)
    gb = (2 * (gb >= 0) - 1) * jnp.maximum(jnp.abs(gb), 0.25)
    h = _layernorm(x, axis=-1) * (1 + ca) + sa
    x = x + ga * _L0_attn_ref(h, L0_attn_Wq, L0_attn_bq, L0_attn_Wk, L0_attn_bk, L0_attn_Wv, L0_attn_bv, L0_attn_Wo, L0_attn_bo)
    h = _layernorm(x, axis=-1) * (1 + cb) + sb
    x = x + gb * _L0_ffn_ref(h, L0_ffn_gate_w, L0_ffn_cls_w, L0_ffn_extra_scale, L0_ffn_extra_bias, L0_ffn_wg, L0_ffn_wu, L0_ffn_wd, L0_ffn_sg, L0_ffn_su, L0_ffn_sd)
    return x

_drawn_inputs = setup_inputs


def setup_inputs(seed=0):
    import zlib

    import numpy as np

    out = dict(_drawn_inputs(seed))
    spreads = {'L0_attn_bq': (0.0, 0.8),
     'L0_attn_bk': (0.0, 0.8),
     'L0_attn_bv': (0.0, 0.315),
     'L0_attn_bo': (0.0, 0.331)}
    factors = {'L0_ffn_gate_w': 8.0,
     'L0_ffn_cls_w': 8.0,
     'L0_ffn_extra_scale': 8.0,
     'L0_ffn_extra_bias': 8.0,
     'L0_ffn_wg': 8.0,
     'L0_ffn_wu': 8.0,
     'L0_ffn_wd': 8.0,
     'L0_ffn_sg': 8.0,
     'L0_ffn_su': 8.0,
     'L0_ffn_sd': 8.0}
    for name, (base, spread) in spreads.items():
        noise = np.random.default_rng([zlib.crc32(name.encode()), seed]).standard_normal(out[name].shape)
        drawn = base * np.exp(spread * noise) if base else spread * noise
        out[name] = jnp.asarray(drawn.astype(out[name].dtype))
    for name, factor in factors.items():
        out[name] = (out[name] * factor).astype(out[name].dtype)
    return out
```

```python
from contextlib import ExitStack

import concourse.bass as bass
import concourse.mybir as mybir
import numpy as np

F32, F32R, I32, U32 = mybir.dt.float32, mybir.dt.float32r, mybir.dt.int32, mybir.dt.uint32
ACT = mybir.ActivationFunctionType
ALU = mybir.AluOpType
AX = mybir.AxisListType
ds = bass.ds

P = 128
BATCH, SEQ, HID = 8, 256, 256
HEADS, HDIM = 16, 16
T = BATCH * SEQ
TILES = T // P
TPB = SEQ // P
KC = HID // P
EXPERTS, INTER, SHARED = 14, 176, 352
HALF = INTER // 2
HPAD = 96
BLOCKS = (2 * T + EXPERTS * (P - 1)) // P
SLOTS = BLOCKS * P
UNROLL = 3
assert BLOCKS % UNROLL == 0
CHUNK = 512
CT = CHUNK // P
SCORE = 3 * HDIM
MROW = 96
STACK = MROW + 2
EPS = 1e-5
HEAD, DMA_HEAD = 3, 16
PADS = UNROLL + 2
CONSTS = 8
SHARED_ROWS = [P, P, SHARED - 2 * P]
UNITS_AFTER = [0, 0, 0, 0, 0, 1, 1, 1, 1, 2, 2, 2, 2, 2, 1, 1]
assert sum(UNITS_AFTER) == 16


def adaln_block(nc, x_d, bqk_d, wq_d, wk_d, wv_d, bv_d, wo_d, bo_d, route_d, escale_d, ebias_d,
                wgu_d, wd_d, sgu_d, sd_d, ct_d, wmod_d, out_d, debug=None):
    mod_scr = nc.dram_tensor("mod_scr", (BATCH, 4 * HID), F32, kind="Internal").ap()
    scr = [nc.dram_tensor(f"stack_scr{i}", (2, HEADS, 2, HDIM, SEQ), F32, kind="Internal").ap() for i in range(2)]
    slots_in = nc.dram_tensor("slots_in", (SLOTS, HID), F32, kind="Internal").ap()
    slots_out = nc.dram_tensor("slots_out", (SLOTS, HID), F32, kind="Internal").ap()

    ctx = ExitStack()
    phase1, phase2 = ExitStack(), ExitStack()

    def sb(name, shape, dt=F32, where=None):
        return (where or ctx).enter_context(nc.sbuf_tensor(name, shape, dt))

    def flag(name):
        return ctx.enter_context(nc.semaphore(name))

    with ctx:
        x = sb("x", [P, TILES, HID])
        h2 = sb("h2", [P, TILES, HID])
        ident = sb("ident", [P, P])
        modb = sb("modb", [P, BATCH, 4, HID])
        stats = sb("stats", [P, TILES, 6])
        mv = sb("mv", [P, TILES, 2])
        rstd = sb("rstd", [P, TILES])
        neghalf = sb("neghalf", [P, TILES])
        route_w = sb("route_w", [P, KC, 2 * EXPERTS])
        sgu = sb("sgu", [P, KC, 2 * SHARED])
        sd = sb("sd", [P, 3, HID])
        escale = sb("escale", [P, EXPERTS])
        ebias = sb("ebias", [P, EXPERTS])

        def sb1(name, shape, dt=F32):
            return sb(name, shape, dt, phase1)

        qst = [sb1(f"qst{i}", [P, HEADS, SEQ], F32R) for i in range(2)]
        kst = [sb1(f"kst{i}", [P, HEADS, SEQ], F32R) for i in range(2)]
        probs = sb1("probs", [P, 8, TPB, SEQ])
        vst = [sb1(f"vst{i}", [P, TPB, HEADS, 32]) for i in range(2)]
        wq, wk, wv, wo = (sb1(n, [P, KC, HID]) for n in ("wq", "wk", "wv", "wo"))
        wmod = probs[:].rearrange("p j t q -> p (j t q)")[:, 0:KC * 6 * HID].rearrange("p (k n) -> p k n", k=KC)
        ct = sb1("ct", [P, KC, BATCH])
        esc = sb1("esc", [P, KC, BATCH])
        rec = sb1("rec", [P, KC, BATCH])
        siluc = sb1("siluc", [P, KC, BATCH])
        zero = sb1("zero", [P, HID])
        sa = sb1("sa", [P, KC, BATCH])
        ca1 = sb1("ca1", [P, KC, BATCH])
        modr = h2[0:BATCH, 0:6, :].rearrange("b m d -> b (m d)")
        sgn = h2[0:BATCH, 6:8, :]
        minus = h2[0:BATCH, 8:10, :]
        bqk = sb1("bqk", [P, 4])
        bvb = sb1("bvb", [P, HID])
        bob = sb1("bob", [P, HID])
        z1 = sb1("z1", [P, TPB, HID])
        hT = sb1("hT", [P, KC, SEQ])
        qkf = sb1("qkf", [P, 4, SEQ])
        qks = sb1("qks", [P, 2, 4, SEQ], F32R)
        mx = sb1("mx", [P, TPB, HEADS])
        mneg = sb1("mneg", [HEADS, SEQ])
        mrow = sb1("mrow", [HEADS, 2, SEQ], F32R)
        OT = h2[:, 10:14, :]
        rs = sb1("rs", [P, TPB, HEADS])
        On = h2[:, 14:16, :]
        OnT = sb1("OnT", [P, KC, SEQ])
        att = sb1("att", [P, TPB, HID])
        att2 = h2[:, 8:10, :]
        phase1.close()

        def sb2(name, shape, dt=F32):
            return sb(name, shape, dt, phase2)

        wgu = sb2("wgu", [P, KC, EXPERTS, 2 * INTER])
        wd = sb2("wd", [HPAD, 2, EXPERTS, HID])
        zsh = sb2("zsh", [P, TILES, HID])
        h2c = sb2("h2c", [P, CT, HID])
        h2T = sb2("h2T", [P, KC, CHUNK])
        ssil = sb2("ssil", [P, CHUNK])
        sgT = sb2("sgT", [P, 3, CHUNK])
        lg = sb2("lg", [P, TILES, 2 * EXPERTS])
        r3 = [sb2(f"r{i}", [P, TILES, EXPERTS]) for i in range(8)]
        c1 = [sb2(f"c{i}", [P, TILES]) for i in range(8)]
        iotaf = sb2("iotaf", [P, EXPERTS])
        iotai = sb2("iotai", [P, EXPERTS], I32)
        bnumi = sb2("bnumi", [P, BLOCKS], I32)
        tri = sb2("tri", [P, P])
        ones = sb2("ones", [P, P])
        cnt = sb2("cnt", [P, TILES + 1, EXPERTS])
        blk = sb2("blk", [P, 4, EXPERTS])
        blki = sb2("blki", [P, EXPERTS], I32)
        cend = sb2("cend", [P, EXPERTS + 1])
        bnum = sb2("bnum", [P, BLOCKS])
        bcmp = sb2("bcmp", [P, BLOCKS, EXPERTS])
        eidf = sb2("eidf", [P, BLOCKS])
        eid = sb2("eid", [P, BLOCKS], I32)
        slotf = sb2("slotf", [P, 2, TILES])
        slot = sb2("slot", [P, 2, TILES], U32)
        wsel = sb2("wsel", [P, 2, TILES])
        hb = [sb2(f"hb{i}", [P, HID]) for i in range(UNROLL)]
        hbT = [sb2(f"hbT{i}", [P, KC, P]) for i in range(UNROLL)]
        bsil = [sb2(f"bsil{i}", [P, INTER]) for i in range(UNROLL)]
        hg = [sb2(f"hg{i}", [P, 2, HPAD]) for i in range(UNROLL)]
        hgT = [sb2(f"hgT{i}", [HPAD, 2, P]) for i in range(UNROLL)]
        ob = [sb2(f"ob{i}", [P, HID]) for i in range(UNROLL)]
        picked = wgu[:].rearrange("p k e n -> p (k e n)")[:, 0:TILES * 2 * HID].rearrange("p (t c d) -> p t c d", t=TILES, c=2)
        phase2.close()

        bank = [ctx.enter_context(nc.psum_tensor(f"bank{i}", [P, 512], F32)) for i in range(8)]
        ST, SM, PV, MISC = bank[0:2], bank[2:4], bank[4:6], bank[6:8]

        x_in = flag("x_in")
        small_in = flag("small_in")
        attn_w_in = flag("attn_w_in")
        ffn_w_in = flag("ffn_w_in")
        const_done = flag("const_done")
        ident_step, zero_set = flag("ident_step"), flag("zero_set")
        slots_zeroed, tri_step = flag("slots_zeroed"), flag("tri_step")
        stat_step = flag("stat_step")
        rstd_done = flag("rstd_done")
        esc_done = flag("esc_done")
        siluc_step = flag("siluc_step")
        ps_mod = flag("ps_mod")
        mod_raw, floor_step, modr_done, cols_done = flag("mod_raw"), flag("floor_step"), flag("modr_done"), flag("cols_done")
        mod_stored = flag("mod_stored")
        modb_in = flag("modb_in")
        z1_done = flag("z1_done")
        psT, psQ, psK, psV = flag("psT"), flag("psQ"), flag("psK"), flag("psV")
        hT_done = flag("hT_done")
        q_evac, k_evac, v_done = flag("q_evac"), flag("k_evac"), flag("v_done")
        split_hi, split_lo = flag("split_hi"), flag("split_lo")
        stored, loaded = flag("stored"), flag("loaded")
        psMax, max_done = flag("psMax"), flag("max_done")
        psM, mT_evac, m_hi, m_lo = flag("psM"), flag("mT_evac"), flag("m_hi"), flag("m_lo")
        mrow_in = flag("mrow_in")
        psS, exp_done = flag("psS"), flag("exp_done")
        psPV, pv_evac = flag("psPV"), flag("pv_evac")
        psOT, rs_done, on_done = flag("psOT"), flag("rs_done"), flag("on_done")
        psOnT, onT_evac = flag("psOnT"), flag("onT_evac")
        psWo, wo_evac = flag("psWo"), flag("wo_evac")
        ga_done, x1_done = flag("ga_done"), flag("x1_done")
        stat2_step, rstd2_done, z2_done, h2_step = flag("stat2_step"), flag("rstd2_done"), flag("z2_done"), flag("h2_step")
        h2c_done, h2_kept = flag("h2c_done"), flag("h2_kept")
        psT2, h2T_a, h2T_v = flag("psT2"), flag("h2T_a"), flag("h2T_v")
        ps_r, r_evac = flag("ps_r"), flag("r_evac")
        ps_gu, silu_done, sg_mul = flag("ps_gu"), flag("silu_done"), flag("sg_mul")
        ps_dn, z_a, z_v = flag("ps_dn"), flag("z_a"), flag("z_v")
        route_step, route_silu, route_exp = flag("route_step"), flag("route_silu"), flag("route_exp")
        masks_done, ps_cnt, slots_known, iota_step = flag("masks_done"), flag("ps_cnt"), flag("slots_known"), flag("iota_step")
        scattered = flag("scattered")
        hb_in = [flag(f"hb_in{u}") for u in range(UNROLL)]
        ob_out = [flag(f"ob_out{u}") for u in range(UNROLL)]
        psTb, hbT_done, psU, bsil_done = flag("psTb"), flag("hbT_done"), flag("psU"), flag("bsil_done")
        hg_done, psG, hgT_done, psD, ob_done = flag("hg_done"), flag("psG"), flag("hgT_done"), flag("psD"), flag("ob_done")
        pads_done = flag("pads_done")
        picked_in = [flag(f"picked_in{t}") for t in range(TILES)]
        sum_step, result_done, stored_out = flag("sum_step"), flag("result_done"), flag("stored_out")
        ahead = [exp_done, h2_kept, hbT_done, hg_done, mT_evac, m_lo, ob_done, onT_evac, psD, psG, psM, psOT, psOnT, psPV, psT, psT2, psU, psV, psWo, ps_dn, ps_gu, pv_evac, sg_mul, split_lo, wo_evac, x1_done, z_a, z_v]
        dma_ahead = [*ob_out, stored, mrow_in]

        block = ctx.enter_context(nc.Block())
        LAST = BATCH - 1

        def batches(eng, first, body):
            first()
            with eng.Fori(0, (BATCH - 2) // 2) as pair:
                for par in range(2):
                    body(pair * 2 + par, par, True)
            body(BATCH - 2, 0, True)
            body(BATCH - 1, 1, False)

        @block.sync
        def _(sp):
            for f in ahead:
                sp.sem_inc(f, HEAD)
            for f in dma_ahead:
                sp.sem_inc(f, DMA_HEAD)
            sp.dma_start(ct[:], ct_d.rearrange("(k p) b -> p k b", p=P)).then_inc(small_in, 16)
            sp.dma_start(wmod, wmod_d.rearrange("(k p) n -> p k n", p=P)).then_inc(small_in, 16)
            for q in range(4):
                n = TILES // 4
                sp.dma_start(x[:, n * q:n * q + n, :], x_d[n * q * P:n * (q + 1) * P, :].rearrange(
                    "(t p) d -> p t d", p=P)).then_inc(x_in, 16)
            sp.dma_start(bqk[:], bqk_d).then_inc(attn_w_in, 16)
            for tile, src in ((wq, wq_d), (wk, wk_d), (wv, wv_d), (wo, wo_d)):
                sp.dma_start(tile[:], src.rearrange("(k p) n -> p k n", p=P)).then_inc(attn_w_in, 16)
            for tile, src, n in ((bvb, bv_d, HID), (bob, bo_d, HID), (escale, escale_d, EXPERTS), (ebias, ebias_d, EXPERTS)):
                sp.dma_start(tile[:], src.rearrange("(o n) -> o n", o=1).to_broadcast((P, n))).then_inc(attn_w_in, 16)
            sp.dma_start(route_w[:], route_d.rearrange("(k p) n -> p k n", p=P)).then_inc(attn_w_in, 16)
            sp.dma_start(sgu[:], sgu_d.rearrange("(k p) n -> p k n", p=P)).then_inc(attn_w_in, 16)
            for m, rows in enumerate(SHARED_ROWS):
                sp.dma_start(sd[0:rows, m, :], sd_d[m * P:m * P + rows, :]).then_inc(attn_w_in, 16)
            sp.wait_ge(modr_done, 3)
            sp.dma_start(mod_scr, modr[:, 2 * HID:6 * HID]).then_inc(mod_stored, 16)
            sp.wait_ge(mod_stored, 16)
            sp.dma_start(modb[:].rearrange("p b m d -> p (b m d)"), mod_scr.rearrange("b n -> (b n)").rearrange(
                "(o n) -> o n", o=1).to_broadcast((P, BATCH * 4 * HID))).then_inc(modb_in, 16)

            def stacks(b, par):
                sp.wait_ge(split_lo, HEAD + b + 1)
                for side in range(2):
                    for part in range(2):
                        kind = part if side else 1 - part
                        for c in range(2):
                            sp.dma_start(scr[par][side, 8 * c:8 * c + 8, kind, :, :],
                                         qks[:, part, 2 * side + c, :].bitcast(F32)).then_inc(stored, 16)
                sp.wait_ge(stored, DMA_HEAD + (b + 1) * 128)
                q = scr[par][0].rearrange("h k d t -> (k d) h t")
                k = scr[par][1].rearrange("h k d t -> (k d) h t")
                for dst, src in ((qst[par][0:32], q), (qst[par][32:48], q[16:32]),
                                 (kst[par][16:48], k), (kst[par][0:16], k[0:16])):
                    sp.dma_start(dst.bitcast(F32), src).then_inc(loaded, 16)
                sp.wait_ge(loaded, (b + 1) * 64)

            def maxima(b, par):
                sp.wait_ge(m_lo, HEAD + b + 1)
                for part in range(2):
                    sp.dma_start(qst[par][MROW + part:MROW + part + 1].bitcast(F32),
                                 mrow[:, part, :].bitcast(F32)).then_inc(mrow_in, 16)

            def first():
                sp.wait_ge(const_done, CONSTS)
                stacks(0, 0)
                maxima(0, 0)

            def body(b, par, more):
                if more:
                    stacks(b + 1, 1 - par)
                    maxima(b + 1, 1 - par)

            batches(sp, first, body)
            sp.wait_ge(x1_done, HEAD + BATCH)
            sp.wait_ge(mrow_in, DMA_HEAD + 32 * BATCH)
            sp.wait_ge(slots_zeroed, 16)
            sp.wait_ge(pads_done, PADS)
            for k in range(KC):
                sp.dma_start(wgu[:, k], wgu_d[k * P:(k + 1) * P]).then_inc(ffn_w_in, 16)
            for s in range(2):
                sp.dma_start(wd[0:HALF, s], wd_d[:, s * HALF:(s + 1) * HALF, :].rearrange("e p n -> p e n")).then_inc(ffn_w_in, 16)
            sp.wait_ge(scattered, 32 * TILES)

            def load_block(n, u):
                sp.dma_start(hb[u][:], slots_in[ds(n * P, P), :]).then_inc(hb_in[u], 16)

            def store_block(n, u):
                sp.wait_ge(ob_done, HEAD + n + 1)
                sp.dma_start(slots_out[ds(n * P, P), :], ob[u][:]).then_inc(ob_out[u], 16)

            for u in range(UNROLL):
                load_block(u, u)
            with sp.Fori(0, BLOCKS // UNROLL - 1) as i:
                for u in range(UNROLL):
                    n = i * UNROLL + u
                    sp.wait_ge(psTb, n + 1)
                    load_block(n + UNROLL, u)
                    store_block(n, u)
            for u in range(UNROLL):
                store_block(BLOCKS - UNROLL + u, u)
            for t in range(0, TILES, 2):
                sp.wait_ge(result_done, t + 2)
                sp.dma_start(out_d[t * P:(t + 2) * P, :].rearrange("(t p) d -> p t d", p=P), x[:, t:t + 2, :]
                             ).then_inc(stored_out, 16)
            sp.wait_ge(stored_out, 8 * TILES)
            if debug is not None:
                dbg = flag("dbg")
                sp.dma_start(debug.rearrange("(t p) d -> p t d", p=P), h2[:]).then_inc(dbg, 16)
                sp.wait_ge(dbg, 16)

        @block.tensor
        def _(pe):
            pe.wait_ge(siluc_step, 3)
            pe.wait_ge(small_in, 32)
            for n in range(3):
                for k in range(KC):
                    mm = pe.matmul(bank[n][0:BATCH, :], siluc[:, k, :], wmod[:, k, n * 512:n * 512 + 512],
                                   start=(k == 0), stop=(k == KC - 1))
                mm.then_inc(ps_mod, 1)
            for n in range(2 * KC):
                for k in range(KC):
                    mm = pe.matmul(bank[3][:, n * BATCH:(n + 1) * BATCH], wmod[:, k, n * P:(n + 1) * P], siluc[:, k, :],
                                   start=(k == 0), stop=(k == KC - 1))
            mm.then_inc(ps_mod, 1)
            pe.wait_ge(mod_raw, 3)
            pe.wait_ge(cols_done, 3)
            pe.wait_ge(const_done, CONSTS)
            pe.wait_ge(attn_w_in, 16 * 14)

            def project(b, par):
                pe.wait_ge(z1_done, (b + 1) * 2)
                pe.wait_ge(onT_evac, HEAD + b - 1)
                for t in range(TPB):
                    for k in range(KC):
                        mm = pe.transpose(MISC[0][:, k * SEQ + t * P:k * SEQ + t * P + P], z1[:, t, k * P:k * P + P], ident[:])
                mm.then_inc(psT, 1)
                pe.wait_ge(hT_done, (b + 1) * 2)
                pe.wait_ge(wo_evac, HEAD + b - 1)
                for w, out, ready in ((wq, MISC[1], psQ), (wk, MISC[0], psK)):
                    for c in range(2):
                        for k in range(KC):
                            mm = pe.matmul(out[:, c * SEQ:(c + 1) * SEQ], w[:, k, c * P:c * P + P], hT[:, k, :],
                                           start=(k == 0), stop=(k == KC - 1))
                    mm.then_inc(ready, 1)
                pe.wait_ge(q_evac, (b + 1) * 2)
                for t in range(TPB):
                    for k in range(KC):
                        mm = pe.matmul(MISC[1][:, t * HID:(t + 1) * HID], hT[:, k, t * P:t * P + P], wv[:, k, :],
                                       start=(k == 0), stop=(k == KC - 1))
                mm.then_inc(psV, 1)

            def max_unit(b, par, u):
                pair, qt = u // 2, u % 2
                if u == 0:
                    pe.wait_ge(loaded, (b + 1) * 64)
                if pair == 0:
                    pe.wait_ge(mT_evac, HEAD + b * 2 + (qt - 1))
                else:
                    pe.wait_ge(max_done, b * 16 + (u - 1))
                for i in range(2):
                    h = 2 * pair + i
                    mm = pe.matmul(SM[qt][:, i * SEQ:(i + 1) * SEQ], qst[par][0:MROW, h, qt * P:qt * P + P],
                                   kst[par][0:MROW, h, :], start=True, stop=True)
                mm.then_inc(psMax, 1)

            def turn_maxima(b):
                pe.wait_ge(max_done, (b + 1) * 16)
                for qt in range(TPB):
                    pe.transpose(SM[qt][0:HEADS, 0:P], mx[:, qt, :], ident[:]).then_inc(psM, 1)

            def scores(b, par, h):
                if h == 0:
                    pe.wait_ge(mrow_in, DMA_HEAD + (b + 1) * 32)
                pe.wait_ge(exp_done, HEAD + b * 16 + (h - 1))
                for kt in range(TPB):
                    mm = pe.matmul(ST[h % 2][:, kt * SEQ:(kt + 1) * SEQ], kst[par][0:STACK, h, kt * P:kt * P + P],
                                   qst[par][0:STACK, h, :], start=True, stop=True)
                mm.then_inc(psS, 1)

            def weigh(b, par, g):
                if g == 0:
                    pe.wait_ge(v_done, (b + 1) * 2)
                if g % 2 == 0:
                    pe.wait_ge(pv_evac, HEAD + b * 2 + (g // 2 - 1))
                pe.wait_ge(exp_done, HEAD + b * 16 + (4 * g + 4))
                for kt in range(TPB):
                    for j in range(4):
                        mm = pe.matmul(PV[g // 2][32 * j:32 * j + 32, (g % 2) * SEQ:(g % 2 + 1) * SEQ],
                                       vst[par][:, kt, 4 * g + j, :], probs[:, (g % 2) * 4 + j, kt, :],
                                       start=(kt == 0), stop=(kt == TPB - 1))
                mm.then_inc(psPV, 1)

            def output(b, par, more):
                pe.wait_ge(pv_evac, HEAD + (b + 1) * 2)
                for qt in range(TPB):
                    if more and qt == 0:
                        pe.wait_ge(k_evac, (b + 2) * 2)
                    elif more:
                        pe.wait_ge(v_done, (b + 2) * 2)
                    elif qt == 0:
                        pe.wait_ge(onT_evac, HEAD + b)
                    else:
                        pe.wait_ge(wo_evac, HEAD + b)
                    for g in range(4):
                        mm = pe.transpose(MISC[qt][:, g * P:(g + 1) * P], OT[:, g, qt * P:qt * P + P], ident[:])
                    mm.then_inc(psOT, 1)
                pe.wait_ge(on_done, (b + 1) * 2)
                for t in range(TPB):
                    for k in range(KC):
                        mm = pe.transpose(MISC[0][:, k * SEQ + t * P:k * SEQ + t * P + P], On[:, t, k * P:k * P + P], ident[:])
                mm.then_inc(psOnT, 1)
                pe.wait_ge(onT_evac, HEAD + b + 1)
                for t in range(TPB):
                    for k in range(KC):
                        mm = pe.matmul(MISC[1][:, t * HID:(t + 1) * HID], OnT[:, k, t * P:t * P + P], wo[:, k, :],
                                       start=(k == 0), stop=(k == KC - 1))
                mm.then_inc(psWo, 1)

            def first():
                project(0, 0)
                for u in range(16):
                    max_unit(0, 0, u)
                turn_maxima(0)

            def body(b, par, more):
                if more:
                    project(b + 1, 1 - par)
                u = 0
                for h in range(HEADS):
                    if more:
                        for _ in range(UNITS_AFTER[h]):
                            max_unit(b + 1, 1 - par, u)
                            u += 1
                    scores(b, par, h)
                    if h % 4 == 3 and h > 3:
                        weigh(b, par, h // 4 - 1)
                weigh(b, par, 3)
                if more:
                    turn_maxima(b + 1)
                output(b, par, more)

            batches(pe, first, body)

            with pe.Fori(0, TILES // CT) as c:
                pe.wait_ge(h2c_done, c * 2 + 2)
                pe.wait_ge(z_v, HEAD + c)
                pe.wait_ge(z_a, HEAD + c)
                for k in range(KC):
                    for t in range(CT):
                        mm = pe.transpose(bank[k][:, t * P:(t + 1) * P], h2c[:, t, k * P:k * P + P], ident[:])
                    mm.then_inc(psT2, 1)
                pe.wait_ge(h2T_a, c + 1)
                pe.wait_ge(h2T_v, c + 1)
                for t in range(CT):
                    for k in range(KC):
                        mm = pe.matmul(bank[0][:, t * 2 * EXPERTS:(t + 1) * 2 * EXPERTS], h2T[:, k, t * P:t * P + P],
                                       route_w[:, k, :], start=(k == 0), stop=(k == KC - 1))
                mm.then_inc(ps_r, 1)
                for m, rows in enumerate(SHARED_ROWS):
                    pe.wait_ge(sg_mul, HEAD + c * 3 + (m - 2))
                    for side in range(2):
                        at = side * SHARED + m * P
                        for k in range(KC):
                            mm = pe.matmul(bank[2 + 2 * m + side][0:rows, :], sgu[:, k, at:at + rows], h2T[:, k, :],
                                           start=(k == 0), stop=(k == KC - 1))
                    mm.then_inc(ps_gu, 1)
                pe.wait_ge(sg_mul, HEAD + c * 3 + 3)
                pe.wait_ge(r_evac, c + 1)
                for half in range(2):
                    for t in range(2):
                        tok = (2 * half + t) * P
                        for m, rows in enumerate(SHARED_ROWS):
                            mm = pe.matmul(bank[1 - half][:, t * HID:(t + 1) * HID], sgT[0:rows, m, tok:tok + P],
                                           sd[0:rows, m, :], start=(m == 0), stop=(m == 2))
                    mm.then_inc(ps_dn, 1)

            pe.wait_ge(masks_done, 1)
            pe.wait_ge(tri_step, 3)
            pe.wait_ge(z_v, HEAD + TILES // CT)
            pe.wait_ge(z_a, HEAD + TILES // CT)
            n = TILES * EXPERTS
            for at, weights in ((0, tri), (1, ones)):
                pe.matmul(bank[at][:, 0:n], weights[:], r3[0][:].rearrange("p t e -> p (t e)"), start=True, stop=True
                          ).then_inc(ps_cnt, 1)

            pe.wait_ge(ffn_w_in, 64)
            pe.wait_ge(pads_done, PADS)
            pe.wait_ge(slots_known, 1)

            def expand(i, u):
                n = i * UNROLL + u
                pe.wait_ge(hb_in[u], (i + 1) * 16)
                pe.wait_ge(hbT_done, HEAD + (n, n - 2, n - 1)[u])
                for k in range(KC):
                    mm = pe.transpose(bank[u % 2][:, k * P:(k + 1) * P], hb[u][:, k * P:k * P + P], ident[:])
                mm.then_inc(psTb, 1)
                e = pe.value_load(eid[0:1, ds(n, 1)], min_val=0, max_val=EXPERTS - 1)
                pe.wait_ge(hbT_done, HEAD + n + 1)
                pe.wait_ge(hg_done, HEAD + n - 2)
                for k in range(KC):
                    mm = pe.matmul(bank[2 + u][:, 0:2 * INTER], hbT[u][:, k, :],
                                   wgu[:, k, ds(e, 1), :].rearrange("p o n -> p (o n)"), start=(k == 0), stop=(k == KC - 1))
                mm.then_inc(psU, 1)
                return e

            def contract(i, u, e):
                n = i * UNROLL + u
                pe.wait_ge(hg_done, HEAD + n + 1)
                pe.wait_ge(ob_done, HEAD + n - 2)
                for s in range(2):
                    mm = pe.transpose(bank[5 + u][0:HPAD, s * P:(s + 1) * P], hg[u][:, s, :], ident[:])
                mm.then_inc(psG, 1)
                pe.wait_ge(hgT_done, n + 1)
                for s in range(2):
                    mm = pe.matmul(bank[5 + u][:, HID:2 * HID], hgT[u][:, s, :],
                                   wd[:, s, ds(e, 1), :].rearrange("p o n -> p (o n)"), start=(s == 0), stop=(s == 1))
                mm.then_inc(psD, 1)

            with pe.Fori(0, BLOCKS // UNROLL) as i:
                e0 = expand(i, 0)
                e1 = expand(i, 1)
                contract(i, 0, e0)
                e2 = expand(i, 2)
                contract(i, 1, e1)
                contract(i, 2, e2)

        @block.scalar
        def _(act):
            act.wait_ge(small_in, 32)
            act.wait_ge(zero_set, 1)
            act.dma_start(slots_in.rearrange("(n p) d -> p n d", p=P), zero[:].rearrange("p (o d) -> p o d", o=1).to_broadcast(
                (P, BLOCKS, HID))).then_inc(slots_zeroed, 16)
            act.activation(esc[:], ct[:], ACT.Exp, scale=-1.0).then_inc(esc_done, 1)
            act.wait_ge(cols_done, 3)

            def project(b, par):
                act.wait_ge(psT, HEAD + b + 1)
                act.wait_ge(psV, HEAD + b)
                for k in range(KC):
                    act.activation(hT[:, k, :], MISC[0][:, k * SEQ:(k + 1) * SEQ], ACT.Identity,
                                   bias=sa[:, k, ds(b, 1)], scale=ca1[:, k, ds(b, 1)]).then_inc(hT_done, 1)
                act.wait_ge(split_lo, HEAD + b)
                for ready, done, src, at, scale in ((psQ, q_evac, MISC[1], 0, HDIM ** -0.5), (psK, k_evac, MISC[0], 2, 1.0)):
                    act.wait_ge(ready, b + 1)
                    for c in range(2):
                        act.activation(qkf[:, at + c, :], src[:, c * SEQ:(c + 1) * SEQ], ACT.Identity,
                                       bias=bqk[:, at + c:at + c + 1], scale=scale).then_inc(done, 1)

            def negate_maxima(b):
                act.wait_ge(m_lo, HEAD + b)
                for qt in range(TPB):
                    act.wait_ge(psM, HEAD + b * 2 + (qt + 1))
                    act.activation(mneg[:, qt * P:qt * P + P], SM[qt][0:HEADS, 0:P], ACT.Copy, scale=-1.0).then_inc(mT_evac, 1)

            def exponentials(b, par):
                for h in range(HEADS):
                    g, j = h // 4, h % 4
                    act.wait_ge(psS, b * 16 + (h + 1))
                    if j == 0:
                        act.wait_ge(psPV, HEAD + b * 4 + (g - 1))
                    act.activation(probs[:, (g % 2) * 4 + j], ST[h % 2][:], ACT.Exp).then_inc(exp_done, 1)
                    if h in (11, 15):
                        half = (h - 11) // 4
                        act.wait_ge(psPV, HEAD + b * 4 + (2 * half + 2))
                        act.wait_ge(psOT, HEAD + b * 2)
                        act.activation(OT[:, 2 * half:2 * half + 2, :], PV[half][:], ACT.Copy).then_inc(pv_evac, 1)

            def first():
                project(0, 0)
                negate_maxima(0)

            def body(b, par, more):
                if more:
                    project(b + 1, 1 - par)
                exponentials(b, par)
                if more:
                    negate_maxima(b + 1)
                act.wait_ge(psOnT, HEAD + b + 1)
                act.wait_ge(psWo, HEAD + b)
                act.activation(OnT[:], MISC[0][:], ACT.Copy).then_inc(onT_evac, 1)

            batches(act, first, body)

            with act.Fori(0, TILES // CT) as c:
                act.wait_ge(h2c_done, c * 2 + 2)
                act.activation(h2[:, ds(c * CT, CT), :], h2c[:], ACT.Copy).then_inc(h2_kept, 1)
                act.wait_ge(psT2, HEAD + c * 2 + 1)
                act.wait_ge(ps_gu, HEAD + c * 3)
                act.activation(h2T[:, 0, :], bank[0][:], ACT.Copy).then_inc(h2T_a, 1)
                for m, rows in enumerate(SHARED_ROWS):
                    act.wait_ge(ps_gu, HEAD + c * 3 + (m + 1))
                    act.wait_ge(sg_mul, HEAD + c * 3 + m)
                    act.activation(ssil[0:rows, :], bank[2 + 2 * m][0:rows, :], ACT.Silu).then_inc(silu_done, 1)
                act.wait_ge(ps_dn, HEAD + c * 2 + 1)
                act.activation(zsh[:, ds(c * CT, 2), :], bank[1][:], ACT.Copy).then_inc(z_a, 1)
            act.wait_ge(r_evac, TILES // CT)
            act.activation(r3[0][:], lg[:, :, EXPERTS:], ACT.Silu).then_inc(route_silu, 1)
            act.wait_ge(route_step, 4)
            act.activation(r3[2][:], r3[1][:], ACT.Exp).then_inc(route_exp, 1)
            with act.Fori(0, BLOCKS // UNROLL) as i:
                def turned(u):
                    n = i * UNROLL + u
                    act.wait_ge(psTb, n + 1)
                    act.wait_ge(psU, HEAD + n - 2)
                    act.activation(hbT[u][:], bank[u % 2][:, 0:HID], ACT.Copy).then_inc(hbT_done, 1)

                def gate(u):
                    n = i * UNROLL + u
                    act.wait_ge(psU, HEAD + n + 1)
                    act.wait_ge(hg_done, HEAD + n - 2)
                    act.activation(bsil[u][:], bank[2 + u][:, 0:INTER], ACT.Silu).then_inc(bsil_done, 1)

                for u in range(UNROLL):
                    turned(u)
                    gate(u)

        @block.vector
        def _(dve):
            dve.memset(zero[:], 0.0).then_inc(zero_set, 1)
            for i in range(2):
                dve.memset(kst[i][0:STACK].bitcast(F32), 1.0).then_inc(const_done, 1)
                dve.memset(vst[i][:], 1.0).then_inc(const_done, 1)
            dve.wait_ge(esc_done, 1)
            dve.tensor_scalar(esc[:], esc[:], 1.0, None, ALU.add).then_inc(siluc_step, 1)
            dve.wait_ge(siluc_step, 1)
            dve.reciprocal(rec[:], esc[:]).then_inc(siluc_step, 1)
            dve.wait_ge(siluc_step, 2)
            dve.tensor_tensor(siluc[:], ct[:], rec[:], ALU.mult).then_inc(siluc_step, 1)
            dve.wait_ge(x_in, 64)
            for t in range(TILES):
                dve.bn_stats(stats[:, t, :], x[:, t, :]).then_inc(stat_step, 1)
            for t in range(TILES):
                dve.wait_ge(stat_step, TILES)
                dve.bn_aggr(mv[:, t, :], stats[:, t, :]).then_inc(stat_step, 1)
            dve.wait_ge(ps_mod, 3)
            for n in range(3):
                dve.tensor_copy(modr[:, n * 512:(n + 1) * 512], bank[n][0:BATCH, :]).then_inc(mod_raw, 1)
            dve.wait_ge(ps_mod, 4)
            dve.tensor_copy(sa[:].rearrange("p k b -> p (k b)"), bank[3][:, 0:KC * BATCH]).then_inc(cols_done, 1)
            dve.tensor_scalar(ca1[:].rearrange("p k b -> p (k b)"), bank[3][:, KC * BATCH:2 * KC * BATCH], 1.0, None,
                              ALU.add).then_inc(cols_done, 1)
            dve.wait_ge(attn_w_in, 16 * 14)
            dve.tensor_scalar(bqk[:, 0:2], bqk[:, 0:2], HDIM ** -0.5, None, ALU.mult).then_inc(cols_done, 1)
            dve.wait_ge(mod_raw, 3)
            for n, at in enumerate((2 * HID, 5 * HID)):
                g = modr[:, at:at + HID]
                dve.tensor_scalar(sgn[:, n, :], g, 0.0, 2.0, ALU.is_ge, ALU.mult).then_inc(floor_step, 1)
                dve.tensor_scalar(minus[:, n, :], g, -1.0, 0.25, ALU.mult, ALU.max).then_inc(floor_step, 1)
                dve.wait_ge(floor_step, 3 * n + 2)
                dve.tensor_tensor(g, g, minus[:, n, :], ALU.max).then_inc(floor_step, 1)
                dve.wait_ge(floor_step, 3 * n + 3)
                dve.scalar_tensor_tensor(out=g, in0=sgn[:, n, :], scalar=-1.0, in1=g, op0=ALU.add, op1=ALU.mult
                                         ).then_inc(modr_done, 1)
            dve.tensor_scalar(modr[:, 4 * HID:5 * HID], modr[:, 4 * HID:5 * HID], 1.0, None, ALU.add).then_inc(modr_done, 1)
            dve.wait_ge(rstd_done, 3)

            def normalise(b):
                dve.wait_ge(psT, HEAD + b)
                for t in range(TPB):
                    at = b * TPB + t
                    dve.tensor_scalar(z1[:, t, :], x[:, ds(at, 1), :].rearrange("p o d -> p (o d)"),
                                      mv[:, ds(at, 1), 0:1].rearrange("p o i -> p (o i)"), rstd[:, ds(at, 1)],
                                      ALU.subtract, ALU.mult).then_inc(z1_done, 1)

            def split(b, par):
                dve.wait_ge(q_evac, (b + 1) * 2)
                dve.wait_ge(k_evac, (b + 1) * 2)
                dve.wait_ge(stored, DMA_HEAD + b * 128)
                dve.tensor_copy(qks[:, 0], qkf[:]).then_inc(split_hi, 1)
                dve.wait_ge(split_hi, b + 1)
                dve.tensor_tensor(qks[:, 1], qkf[:], qks[:, 0].bitcast(F32), ALU.subtract).then_inc(split_lo, 1)
                dve.wait_ge(psV, HEAD + b + 1)
                for t in range(TPB):
                    dve.tensor_tensor(vst[par][:, t, :, 0:HDIM], MISC[1][:, t * HID:(t + 1) * HID].rearrange(
                        "p (h d) -> p h d", h=HEADS), bvb[:].rearrange("p (h d) -> p h d", h=HEADS), ALU.add
                                      ).then_inc(v_done, 1)

            def max_unit(b, u):
                pair, qt = u // 2, u % 2
                if u == 0:
                    dve.wait_ge(psM, HEAD + b * 2)
                dve.wait_ge(psMax, b * 16 + (u + 1))
                dve.tensor_reduce(mx[:, qt, 2 * pair:2 * pair + 2], SM[qt][:].rearrange("p (h k) -> p h k", h=2),
                                  AX.X, ALU.max).then_inc(max_done, 1)

            def split_maxima(b):
                dve.wait_ge(mT_evac, HEAD + (b + 1) * 2)
                dve.wait_ge(mrow_in, DMA_HEAD + b * 32)
                dve.tensor_copy(mrow[:, 0, :], mneg[:]).then_inc(m_hi, 1)
                dve.wait_ge(m_hi, b + 1)
                dve.tensor_tensor(mrow[:, 1, :], mneg[:], mrow[:, 0, :].bitcast(F32), ALU.subtract).then_inc(m_lo, 1)

            def first():
                normalise(0)
                split(0, 0)
                for u in range(16):
                    max_unit(0, u)
                split_maxima(0)

            def body(b, par, more):
                if more:
                    normalise(b + 1)
                    split(b + 1, 1 - par)
                    for u in range(16):
                        max_unit(b + 1, u)
                    split_maxima(b + 1)
                for qt in range(TPB):
                    dve.wait_ge(psOT, HEAD + b * 2 + (qt + 1))
                    heads = MISC[qt][:].rearrange("p (h d) -> p h d", h=HEADS)
                    dve.reciprocal(rs[:, qt, :], heads[:, :, HDIM]).then_inc(rs_done, 1)
                    dve.wait_ge(rs_done, b * 2 + (qt + 1))
                    if qt == 0:
                        dve.wait_ge(psOnT, HEAD + b)
                    dve.tensor_tensor(On[:, qt, :].rearrange("p (h d) -> p h d", h=HEADS), heads[:, :, 0:HDIM],
                                      rs[:, qt, :].rearrange("p (h o) -> p h o", o=1).to_broadcast((P, HEADS, HDIM)),
                                      ALU.mult).then_inc(on_done, 1)
                dve.wait_ge(psWo, HEAD + b + 1)
                dve.wait_ge(x1_done, HEAD + b)
                dve.tensor_tensor(att[:], MISC[1][:].rearrange("p (t d) -> p t d", t=TPB),
                                  bob[:].rearrange("p (o d) -> p o d", o=1).to_broadcast((P, TPB, HID)), ALU.add
                                  ).then_inc(wo_evac, 1)

            batches(dve, first, body)

            dve.wait_ge(x1_done, HEAD + BATCH)
            dve.wait_ge(slots_zeroed, 16)
            for t in range(TILES):
                dve.bn_stats(stats[:, t, :], x[:, t, :]).then_inc(stat2_step, 1)
            for t in range(TILES):
                dve.wait_ge(stat2_step, TILES)
                dve.bn_aggr(mv[:, t, :], stats[:, t, :]).then_inc(stat2_step, 1)
            dve.wait_ge(rstd2_done, 3)
            with dve.Fori(0, TILES) as t:
                dve.tensor_scalar(h2[:, ds(t, 1), :].rearrange("p o d -> p (o d)"), x[:, ds(t, 1), :].rearrange("p o d -> p (o d)"),
                                  mv[:, ds(t, 1), 0:1].rearrange("p o i -> p (o i)"), rstd[:, ds(t, 1)],
                                  ALU.subtract, ALU.mult).then_inc(z2_done, 1)
            for u in range(UNROLL):
                dve.memset(hg[u][:], 0.0).then_inc(pads_done, 1)
            for s in range(2):
                dve.memset(wd[64:HPAD, s], 0.0).then_inc(pads_done, 1)
            with dve.Fori(0, TILES // CT) as c:
                dve.wait_ge(psT2, HEAD + c * 2 + 2)
                dve.wait_ge(ps_gu, HEAD + c * 3)
                dve.tensor_copy(h2T[:, 1, :], bank[1][:]).then_inc(h2T_v, 1)
                dve.wait_ge(ps_r, c + 1)
                dve.tensor_copy(lg[:, ds(c * CT, CT), :], bank[0][:, 0:CT * 2 * EXPERTS]).then_inc(r_evac, 1)
                for m, rows in enumerate(SHARED_ROWS):
                    dve.wait_ge(silu_done, c * 3 + (m + 1))
                    dve.wait_ge(ps_dn, HEAD + c * 2)
                    dve.tensor_tensor(sgT[0:rows, m, :], ssil[0:rows, :], bank[3 + 2 * m][0:rows, :], ALU.mult
                                      ).then_inc(sg_mul, 1)
                dve.wait_ge(ps_dn, HEAD + c * 2 + 2)
                dve.tensor_copy(zsh[:, ds(c * CT + 2, 2), :], bank[0][:]).then_inc(z_v, 1)

            steps = [0]

            def step(ins):
                steps[0] += 1
                ins.then_inc(route_step, 1)
                dve.wait_ge(route_step, steps[0])

            def rows(v):
                return v[:].rearrange("p (t o) -> p t o", o=1).to_broadcast((P, TILES, EXPERTS))

            def cols(v):
                return v.rearrange("p (o e) -> p o e", o=1).to_broadcast((P, TILES, EXPERTS))

            gate, logit, prob, biased, weight, tie, first_of, second_of = (r[:] for r in r3)
            dve.wait_ge(route_silu, 1)
            step(dve.tensor_tensor(logit, lg[:, :, 0:EXPERTS], gate, ALU.mult))
            step(dve.scalar_tensor_tensor(out=logit, in0=logit, scalar=-1.0, in1=logit, op0=ALU.mult, op1=ALU.max))
            step(dve.tensor_reduce(c1[0][:], logit, AX.X, ALU.max))
            step(dve.tensor_tensor(logit, logit, rows(c1[0]), ALU.subtract))
            dve.wait_ge(route_exp, 1)
            step(dve.tensor_reduce(c1[1][:], prob, AX.X, ALU.add))
            step(dve.reciprocal(c1[2][:], c1[1][:]))
            step(dve.tensor_tensor(prob, prob, rows(c1[2]), ALU.mult))
            step(dve.tensor_tensor(biased, prob, cols(ebias[:]), ALU.add))
            step(dve.tensor_tensor(weight, prob, cols(escale[:]), ALU.mult))
            step(dve.tensor_scalar(weight, weight, 1.0, None, ALU.add))
            dve.wait_ge(iota_step, 4)
            for onehot in (first_of, second_of):
                step(dve.tensor_reduce(c1[3][:], biased, AX.X, ALU.max))
                step(dve.tensor_tensor(tie, biased, rows(c1[3]), ALU.is_equal))
                step(dve.tensor_tensor(tie, tie, cols(iotaf[:]), ALU.mult))
                step(dve.tensor_reduce(c1[4][:], tie, AX.X, ALU.max))
                step(dve.tensor_tensor(onehot, tie, rows(c1[4]), ALU.is_equal))
                if onehot is first_of:
                    step(dve.scalar_tensor_tensor(out=biased, in0=onehot, scalar=-1e30, in1=biased, op0=ALU.mult, op1=ALU.add))
            dve.tensor_tensor(gate, first_of, second_of, ALU.add).then_inc(masks_done, 1)
            for choice, onehot in enumerate((first_of, second_of)):
                step(dve.tensor_tensor(tie, onehot, weight, ALU.mult))
                step(dve.tensor_reduce(wsel[:, choice, :], tie, AX.X, ALU.add))
            dve.wait_ge(ps_cnt, 2)
            step(dve.memset(cnt[:, 0, :], 0.0))
            for t in range(TILES):
                step(dve.tensor_tensor(cnt[:, t + 1, :], cnt[:, t, :], bank[1][:, t * EXPERTS:(t + 1) * EXPERTS], ALU.add))
            step(dve.tensor_scalar(blk[:, 0, :], cnt[:, TILES, :], float(P - 1), None, ALU.add))
            step(dve.tensor_copy(blki[:], blk[:, 0, :]))
            step(dve.tensor_scalar(blki[:], blki[:], 7, None, ALU.logical_shift_right))
            step(dve.tensor_copy(blk[:, 1, :], blki[:]))
            step(dve.memset(cend[:], 0.0))
            for e in range(EXPERTS):
                step(dve.tensor_tensor(cend[:, e + 1:e + 2], cend[:, e:e + 1], blk[:, 1, e:e + 1], ALU.add))
            step(dve.tensor_scalar(blk[:, 2, :], cend[:, 0:EXPERTS], float(P), None, ALU.mult))
            step(dve.tensor_tensor(cnt[:, 0:TILES, :], cnt[:, 0:TILES, :], cols(blk[:, 2, :]), ALU.add))
            step(dve.tensor_tensor(prob, cnt[:, 0:TILES, :], bank[0][:, 0:TILES * EXPERTS].rearrange("p (t e) -> p t e", e=EXPERTS), ALU.add))
            for choice, onehot in enumerate((first_of, second_of)):
                step(dve.tensor_tensor(tie, onehot, prob, ALU.mult))
                step(dve.tensor_reduce(slotf[:, choice, :], tie, AX.X, ALU.add))
            step(dve.tensor_copy(slot[:], slotf[:]))
            step(dve.tensor_tensor(bcmp[:], cend[:, 1:EXPERTS + 1].rearrange("p (o e) -> p o e", o=1).to_broadcast((P, BLOCKS, EXPERTS)),
                                   bnum[:].rearrange("p (b o) -> p b o", o=1).to_broadcast((P, BLOCKS, EXPERTS)), ALU.is_le))
            step(dve.tensor_reduce(eidf[:], bcmp[:], AX.X, ALU.add))
            step(dve.tensor_scalar(eidf[:], eidf[:], float(EXPERTS - 1), None, ALU.min))
            dve.tensor_copy(eid[:], eidf[:]).then_inc(slots_known, 1)

            with dve.Fori(0, BLOCKS // UNROLL) as i:
                def product(u):
                    n = i * UNROLL + u
                    dve.wait_ge(bsil_done, n + 1)
                    dve.wait_ge(psG, HEAD + n - 2)
                    dve.tensor_tensor(hg[u][:, :, 0:HALF], bsil[u][:].rearrange("p (s n) -> p s n", s=2),
                                      bank[2 + u][:, INTER:2 * INTER].rearrange("p (s n) -> p s n", s=2), ALU.mult
                                      ).then_inc(hg_done, 1)

                def finish(u):
                    n = i * UNROLL + u
                    dve.wait_ge(psG, HEAD + n + 1)
                    dve.wait_ge(psD, HEAD + n - 2)
                    dve.tensor_copy(hgT[u][:], bank[5 + u][0:HPAD, 0:2 * P]).then_inc(hgT_done, 1)

                def keep(u):
                    n = i * UNROLL + u
                    dve.wait_ge(psD, HEAD + n + 1)
                    dve.wait_ge(ob_out[u], DMA_HEAD + i * 16)
                    dve.tensor_copy(ob[u][:], bank[5 + u][:, HID:2 * HID]).then_inc(ob_done, 1)

                product(0)
                product(1)
                finish(0)
                keep(0)
                product(2)
                finish(1)
                keep(1)
                finish(2)
                keep(2)
            dve.wait_ge(z_a, HEAD + TILES // CT)
            for t in range(TILES):
                dve.wait_ge(picked_in[t], 32)
                z, g = zsh[:, t, :], modb[:, t // TPB, 3, :]
                for choice in range(2):
                    dve.scalar_tensor_tensor(out=z, in0=picked[:, t, choice, :], scalar=wsel[:, choice, t:t + 1], in1=z,
                                             op0=ALU.mult, op1=ALU.add).then_inc(sum_step, 1)
                    dve.wait_ge(sum_step, 3 * t + 1 + choice)
                dve.tensor_tensor(z, z, g, ALU.mult).then_inc(sum_step, 1)
                dve.wait_ge(sum_step, 3 * t + 3)
                dve.tensor_tensor(x[:, t, :], x[:, t, :], z, ALU.add).then_inc(result_done, 1)

        @block.gpsimd
        def _(pool):
            pool.memset(ident[:], 0.0).then_inc(ident_step, 1)
            pool.wait_ge(ident_step, 1)
            pool.affine_select(out=ident[:], in_=ident[:], compare_op=ALU.not_equal, fill=1.0, base=0,
                               pattern=[[-1, P]], channel_multiplier=1).then_inc(const_done, 1)
            pool.memset(neghalf[:], -0.5).then_inc(const_done, 1)
            for i in range(2):
                pool.memset(qst[i][0:MROW].bitcast(F32), 0.0).then_inc(const_done, 1)
            pool.wait_ge(stat_step, 2 * TILES)
            pool.tensor_scalar(rstd[:], mv[:, :, 1], EPS, None, ALU.add).then_inc(rstd_done, 1)
            pool.wait_ge(rstd_done, 1)
            pool.wait_ge(const_done, CONSTS)
            pool.tensor_tensor(rstd[:], rstd[:], neghalf[:], ALU.pow).then_inc(rstd_done, 2)
            pool.wait_ge(modb_in, 16)

            def residual(b):
                pool.wait_ge(wo_evac, HEAD + b + 1)
                pool.tensor_tensor(att2, att[:], modb[:, ds(b, 1), 0, :].to_broadcast((P, TPB, HID)), ALU.mult
                                   ).then_inc(ga_done, 1)
                pool.wait_ge(ga_done, b + 1)
                tiles = x[:, ds(b * TPB, TPB), :]
                pool.tensor_tensor(tiles, att2, tiles, ALU.add).then_inc(x1_done, 1)

            def first():
                pass

            def body(b, par, more):
                residual(b)

            batches(pool, first, body)

            pool.iota(iotai[:], pattern=[[-1, EXPERTS]], base=EXPERTS, channel_multiplier=0).then_inc(iota_step, 1)
            pool.iota(bnumi[:], pattern=[[1, BLOCKS]], base=0, channel_multiplier=0).then_inc(iota_step, 1)
            pool.memset(tri[:], 0.0).then_inc(tri_step, 1)
            pool.memset(ones[:], 1.0).then_inc(tri_step, 1)
            pool.wait_ge(iota_step, 2)
            pool.wait_ge(tri_step, 2)
            pool.tensor_copy(iotaf[:], iotai[:]).then_inc(iota_step, 1)
            pool.tensor_copy(bnum[:], bnumi[:]).then_inc(iota_step, 1)
            pool.affine_select(out=tri[:], in_=tri[:], compare_op=ALU.is_ge, fill=1.0, base=0,
                               pattern=[[-1, P]], channel_multiplier=1).then_inc(tri_step, 1)
            pool.wait_ge(stat2_step, 2 * TILES)
            pool.tensor_scalar(rstd[:], mv[:, :, 1], EPS, None, ALU.add).then_inc(rstd2_done, 1)
            pool.wait_ge(rstd2_done, 1)
            pool.tensor_tensor(rstd[:], rstd[:], neghalf[:], ALU.pow).then_inc(rstd2_done, 2)
            with pool.Fori(0, TILES // CT) as c:
                pool.wait_ge(z2_done, c * CT + CT)
                for i in range(2):
                    tiles, m = h2[:, ds(c * CT + 2 * i, 2), :], c * 2 + i
                    pool.tensor_tensor(tiles, tiles, modb[:, ds(m, 1), 2, :].to_broadcast((P, TPB, HID)), ALU.mult
                                       ).then_inc(h2_step, 1)
                pool.wait_ge(h2_step, c * 2 + 2)
                pool.wait_ge(psT2, HEAD + c * 2)
                pool.wait_ge(h2_kept, HEAD + c)
                for i in range(2):
                    tiles, m = h2[:, ds(c * CT + 2 * i, 2), :], c * 2 + i
                    pool.tensor_tensor(h2c[:, 2 * i:2 * i + 2, :], tiles, modb[:, ds(m, 1), 1, :].to_broadcast((P, TPB, HID)), ALU.add
                                       ).then_inc(h2c_done, 1)
            pool.wait_ge(slots_known, 1)
            pool.wait_ge(slots_zeroed, 16)
            pool.wait_ge(h2_kept, HEAD + TILES // CT)
            for t in range(TILES):
                for choice in range(2):
                    pool.indirect_dma_start(slots_in, bass.IndirectOffsetOnAxis(ap=slot[:, choice, t:t + 1], axis=0),
                                            h2[:, t, :], None).then_inc(scattered, 16)
            for u in range(UNROLL):
                pool.wait_ge(ob_out[u], DMA_HEAD + 16 * (BLOCKS // UNROLL))
            for t in range(TILES):
                for choice in range(2):
                    pool.indirect_dma_start(picked[:, t, choice, :], None, slots_out,
                                            bass.IndirectOffsetOnAxis(ap=slot[:, choice, t:t + 1], axis=0)
                                            ).then_inc(picked_in[t], 16)


def kernel(**inputs):
    import concourse.bacc as bacc
    from concourse.bass_utils import run_bass_kernel_spmd

    a = {n.replace("L0_", ""): np.asarray(v) for n, v in inputs.items()}
    arrays = host_layout(a)
    nc = bacc.Bacc("TRN2", target_bir_lowering=False, num_devices=1)
    args = [nc.dram_tensor(n, v.shape, mybir.dt.from_np(v.dtype), kind="ExternalInput").ap() for n, v in arrays.items()]
    out = nc.dram_tensor("out", (T, HID), F32, kind="ExternalOutput").ap()
    adaln_block(nc, *args, out)
    result = run_bass_kernel_spmd(nc, [arrays], core_ids=[0])
    return result.results[0]["out"].reshape(BATCH, SEQ, HID)


def host_layout(a):
    c = np.ascontiguousarray
    return {
        "in_x": c(a["attn_X"].reshape(T, HID)),
        "in_bqk": c(np.concatenate([a["attn_bq"], a["attn_bk"]]).reshape(2 * KC, P).T),
        "in_wq": a["attn_Wq"], "in_wk": a["attn_Wk"],
        "in_wv": a["attn_Wv"], "in_bv": a["attn_bv"], "in_wo": a["attn_Wo"], "in_bo": a["attn_bo"],
        "in_route": c(np.concatenate([a["ffn_cls_w"], a["ffn_gate_w"]]).T),
        "in_escale": a["ffn_extra_scale"], "in_ebias": a["ffn_extra_bias"],
        "in_wgu": c(np.concatenate([a["ffn_wg"], a["ffn_wu"]], axis=1).transpose(2, 0, 1)),
        "in_wd": c(a["ffn_wd"].transpose(0, 2, 1)),
        "in_sgu": c(np.concatenate([a["ffn_sg"], a["ffn_su"]]).T),
        "in_sd": c(a["ffn_sd"].T),
        "in_ct": c(a["c"].T), "in_wmod": a["wmod"],
    }
```

```python
from contextlib import ExitStack

import concourse.bass as bass
import concourse.mybir as mybir
import numpy as np

F32, F32R, I32, U32 = mybir.dt.float32, mybir.dt.float32r, mybir.dt.int32, mybir.dt.uint32
ACT = mybir.ActivationFunctionType
ALU = mybir.AluOpType
AX = mybir.AxisListType
ds = bass.ds

P = 128
BATCH, SEQ, HID = 8, 256, 256
HEADS, HDIM = 16, 16
T = BATCH * SEQ
TILES = T // P
TPB = SEQ // P
KC = HID // P
EXPERTS, INTER, SHARED = 14, 176, 352
HALF = INTER // 2
HPAD = 96
BLOCKS = (2 * T + EXPERTS * (P - 1)) // P
SLOTS = BLOCKS * P
QUADS = (BLOCKS - 3) // 4
CHUNK = 512
CT = CHUNK // P
CHUNKS = T // CHUNK
SCORE = 3 * HDIM
MROW = 96
STACK = MROW + 2
EPS = 1e-5
HEAD, DMA_HEAD = 3, 16
CONSTS = 8
NORMS = ((0, 1), (2, 3), (4, 5), (6,))
SHARED_ROWS = [P, P, SHARED - 2 * P]
UNITS_AFTER = [0, 0, 1, 1, 1, 1, 1, 1, 1, 1, 1, 1, 1, 1, 2, 2]
assert sum(UNITS_AFTER) == 16


def adaln_block(nc, x_d, bqk_d, wq_d, wk_d, wv_d, bv_d, wo_d, bo_d, route_d, escale_d, ebias_d,
                wgu_d, wd_d, sgu_d, sd_d, ct_d, wmod_d, out_d, debug=None):
    mod_scr = nc.dram_tensor("mod_scr", (BATCH, 4 * HID), F32, kind="Internal").ap()
    scr = [nc.dram_tensor(f"stack_scr{i}", (2, HEADS, 2, HDIM, SEQ), F32, kind="Internal").ap() for i in range(2)]
    slots_in = nc.dram_tensor("slots_in", (SLOTS + SLOTS % (2 * P), HID), F32, kind="Internal").ap()
    slots_out = nc.dram_tensor("slots_out", (SLOTS, HID), F32, kind="Internal").ap()

    ctx = ExitStack()
    phase1, phase2 = ExitStack(), ExitStack()

    def sb(name, shape, dt=F32, where=None):
        return (where or ctx).enter_context(nc.sbuf_tensor(name, shape, dt))

    def flag(name):
        return ctx.enter_context(nc.semaphore(name))

    with ctx:
        x = sb("x", [P, TILES, HID])
        h2 = sb("h2", [P, TILES, HID])
        ident = sb("ident", [P, P])
        modb = sb("modb", [P, BATCH, 4, HID])
        stats = sb("stats", [P, TILES, 6])
        mv = sb("mv", [P, TILES, 2])
        rstd = sb("rstd", [P, TILES])
        nmean = sb("nmean", [P, TILES])
        neghalf = sb("neghalf", [P, TILES])
        route_w = sb("route_w", [P, KC, 2 * EXPERTS])
        sgu = sb("sgu", [P, KC, 2 * SHARED])
        sd = sb("sd", [P, 3, HID])
        escale = sb("escale", [P, EXPERTS])
        ebias = sb("ebias", [P, EXPERTS])

        def sb1(name, shape, dt=F32):
            return sb(name, shape, dt, phase1)

        qst = [sb1(f"qst{i}", [P, HEADS, SEQ], F32R) for i in range(2)]
        kst = [sb1(f"kst{i}", [P, HEADS, SEQ], F32R) for i in range(2)]
        probs = sb1("probs", [P, 8, TPB, SEQ])
        vst = [sb1(f"vst{i}", [P, TPB, HEADS, 32]) for i in range(2)]
        wq, wk, wv, wo = (sb1(n, [P, KC, HID]) for n in ("wq", "wk", "wv", "wo"))
        wmod = probs[:].rearrange("p j t q -> p (j t q)")[:, 0:KC * 6 * HID].rearrange("p (k n) -> p k n", k=KC)
        ct = sb1("ct", [P, KC, BATCH])
        esc = sb1("esc", [P, KC, BATCH])
        rec = sb1("rec", [P, KC, BATCH])
        siluc = sb1("siluc", [P, KC, BATCH])
        zero = sb1("zero", [P, HID])
        sa = sb1("sa", [P, KC, BATCH])
        ca1 = sb1("ca1", [P, KC, BATCH])
        modr = h2[0:BATCH, 0:6, :].rearrange("b m d -> b (m d)")
        sgn = h2[0:BATCH, 6:8, :]
        minus = h2[0:BATCH, 8:10, :]
        bqk = sb1("bqk", [P, 4])
        bvb = sb1("bvb", [P, HID])
        bob = sb1("bob", [P, HID])
        z1 = sb1("z1", [P, TPB, HID])
        hT = sb1("hT", [P, KC, SEQ])
        qkf = sb1("qkf", [P, 4, SEQ])
        qks = sb1("qks", [P, 2, 4, SEQ], F32R)
        mx = sb1("mx", [P, TPB, HEADS])
        mneg = sb1("mneg", [HEADS, SEQ])
        mrow = sb1("mrow", [HEADS, 2, SEQ], F32R)
        OT = sb1("OT", [P, 4, SEQ])
        rs = sb1("rs", [P, TPB, HEADS])
        On = sb1("On", [P, TPB, HID])
        OnT = sb1("OnT", [P, KC, SEQ])
        att = sb1("att", [P, TPB, HID])
        att2 = sb1("att2", [P, TPB, HID])
        phase1.close()

        def sb2(name, shape, dt=F32):
            return sb(name, shape, dt, phase2)

        wgu = sb2("wgu", [P, KC, EXPERTS, 2 * INTER])
        wd = sb2("wd", [HPAD, 2, EXPERTS, HID])
        zsh = sb2("zsh", [P, TILES, HID])
        sgT = [sb2(f"sgT{i}", [P, 3, CHUNK]) for i in range(2)]
        sup = [sb2(f"sup{i}", [P, CHUNK]) for i in range(2)]
        lg = sb2("lg", [P, TILES, 2 * EXPERTS])
        r3 = [sb2(f"r{i}", [P, TILES, EXPERTS]) for i in range(8)]
        c1 = [sb2(f"c{i}", [P, TILES]) for i in range(8)]
        iotaf = sb2("iotaf", [P, EXPERTS])
        iotai = sb2("iotai", [P, EXPERTS], I32)
        bnumi = sb2("bnumi", [P, BLOCKS], I32)
        tri = sb2("tri", [P, P])
        ones = sb2("ones", [P, P])
        cnt = sb2("cnt", [P, TILES + 1, EXPERTS])
        blk = sb2("blk", [P, 4, EXPERTS])
        blki = sb2("blki", [P, EXPERTS], I32)
        cend = sb2("cend", [P, EXPERTS + 1])
        bnum = sb2("bnum", [P, BLOCKS])
        bcmp = sb2("bcmp", [P, BLOCKS, EXPERTS])
        eidf = sb2("eidf", [P, BLOCKS])
        eid = sb2("eid", [P, BLOCKS], I32)
        slotf = sb2("slotf", [P, 2, TILES])
        slot = sb2("slot", [P, 2, TILES], U32)
        wsel = sb2("wsel", [P, 2, TILES])
        phase3 = ExitStack()
        h2T = sb("h2T", [P, KC, T], F32, phase3)
        phase3.close()
        hb = [sb2(f"hb{i}", [P, 2, HID]) for i in range(2)]
        hbT = [sb2(f"hbT{i}", [P, KC, P]) for i in range(2)]
        bsil = [sb2(f"bsil{i}", [P, INTER]) for i in range(2)]
        hg = [sb2(f"hg{i}", [P, 2, HPAD]) for i in range(2)]
        hgT = [sb2(f"hgT{i}", [HPAD, 2, P]) for i in range(2)]
        ob = [sb2(f"ob{i}", [P, 2, HID]) for i in range(2)]
        picked = wgu[:].rearrange("p k e n -> p (k e n)")[:, 0:TILES * 2 * HID].rearrange("p (t c d) -> p t c d", t=TILES, c=2)
        phase2.close()

        bank = [ctx.enter_context(nc.psum_tensor(f"bank{i}", [P, 512], F32)) for i in range(8)]
        ST, SM, PV, MISC = bank[0:2], bank[2:4], bank[4:6], bank[6:8]
        TURNED, GATE_UP = (bank[0:2], bank[2:4]), (bank[4:6], bank[2:4])
        LOGITS, COUNTS, DOWN = bank[6], bank[7], bank[0:2]
        ROWS, GU, PROD, OUT = bank[0:2], bank[2:4], bank[4:6], bank[6:8]

        x_in = flag("x_in")
        ct_in, wmod_in, bqk_in, shared_w_in = flag("ct_in"), flag("wmod_in"), flag("bqk_in"), flag("shared_w_in")
        attn_w_in = flag("attn_w_in")
        ffn_w_in = flag("ffn_w_in")
        const_done = flag("const_done")
        ident_step, zero_set = flag("ident_step"), flag("zero_set")
        slots_zeroed, tri_step = flag("slots_zeroed"), flag("tri_step")
        stat_step = flag("stat_step")
        rstd_done = flag("rstd_done")
        esc_done = flag("esc_done")
        siluc_step = flag("siluc_step")
        ps_mod, ps_cols = flag("ps_mod"), flag("ps_cols")
        mod_raw, floor_step, modr_done, cols_done = flag("mod_raw"), flag("floor_step"), flag("modr_done"), flag("cols_done")
        mod_stored = flag("mod_stored")
        modb_in = flag("modb_in")
        z1_done = flag("z1_done")
        psT, psQ, psK, psV = flag("psT"), flag("psQ"), flag("psK"), flag("psV")
        hT_done = flag("hT_done")
        q_evac, k_evac, v_done = flag("q_evac"), flag("k_evac"), flag("v_done")
        split_hi, split_lo = flag("split_hi"), flag("split_lo")
        stored, loaded = flag("stored"), [flag(f"loaded{i}") for i in range(2)]
        psMax, max_done = flag("psMax"), flag("max_done")
        psM, mT_evac, m_hi, m_lo = flag("psM"), flag("mT_evac"), flag("m_hi"), flag("m_lo")
        mrow_in = flag("mrow_in")
        psS, exp_done = flag("psS"), flag("exp_done")
        psPV, pv_evac = flag("psPV"), flag("pv_evac")
        psOT, rs_done, on_done = flag("psOT"), flag("rs_done"), flag("on_done")
        psOnT, onT_evac = flag("psOnT"), flag("onT_evac")
        psWo, wo_evac = flag("psWo"), flag("wo_evac")
        ga_done, x1_done = flag("ga_done"), flag("x1_done")
        stat2_step, rstd2_done, z2_done, h2_step = flag("stat2_step"), flag("rstd2_done"), flag("z2_done"), flag("h2_step")
        h2_done = flag("h2_done")
        psT2, h2T_a, h2T_v = flag("psT2"), flag("h2T_a"), flag("h2T_v")
        ps_r, r_evac = flag("ps_r"), flag("r_evac")
        ps_gu, gu_evac, sg_mul = flag("ps_gu"), flag("gu_evac"), flag("sg_mul")
        ps_dn, z_evac = flag("ps_dn"), flag("z_evac")
        route_step, route_silu, route_exp = flag("route_step"), flag("route_silu"), flag("route_exp")
        masks_done, ps_cnt, slots_known, iota_step = flag("masks_done"), flag("ps_cnt"), flag("slots_known"), flag("iota_step")
        scattered = flag("scattered")
        hb_in = [flag(f"hb_in{u}") for u in range(2)]
        ob_out = [flag(f"ob_out{u}") for u in range(2)]
        psRows, hbT_done, psGU, bsil_done = flag("psRows"), flag("hbT_done"), flag("psGU"), flag("bsil_done")
        hg_done, psProd, hgT_done, psOut, ob_done = flag("hg_done"), flag("psProd"), flag("hgT_done"), flag("psOut"), flag("ob_done")
        pads_done, wd_pads_done = flag("pads_done"), flag("wd_pads_done")
        picked_in = [flag(f"picked_in{t}") for t in range(TILES)]
        sum_step, result_done, stored_out = flag("sum_step"), flag("result_done"), flag("stored_out")
        ahead = [exp_done, gu_evac, hbT_done, hg_done, mT_evac, m_lo, ob_done, onT_evac, psOut, psProd, hgT_done, psM, psOT, psOnT, psPV, psT, psGU, psV, psWo, ps_dn, pv_evac, split_lo, v_done, wo_evac, x1_done, z_evac]
        dma_ahead = [*ob_out, stored, mrow_in]

        block = ctx.enter_context(nc.Block())
        LAST = BATCH - 1

        def batches(eng, body):
            with eng.Fori(0, (BATCH - 4) // 2) as pair:
                for par in range(2):
                    body(pair * 2 + par, par, 3, False)
            for b in range(BATCH - 4, BATCH):
                body(b, b % 2, BATCH - 1 - b, True)

        def second_norms(b, in_line):
            return NORMS[b - (BATCH - 4)] if in_line else ()

        def gate_times_up(eng, c, m, rows):
            j = 3 * c + m
            eng.wait_ge(gu_evac, HEAD + 2 * (j + 1))
            if j > 0:
                eng.wait_ge(sg_mul, j)
            eng.tensor_tensor(sgT[c % 2][0:rows, m, :], sgT[c % 2][0:rows, m, :], sup[j % 2][0:rows, :], ALU.mult
                              ).then_inc(sg_mul, 1)

        def blocks(eng, body):
            with eng.Fori(0, QUADS) as quad:
                for r in range(4):
                    body(quad * 4 + r, r, BLOCKS - 1 - 4 * QUADS + 1)
            for n in range(4 * QUADS, BLOCKS):
                body(n, n % 4, BLOCKS - 1 - n)

        @block.sync
        def _(sp):
            for f in ahead:
                sp.sem_inc(f, HEAD)
            for f in dma_ahead:
                sp.sem_inc(f, DMA_HEAD)
            sp.dma_start(ct[:], ct_d.rearrange("(k p) b -> p k b", p=P)).then_inc(ct_in, 16)
            sp.dma_start(wmod, wmod_d.rearrange("(k p) n -> p k n", p=P)).then_inc(wmod_in, 16)
            for q in range(4):
                n = TILES // 4
                sp.dma_start(x[:, n * q:n * q + n, :], x_d[n * q * P:n * (q + 1) * P, :].rearrange(
                    "(t p) d -> p t d", p=P)).then_inc(x_in, 16)
            sp.dma_start(bqk[:], bqk_d).then_inc(bqk_in, 16)
            for tile, src in ((wq, wq_d), (wk, wk_d), (wv, wv_d), (wo, wo_d)):
                sp.dma_start(tile[:], src.rearrange("(k p) n -> p k n", p=P)).then_inc(attn_w_in, 16)
            for tile, src, n in ((bvb, bv_d, HID), (bob, bo_d, HID), (escale, escale_d, EXPERTS), (ebias, ebias_d, EXPERTS)):
                sp.dma_start(tile[:], src.rearrange("(o n) -> o n", o=1).to_broadcast((P, n))).then_inc(attn_w_in, 16)
            sp.wait_ge(modr_done, 3)
            sp.dma_start(mod_scr, modr[:, 2 * HID:6 * HID]).then_inc(mod_stored, 16)

            def store_parts(b, par, first=False):
                sp.wait_ge(split_lo, HEAD + b + 1)
                if not first:
                    sp.wait_ge(loaded[par], (b - 2 - par) * 32 + 64)
                for side in range(2):
                    for part in range(2):
                        kind = part if side else 1 - part
                        for c in range(2):
                            sp.dma_start(scr[par][side, 8 * c:8 * c + 8, kind, :, :],
                                         qks[:, part, 2 * side + c, :].bitcast(F32)).then_inc(stored, 16)

            def load_stacks(b, par):
                sp.wait_ge(stored, DMA_HEAD + (b + 1) * 128)
                q = scr[par][0].rearrange("h k d t -> (k d) h t")
                k = scr[par][1].rearrange("h k d t -> (k d) h t")
                for dst, src in ((qst[par][0:32], q), (qst[par][32:48], q[16:32]),
                                 (kst[par][16:48], k), (kst[par][0:16], k[0:16])):
                    sp.dma_start(dst.bitcast(F32), src).then_inc(loaded[par], 16)

            def place_maxima(b, par):
                sp.wait_ge(m_lo, HEAD + b + 1)
                for part in range(2):
                    sp.dma_start(qst[par][MROW + part:MROW + part + 1].bitcast(F32),
                                 mrow[:, part, :].bitcast(F32)).then_inc(mrow_in, 16)

            sp.wait_ge(const_done, CONSTS)
            store_parts(0, 0, first=True)
            load_stacks(0, 0)
            store_parts(1, 1, first=True)
            load_stacks(1, 1)
            sp.wait_ge(mod_stored, 16)
            sp.dma_start(modb[:].rearrange("p b m d -> p (b m d)"), mod_scr.rearrange("b n -> (b n)").rearrange(
                "(o n) -> o n", o=1).to_broadcast((P, BATCH * 4 * HID))).then_inc(modb_in, 16)
            store_parts(2, 0)
            place_maxima(0, 0)
            sp.dma_start(route_w[:], route_d.rearrange("(k p) n -> p k n", p=P)).then_inc(shared_w_in, 16)
            sp.dma_start(sgu[:], sgu_d.rearrange("(k p) n -> p k n", p=P)).then_inc(shared_w_in, 16)
            for m, rows in enumerate(SHARED_ROWS):
                sp.dma_start(sd[0:rows, m, :], sd_d[m * P:m * P + rows, :]).then_inc(shared_w_in, 16)
            sp.wait_ge(zero_set, 1)
            sp.dma_start(slots_in.rearrange("(n p) d -> p n d", p=P), zero[:].rearrange("p (o d) -> p o d", o=1).to_broadcast(
                (P, BLOCKS + BLOCKS % 2, HID))).then_inc(slots_zeroed, 16)

            def body(b, par, left, in_line):
                if left >= 2:
                    sp.wait_ge(psPV, HEAD + (b + 1) * 4)
                    load_stacks(b + 2, par)
                if left >= 1:
                    place_maxima(b + 1, 1 - par)
                if left >= 3:
                    store_parts(b + 3, 1 - par)

            batches(sp, body)
            sp.wait_ge(x1_done, HEAD + BATCH)
            sp.wait_ge(mrow_in, DMA_HEAD + 32 * BATCH)
            sp.wait_ge(slots_zeroed, 16)
            sp.wait_ge(wd_pads_done, 2)
            for k in range(KC):
                sp.dma_start(wgu[:, k], wgu_d[k * P:(k + 1) * P]).then_inc(ffn_w_in, 16)
            for s in range(2):
                sp.dma_start(wd[0:HALF, s], wd_d[:, s * HALF:(s + 1) * HALF, :].rearrange("e p n -> p e n")).then_inc(ffn_w_in, 16)
            sp.wait_ge(ps_gu, 3 * CHUNKS)
            sp.wait_ge(scattered, 32 * TILES)

            def load_pair(n, half):
                sp.dma_start(hb[half][:], slots_in[ds(n * P, 2 * P), :].rearrange("(t p) d -> p t d", p=P)
                             ).then_inc(hb_in[half], 16)

            load_pair(0, 0)
            load_pair(2, 1)

            def body(n, r, left):
                if r % 2 == 1 and left >= 3:
                    sp.wait_ge(psRows, n + 1)
                    load_pair(n + 3, r // 2)
                if r % 2 == 1:
                    sp.wait_ge(ob_done, HEAD + n + 1)
                    sp.dma_start(slots_out[ds((n - 1) * P, 2 * P), :].rearrange("(t p) d -> p t d", p=P), ob[r // 2][:]
                                 ).then_inc(ob_out[r // 2], 16)
                elif left == 0:
                    sp.wait_ge(ob_done, HEAD + n + 1)
                    sp.dma_start(slots_out[n * P:(n + 1) * P, :], ob[r // 2][:, 0, :]).then_inc(ob_out[r // 2], 16)

            blocks(sp, body)
            for t in range(0, TILES, 2):
                sp.wait_ge(result_done, t + 2)
                sp.dma_start(out_d[t * P:(t + 2) * P, :].rearrange("(t p) d -> p t d", p=P), x[:, t:t + 2, :]
                             ).then_inc(stored_out, 16)
            sp.wait_ge(stored_out, 8 * TILES)
            if debug is not None:
                dbg = flag("dbg")
                sp.dma_start(debug.rearrange("(t p) d -> p t d", p=P), h2[:]).then_inc(dbg, 16)
                sp.wait_ge(dbg, 16)

        @block.tensor
        def _(pe):
            pe.wait_ge(siluc_step, 3)
            pe.wait_ge(wmod_in, 16)
            for n in range(2 * KC):
                for k in range(KC):
                    mm = pe.matmul(bank[3][:, n * BATCH:(n + 1) * BATCH], wmod[:, k, n * P:(n + 1) * P], siluc[:, k, :],
                                   start=(k == 0), stop=(k == KC - 1))
            mm.then_inc(ps_cols, 1)
            for n in range(3):
                for k in range(KC):
                    mm = pe.matmul(bank[n][0:BATCH, :], siluc[:, k, :], wmod[:, k, n * 512:n * 512 + 512],
                                   start=(k == 0), stop=(k == KC - 1))
                mm.then_inc(ps_mod, 1)
            pe.wait_ge(const_done, CONSTS)
            pe.wait_ge(attn_w_in, 16 * 8)
            pe.wait_ge(cols_done, 3)

            def turn_tokens(b, filling=False):
                pe.wait_ge(z1_done, (b + 1) * 2)
                if not filling:
                    pe.wait_ge(mT_evac, HEAD + b * 2 - 2)
                for t in range(TPB):
                    for k in range(KC):
                        mm = pe.transpose(SM[1][:, k * SEQ + t * P:k * SEQ + t * P + P], z1[:, t, k * P:k * P + P], ident[:])
                mm.then_inc(psT, 1)

            def project_qk(b, filling=False):
                pe.wait_ge(hT_done, (b + 1) * 2)
                if not filling:
                    pe.wait_ge(onT_evac, HEAD + b - 2)
                for w, out, ready in ((wq, MISC[0], psQ), (wk, SM[0], psK)):
                    if out is SM[0]:
                        pe.wait_ge(v_done, HEAD + b * 2)
                    for c in range(2):
                        for k in range(KC):
                            mm = pe.matmul(out[:, c * SEQ:(c + 1) * SEQ], w[:, k, c * P:c * P + P], hT[:, k, :],
                                           start=(k == 0), stop=(k == KC - 1))
                    mm.then_inc(ready, 1)

            def project_v(b, filling=False):
                if not filling:
                    pe.wait_ge(mT_evac, HEAD + b * 2 - 1)
                pe.wait_ge(k_evac, (b + 1) * 2)
                for t in range(TPB):
                    for k in range(KC):
                        mm = pe.matmul(SM[0][:, t * HID:(t + 1) * HID], hT[:, k, t * P:t * P + P], wv[:, k, :],
                                       start=(k == 0), stop=(k == KC - 1))
                mm.then_inc(psV, 1)

            def max_unit(b, par, u, newest):
                pair, qt = u // 2, u % 2
                if u == 0:
                    pe.wait_ge(loaded[par], b * 32 + 64 - 32 * par)
                if u == 0 and newest is not None:
                    pe.wait_ge(k_evac, (newest + 1) * 2)
                elif u == 1 and newest is not None:
                    pe.wait_ge(hT_done, (newest + 1) * 2)
                elif u < 2:
                    pe.wait_ge(mT_evac, HEAD + b * 2 - 1 + u)
                    pe.wait_ge(v_done, HEAD + b * 2 + 2)
                else:
                    pe.wait_ge(max_done, b * 16 + (u - 1))
                for i in range(2):
                    h = 2 * pair + i
                    mm = pe.matmul(SM[qt][:, i * SEQ:(i + 1) * SEQ], qst[par][0:MROW, h, qt * P:qt * P + P],
                                   kst[par][0:MROW, h, :], start=True, stop=True)
                mm.then_inc(psMax, 1)

            def turn_maxima(b):
                pe.wait_ge(max_done, (b + 1) * 16)
                for qt in range(TPB):
                    pe.transpose(SM[qt][0:HEADS, 0:P], mx[:, qt, :], ident[:]).then_inc(psM, 1)

            def scores(b, par, h):
                if h == 0:
                    pe.wait_ge(mrow_in, DMA_HEAD + (b + 1) * 32)
                pe.wait_ge(exp_done, HEAD + b * 16 + (h - 1))
                for kt in range(TPB):
                    mm = pe.matmul(ST[h % 2][:, kt * SEQ:(kt + 1) * SEQ], kst[par][0:STACK, h, kt * P:kt * P + P],
                                   qst[par][0:STACK, h, :], start=True, stop=True)
                mm.then_inc(psS, 1)

            def weigh(b, par, g):
                if g == 0:
                    pe.wait_ge(v_done, HEAD + (b + 1) * 2)
                if g % 2 == 0:
                    pe.wait_ge(pv_evac, HEAD + b * 2 + (g // 2 - 1))
                pe.wait_ge(exp_done, HEAD + b * 16 + (4 * g + 4))
                for kt in range(TPB):
                    for j in range(4):
                        mm = pe.matmul(PV[g // 2][32 * j:32 * j + 32, (g % 2) * SEQ:(g % 2 + 1) * SEQ],
                                       vst[par][:, kt, 4 * g + j, :], probs[:, (g % 2) * 4 + j, kt, :],
                                       start=(kt == 0), stop=(kt == TPB - 1))
                mm.then_inc(psPV, 1)

            def turn_output(b, left):
                pe.wait_ge(pv_evac, HEAD + (b + 1) * 2)
                for qt in range(TPB):
                    if qt == 0 and left >= 2:
                        pe.wait_ge(q_evac, (b + 3) * 2)
                    elif qt == 0:
                        pe.wait_ge(onT_evac, HEAD + b)
                    else:
                        pe.wait_ge(wo_evac, HEAD + b)
                    for g in range(4):
                        mm = pe.transpose(MISC[qt][:, g * P:(g + 1) * P], OT[:, g, qt * P:qt * P + P], ident[:])
                    mm.then_inc(psOT, 1)

            def turn_back(b):
                pe.wait_ge(on_done, (b + 1) * 2)
                for t in range(TPB):
                    for k in range(KC):
                        mm = pe.transpose(MISC[0][:, k * SEQ + t * P:k * SEQ + t * P + P], On[:, t, k * P:k * P + P], ident[:])
                mm.then_inc(psOnT, 1)

            def project_out(b):
                pe.wait_ge(onT_evac, HEAD + b + 1)
                for t in range(TPB):
                    for k in range(KC):
                        mm = pe.matmul(MISC[1][:, t * HID:(t + 1) * HID], OnT[:, k, t * P:t * P + P], wo[:, k, :],
                                       start=(k == 0), stop=(k == KC - 1))
                mm.then_inc(psWo, 1)

            turn_tokens(0, filling=True)
            project_qk(0, filling=True)
            pe.wait_ge(mod_raw, 3)
            project_v(0, filling=True)
            turn_tokens(1, filling=True)
            project_qk(1, filling=True)
            project_v(1, filling=True)
            turn_tokens(2, filling=True)
            project_qk(2, filling=True)
            for u in range(16):
                max_unit(0, 0, u, 2)
            turn_maxima(0)

            def body(b, par, left, in_line):
                u = 0
                for h in range(HEADS):
                    if left >= 1:
                        for _ in range(UNITS_AFTER[h]):
                            max_unit(b + 1, 1 - par, u, b + 2 if left >= 2 else None)
                            u += 1
                    scores(b, par, h)
                    if h % 4 == 3 and h > 3:
                        weigh(b, par, h // 4 - 1)
                weigh(b, par, 3)
                if left >= 1:
                    turn_maxima(b + 1)
                turn_output(b, left)
                if left >= 2:
                    project_v(b + 2)
                turn_back(b)
                if left >= 3:
                    turn_tokens(b + 3)
                project_out(b)
                if left >= 3:
                    project_qk(b + 3)

            batches(pe, body)

            def turn_chunk(c):
                pe.wait_ge(h2_done, (c + 1) * CT // TPB)
                if c >= 2:
                    pe.wait_ge(h2T_a, c - 1)
                    pe.wait_ge(h2T_v, c - 1)
                for k in range(KC):
                    for t in range(CT):
                        mm = pe.transpose(TURNED[c % 2][k][:, t * P:(t + 1) * P], h2[:, c * CT + t, k * P:k * P + P], ident[:])
                    mm.then_inc(psT2, 1)

            def router(c):
                pe.wait_ge(h2T_a, c + 1)
                pe.wait_ge(h2T_v, c + 1)
                for t in range(c * CT, (c + 1) * CT):
                    for k in range(KC):
                        mm = pe.matmul(LOGITS[:, t * 2 * EXPERTS:(t + 1) * 2 * EXPERTS], h2T[:, k, t * P:t * P + P],
                                       route_w[:, k, :], start=(k == 0), stop=(k == KC - 1))
                mm.then_inc(ps_r, 1)

            def gate_up(c):
                for m, rows in enumerate(SHARED_ROWS):
                    j = 3 * c + m
                    pe.wait_ge(gu_evac, HEAD + 2 * (j - 1))
                    for side in range(2):
                        at = side * SHARED + m * P
                        for k in range(KC):
                            mm = pe.matmul(GATE_UP[j % 2][side][0:rows, :], sgu[:, k, at:at + rows],
                                           h2T[:, k, c * CHUNK:(c + 1) * CHUNK], start=(k == 0), stop=(k == KC - 1))
                    mm.then_inc(ps_gu, 1)

            def down(c):
                pe.wait_ge(sg_mul, 3 * (c + 1))
                for half in range(2):
                    pe.wait_ge(z_evac, HEAD + 2 * (c - 1) + half + 1)
                    for t in range(2):
                        tok = (2 * half + t) * P
                        for m, rows in enumerate(SHARED_ROWS):
                            mm = pe.matmul(DOWN[half][:, t * HID:(t + 1) * HID], sgT[c % 2][0:rows, m, tok:tok + P],
                                           sd[0:rows, m, :], start=(m == 0), stop=(m == 2))
                    mm.then_inc(ps_dn, 1)

            pe.wait_ge(shared_w_in, 16 * 5)
            pe.wait_ge(x1_done, HEAD + BATCH)
            turn_chunk(0)
            for c in range(1, CHUNKS):
                turn_chunk(c)
                router(c - 1)
            router(CHUNKS - 1)
            gate_up(0)
            gate_up(1)
            pe.wait_ge(masks_done, 1)
            pe.wait_ge(tri_step, 3)
            n = TILES * EXPERTS
            for at, weights in ((0, tri), (1, ones)):
                mm = pe.matmul(COUNTS[:, at * n:(at + 1) * n], weights[:], r3[0][:].rearrange("p t e -> p (t e)"),
                               start=True, stop=True)
            mm.then_inc(ps_cnt, 1)
            down(0)
            for c in range(2, CHUNKS):
                gate_up(c)
                down(c - 1)
            down(CHUNKS - 1)
            pe.wait_ge(z_evac, HEAD + 2 * CHUNKS)

            pe.wait_ge(ffn_w_in, 64)
            pe.wait_ge(pads_done, 2)
            pe.wait_ge(slots_known, 1)

            def turn_rows(n, r):
                half, u = r // 2, r % 2
                if u == 0:
                    pe.wait_ge(hb_in[half], n * 4 + 16 - 4 * r)
                pe.wait_ge(hbT_done, HEAD + n - 1)
                for k in range(KC):
                    mm = pe.transpose(ROWS[u][:, k * P:(k + 1) * P], hb[half][:, u, k * P:k * P + P], ident[:])
                mm.then_inc(psRows, 1)

            def expert(n):
                return pe.value_load(eid[0:1, ds(n, 1)], min_val=0, max_val=EXPERTS - 1)

            def expand(n, u, e):
                pe.wait_ge(hbT_done, HEAD + n + 1)
                pe.wait_ge(hg_done, HEAD + n - 1)
                for k in range(KC):
                    mm = pe.matmul(GU[u][:, 0:2 * INTER], hbT[u][:, k, :],
                                   wgu[:, k, ds(e, 1), :].rearrange("p o n -> p (o n)"), start=(k == 0), stop=(k == KC - 1))
                mm.then_inc(psGU, 1)

            def turn_product(n, u):
                pe.wait_ge(hg_done, HEAD + n + 1)
                pe.wait_ge(hgT_done, HEAD + n - 1)
                for s in range(2):
                    mm = pe.transpose(PROD[u][0:HPAD, s * P:(s + 1) * P], hg[u][:, s, :], ident[:])
                mm.then_inc(psProd, 1)

            def contract(n, u, e):
                pe.wait_ge(hgT_done, HEAD + n + 1)
                pe.wait_ge(ob_done, HEAD + n - 1)
                for s in range(2):
                    mm = pe.matmul(OUT[u][:, 0:HID], hgT[u][:, s, :],
                                   wd[:, s, ds(e, 1), :].rearrange("p o n -> p (o n)"), start=(s == 0), stop=(s == 1))
                mm.then_inc(psOut, 1)

            turn_rows(0, 0)
            turn_rows(1, 1)
            expand(0, 0, expert(0))

            def body(n, r, left):
                u = r % 2
                if left >= 1:
                    e = expert(n + 1)
                turn_product(n, u)
                if left >= 2:
                    turn_rows(n + 2, (r + 2) % 4)
                if left >= 1:
                    expand(n + 1, 1 - u, e)
                contract(n, u, expert(n))

            blocks(pe, body)

        @block.scalar
        def _(act):
            act.wait_ge(ct_in, 16)
            act.activation(esc[:], ct[:], ACT.Exp, scale=-1.0).then_inc(esc_done, 1)
            act.wait_ge(cols_done, 3)

            def modulate(b):
                act.wait_ge(psT, HEAD + b + 1)
                act.wait_ge(psV, HEAD + b)
                for k in range(KC):
                    act.activation(hT[:, k, :], SM[1][:, k * SEQ:(k + 1) * SEQ], ACT.Identity,
                                   bias=sa[:, k, ds(b, 1)], scale=ca1[:, k, ds(b, 1)]).then_inc(hT_done, 1)

            def keep_qk(b):
                act.wait_ge(split_lo, HEAD + b)
                for ready, done, src, at, scale in ((psQ, q_evac, MISC[0], 0, HDIM ** -0.5), (psK, k_evac, SM[0], 2, 1.0)):
                    act.wait_ge(ready, b + 1)
                    for c in range(2):
                        act.activation(qkf[:, at + c, :], src[:, c * SEQ:(c + 1) * SEQ], ACT.Identity,
                                       bias=bqk[:, at + c:at + c + 1], scale=scale).then_inc(done, 1)

            def negate_maxima(b):
                act.wait_ge(m_lo, HEAD + b)
                for qt in range(TPB):
                    act.wait_ge(psM, HEAD + b * 2 + (qt + 1))
                    act.activation(mneg[:, qt * P:qt * P + P], SM[qt][0:HEADS, 0:P], ACT.Copy, scale=-1.0).then_inc(mT_evac, 1)

            def exponentials(b, par):
                for h in range(HEADS):
                    g, j = h // 4, h % 4
                    act.wait_ge(psS, b * 16 + (h + 1))
                    if j == 0:
                        act.wait_ge(psPV, HEAD + b * 4 + (g - 1))
                    act.activation(probs[:, (g % 2) * 4 + j], ST[h % 2][:], ACT.Exp).then_inc(exp_done, 1)
                    if h in (11, 15):
                        half = (h - 11) // 4
                        act.wait_ge(psPV, HEAD + b * 4 + (2 * half + 2))
                        act.wait_ge(psOT, HEAD + b * 2)
                        act.activation(OT[:, 2 * half:2 * half + 2, :], PV[half][:], ACT.Copy).then_inc(pv_evac, 1)

            for b in range(3):
                modulate(b)
                keep_qk(b)
            negate_maxima(0)

            def body(b, par, left, in_line):
                exponentials(b, par)
                if left >= 1:
                    negate_maxima(b + 1)
                act.wait_ge(psOnT, HEAD + b + 1)
                act.wait_ge(psWo, HEAD + b)
                act.activation(OnT[:], MISC[0][:], ACT.Copy).then_inc(onT_evac, 1)
                if left >= 3:
                    modulate(b + 3)
                    keep_qk(b + 3)

            batches(act, body)

            def keep_turned(c):
                act.wait_ge(psT2, c * 2 + 1)
                act.activation(h2T[:, 0, c * CHUNK:(c + 1) * CHUNK], TURNED[c % 2][0][:], ACT.Copy).then_inc(h2T_a, 1)

            def keep_gate_up(c):
                for m, rows in enumerate(SHARED_ROWS):
                    j = 3 * c + m
                    act.wait_ge(ps_gu, j + 1)
                    if m == 0:
                        act.wait_ge(ps_dn, HEAD + 2 * (c - 1))
                    act.activation(sgT[c % 2][0:rows, m, :], GATE_UP[j % 2][0][0:rows, :], ACT.Silu).then_inc(gu_evac, 1)
                    if j >= 2:
                        act.wait_ge(sg_mul, j - 1)
                    act.activation(sup[j % 2][0:rows, :], GATE_UP[j % 2][1][0:rows, :], ACT.Copy).then_inc(gu_evac, 1)

            def keep_down(c):
                for half in range(2):
                    act.wait_ge(ps_dn, HEAD + c * 2 + half + 1)
                    act.activation(zsh[:, c * CT + 2 * half:c * CT + 2 * half + 2, :], DOWN[half][:], ACT.Copy).then_inc(z_evac, 1)

            act.wait_ge(x1_done, HEAD + BATCH)
            for c in range(CHUNKS):
                keep_turned(c)
            keep_gate_up(0)
            act.wait_ge(r_evac, 1)
            act.activation(r3[0][:], lg[:, :, EXPERTS:], ACT.Silu).then_inc(route_silu, 1)
            act.wait_ge(route_step, 4)
            act.activation(r3[2][:], r3[1][:], ACT.Exp).then_inc(route_exp, 1)
            keep_gate_up(1)
            keep_down(0)
            for c in range(2, CHUNKS):
                keep_gate_up(c)
                keep_down(c - 1)
            keep_down(CHUNKS - 1)
            def keep_rows(n, u):
                act.wait_ge(psRows, n + 1)
                act.wait_ge(psGU, HEAD + n - 1)
                act.activation(hbT[u][:], ROWS[u][:, 0:HID], ACT.Copy).then_inc(hbT_done, 1)

            keep_rows(0, 0)
            keep_rows(1, 1)

            def body(n, r, left):
                u = r % 2
                act.wait_ge(psGU, HEAD + n + 1)
                act.wait_ge(hg_done, HEAD + n - 1)
                act.activation(bsil[u][:], GU[u][:, 0:INTER], ACT.Silu).then_inc(bsil_done, 1)
                if left >= 2:
                    keep_rows(n + 2, u)

            blocks(act, body)

        @block.vector
        def _(dve):
            dve.memset(zero[:], 0.0).then_inc(zero_set, 1)
            for i in range(2):
                dve.memset(kst[i][0:STACK].bitcast(F32), 1.0).then_inc(const_done, 1)
                dve.memset(vst[i][:], 1.0).then_inc(const_done, 1)
            dve.wait_ge(esc_done, 1)
            dve.wait_ge(ct_in, 16)
            dve.tensor_scalar(esc[:], esc[:], 1.0, None, ALU.add).then_inc(siluc_step, 1)
            dve.wait_ge(siluc_step, 1)
            dve.reciprocal(rec[:], esc[:]).then_inc(siluc_step, 1)
            dve.wait_ge(siluc_step, 2)
            dve.tensor_tensor(siluc[:], ct[:], rec[:], ALU.mult).then_inc(siluc_step, 1)
            dve.wait_ge(x_in, 64)
            for t in range(TILES):
                dve.bn_stats(stats[:, t, :], x[:, t, :]).then_inc(stat_step, 1)
            for t in range(TILES):
                dve.wait_ge(stat_step, TILES)
                dve.bn_aggr(mv[:, t, :], stats[:, t, :]).then_inc(stat_step, 1)
            dve.wait_ge(ps_cols, 1)
            dve.tensor_copy(sa[:].rearrange("p k b -> p (k b)"), bank[3][:, 0:KC * BATCH]).then_inc(cols_done, 1)
            dve.tensor_scalar(ca1[:].rearrange("p k b -> p (k b)"), bank[3][:, KC * BATCH:2 * KC * BATCH], 1.0, None,
                              ALU.add).then_inc(cols_done, 1)
            dve.wait_ge(bqk_in, 16)
            dve.tensor_scalar(bqk[:, 0:2], bqk[:, 0:2], HDIM ** -0.5, None, ALU.mult).then_inc(cols_done, 1)
            dve.wait_ge(ps_mod, 3)
            for n in range(3):
                dve.tensor_copy(modr[:, n * 512:(n + 1) * 512], bank[n][0:BATCH, :]).then_inc(mod_raw, 1)
            dve.wait_ge(mod_raw, 3)
            for n, at in enumerate((2 * HID, 5 * HID)):
                g = modr[:, at:at + HID]
                dve.tensor_scalar(sgn[:, n, :], g, 0.0, 2.0, ALU.is_ge, ALU.mult).then_inc(floor_step, 1)
                dve.tensor_scalar(minus[:, n, :], g, -1.0, 0.25, ALU.mult, ALU.max).then_inc(floor_step, 1)
                dve.wait_ge(floor_step, 3 * n + 2)
                dve.tensor_tensor(g, g, minus[:, n, :], ALU.max).then_inc(floor_step, 1)
                dve.wait_ge(floor_step, 3 * n + 3)
                dve.scalar_tensor_tensor(out=g, in0=sgn[:, n, :], scalar=-1.0, in1=g, op0=ALU.add, op1=ALU.mult
                                         ).then_inc(modr_done, 1)
            dve.tensor_scalar(modr[:, 4 * HID:5 * HID], modr[:, 4 * HID:5 * HID], 1.0, None, ALU.add).then_inc(modr_done, 1)
            dve.wait_ge(rstd_done, 3)

            def normalise(b):
                dve.wait_ge(psT, HEAD + b)
                for t in range(TPB):
                    at = b * TPB + t
                    dve.tensor_scalar(z1[:, t, :], x[:, ds(at, 1), :].rearrange("p o d -> p (o d)"),
                                      mv[:, ds(at, 1), 0:1].rearrange("p o i -> p (o i)"), rstd[:, ds(at, 1)],
                                      ALU.subtract, ALU.mult).then_inc(z1_done, 1)

            def split(b):
                dve.wait_ge(q_evac, (b + 1) * 2)
                dve.wait_ge(k_evac, (b + 1) * 2)
                dve.wait_ge(stored, DMA_HEAD + b * 128)
                dve.tensor_copy(qks[:, 0], qkf[:]).then_inc(split_hi, 1)
                dve.wait_ge(split_hi, b + 1)
                dve.tensor_tensor(qks[:, 1], qkf[:], qks[:, 0].bitcast(F32), ALU.subtract).then_inc(split_lo, 1)

            def keep_v(b, par):
                dve.wait_ge(psV, HEAD + b + 1)
                for t in range(TPB):
                    dve.tensor_tensor(vst[par][:, t, :, 0:HDIM], SM[0][:, t * HID:(t + 1) * HID].rearrange(
                        "p (h d) -> p h d", h=HEADS), bvb[:].rearrange("p (h d) -> p h d", h=HEADS), ALU.add
                                      ).then_inc(v_done, 1)

            def max_unit(b, u):
                pair, qt = u // 2, u % 2
                if u == 0:
                    dve.wait_ge(psM, HEAD + b * 2)
                dve.wait_ge(psMax, b * 16 + (u + 1))
                dve.tensor_reduce(mx[:, qt, 2 * pair:2 * pair + 2], SM[qt][:].rearrange("p (h k) -> p h k", h=2),
                                  AX.X, ALU.max).then_inc(max_done, 1)

            def split_maxima(b):
                dve.wait_ge(mT_evac, HEAD + (b + 1) * 2)
                dve.wait_ge(mrow_in, DMA_HEAD + b * 32)
                dve.tensor_copy(mrow[:, 0, :], mneg[:]).then_inc(m_hi, 1)
                dve.wait_ge(m_hi, b + 1)
                dve.tensor_tensor(mrow[:, 1, :], mneg[:], mrow[:, 0, :].bitcast(F32), ALU.subtract).then_inc(m_lo, 1)

            def statistics2(b):
                dve.wait_ge(x1_done, HEAD + b + 1)
                first, last = b * TPB, (b + 1) * TPB
                for t in range(first, last):
                    dve.bn_stats(stats[:, t, :], x[:, t, :]).then_inc(stat2_step, 1)
                for t in range(first, last):
                    dve.wait_ge(stat2_step, first + last)
                    dve.bn_aggr(mv[:, t, :], stats[:, t, :]).then_inc(stat2_step, 1)

            def normalise2(b):
                dve.wait_ge(rstd2_done, 2 * b + 2)
                for t in range(b * TPB, (b + 1) * TPB):
                    dve.tensor_scalar(h2[:, t, :], x[:, t, :], mv[:, t, 0:1], rstd[:, t:t + 1],
                                      ALU.subtract, ALU.mult).then_inc(z2_done, 1)

            dve.wait_ge(attn_w_in, 16 * 8)
            normalise(0)
            normalise(1)
            split(0)
            keep_v(0, 0)
            normalise(2)
            split(1)
            keep_v(1, 1)
            split(2)
            for u in range(16):
                max_unit(0, u)
            split_maxima(0)

            def body(b, par, left, in_line):
                if left >= 3:
                    normalise(b + 3)
                if left >= 1:
                    for u in range(16):
                        max_unit(b + 1, u)
                    split_maxima(b + 1)
                for done in second_norms(b, in_line):
                    statistics2(done)
                for qt in range(TPB):
                    dve.wait_ge(psOT, HEAD + b * 2 + (qt + 1))
                    heads = MISC[qt][:].rearrange("p (h d) -> p h d", h=HEADS)
                    dve.reciprocal(rs[:, qt, :], heads[:, :, HDIM]).then_inc(rs_done, 1)
                    dve.wait_ge(rs_done, b * 2 + (qt + 1))
                    if qt == 0:
                        dve.wait_ge(psOnT, HEAD + b)
                    dve.tensor_tensor(On[:, qt, :].rearrange("p (h d) -> p h d", h=HEADS), heads[:, :, 0:HDIM],
                                      rs[:, qt, :].rearrange("p (h o) -> p h o", o=1).to_broadcast((P, HEADS, HDIM)),
                                      ALU.mult).then_inc(on_done, 1)
                if left >= 2:
                    keep_v(b + 2, par)
                dve.wait_ge(psWo, HEAD + b + 1)
                dve.wait_ge(x1_done, HEAD + b)
                dve.tensor_tensor(att[:], MISC[1][:].rearrange("p (t d) -> p t d", t=TPB),
                                  bob[:].rearrange("p (o d) -> p o d", o=1).to_broadcast((P, TPB, HID)), ALU.add
                                  ).then_inc(wo_evac, 1)
                if left >= 3:
                    split(b + 3)
                for done in second_norms(b, in_line):
                    normalise2(done)

            batches(dve, body)
            statistics2(LAST)
            normalise2(LAST)

            dve.wait_ge(x1_done, HEAD + BATCH)
            dve.wait_ge(psWo, HEAD + BATCH)
            for s in range(2):
                dve.memset(wd[64:HPAD, s], 0.0).then_inc(wd_pads_done, 1)
            for c in range(CHUNKS):
                dve.wait_ge(psT2, c * 2 + 2)
                dve.tensor_copy(h2T[:, 1, c * CHUNK:(c + 1) * CHUNK], TURNED[c % 2][1][:]).then_inc(h2T_v, 1)
            dve.wait_ge(ps_r, CHUNKS)
            dve.tensor_copy(lg[:].rearrange("p t e -> p (t e)"), LOGITS[:, 0:TILES * 2 * EXPERTS]).then_inc(r_evac, 1)

            steps = [0]

            def step(ins):
                steps[0] += 1
                ins.then_inc(route_step, 1)
                dve.wait_ge(route_step, steps[0])

            def rows(v):
                return v[:].rearrange("p (t o) -> p t o", o=1).to_broadcast((P, TILES, EXPERTS))

            def cols(v):
                return v.rearrange("p (o e) -> p o e", o=1).to_broadcast((P, TILES, EXPERTS))

            gate, logit, prob, biased, weight, tie, first_of, second_of = (r[:] for r in r3)
            dve.wait_ge(route_silu, 1)
            step(dve.tensor_tensor(logit, lg[:, :, 0:EXPERTS], gate, ALU.mult))
            step(dve.scalar_tensor_tensor(out=logit, in0=logit, scalar=-1.0, in1=logit, op0=ALU.mult, op1=ALU.max))
            step(dve.tensor_reduce(c1[0][:], logit, AX.X, ALU.max))
            step(dve.tensor_tensor(logit, logit, rows(c1[0]), ALU.subtract))
            dve.wait_ge(route_exp, 1)
            step(dve.tensor_reduce(c1[1][:], prob, AX.X, ALU.add))
            step(dve.reciprocal(c1[2][:], c1[1][:]))
            step(dve.tensor_tensor(prob, prob, rows(c1[2]), ALU.mult))
            step(dve.tensor_tensor(biased, prob, cols(ebias[:]), ALU.add))
            step(dve.tensor_tensor(weight, prob, cols(escale[:]), ALU.mult))
            step(dve.tensor_scalar(weight, weight, 1.0, None, ALU.add))
            dve.wait_ge(iota_step, 4)
            for onehot in (first_of, second_of):
                step(dve.tensor_reduce(c1[3][:], biased, AX.X, ALU.max))
                step(dve.tensor_tensor(tie, biased, rows(c1[3]), ALU.is_equal))
                step(dve.tensor_tensor(tie, tie, cols(iotaf[:]), ALU.mult))
                step(dve.tensor_reduce(c1[4][:], tie, AX.X, ALU.max))
                step(dve.tensor_tensor(onehot, tie, rows(c1[4]), ALU.is_equal))
                if onehot is first_of:
                    step(dve.scalar_tensor_tensor(out=biased, in0=onehot, scalar=-1e30, in1=biased, op0=ALU.mult, op1=ALU.add))
            dve.tensor_tensor(gate, first_of, second_of, ALU.add).then_inc(masks_done, 1)
            for choice, onehot in enumerate((first_of, second_of)):
                step(dve.tensor_tensor(tie, onehot, weight, ALU.mult))
                step(dve.tensor_reduce(wsel[:, choice, :], tie, AX.X, ALU.add))
            dve.wait_ge(ps_cnt, 1)
            step(dve.memset(cnt[:, 0, :], 0.0))
            for t in range(TILES):
                step(dve.tensor_tensor(cnt[:, t + 1, :], cnt[:, t, :], COUNTS[:, (TILES + t) * EXPERTS:(TILES + t + 1) * EXPERTS], ALU.add))
            step(dve.tensor_scalar(blk[:, 0, :], cnt[:, TILES, :], float(P - 1), None, ALU.add))
            step(dve.tensor_copy(blki[:], blk[:, 0, :]))
            step(dve.tensor_scalar(blki[:], blki[:], 7, None, ALU.logical_shift_right))
            step(dve.tensor_copy(blk[:, 1, :], blki[:]))
            step(dve.memset(cend[:], 0.0))
            for e in range(EXPERTS):
                step(dve.tensor_tensor(cend[:, e + 1:e + 2], cend[:, e:e + 1], blk[:, 1, e:e + 1], ALU.add))
            step(dve.tensor_scalar(blk[:, 2, :], cend[:, 0:EXPERTS], float(P), None, ALU.mult))
            step(dve.tensor_tensor(cnt[:, 0:TILES, :], cnt[:, 0:TILES, :], cols(blk[:, 2, :]), ALU.add))
            step(dve.tensor_tensor(prob, cnt[:, 0:TILES, :], COUNTS[:, 0:TILES * EXPERTS].rearrange("p (t e) -> p t e", e=EXPERTS), ALU.add))
            for choice, onehot in enumerate((first_of, second_of)):
                step(dve.tensor_tensor(tie, onehot, prob, ALU.mult))
                step(dve.tensor_reduce(slotf[:, choice, :], tie, AX.X, ALU.add))
            step(dve.tensor_copy(slot[:], slotf[:]))
            step(dve.tensor_tensor(bcmp[:], cend[:, 1:EXPERTS + 1].rearrange("p (o e) -> p o e", o=1).to_broadcast((P, BLOCKS, EXPERTS)),
                                   bnum[:].rearrange("p (b o) -> p b o", o=1).to_broadcast((P, BLOCKS, EXPERTS)), ALU.is_le))
            step(dve.tensor_reduce(eidf[:], bcmp[:], AX.X, ALU.add))
            step(dve.tensor_scalar(eidf[:], eidf[:], float(EXPERTS - 1), None, ALU.min))
            dve.tensor_copy(eid[:], eidf[:]).then_inc(slots_known, 1)
            for c in range(2, CHUNKS):
                for m, rows in enumerate(SHARED_ROWS):
                    gate_times_up(dve, c, m, rows)
            for u in range(2):
                dve.memset(hg[u][:], 0.0).then_inc(pads_done, 1)

            def product(n, u):
                dve.wait_ge(bsil_done, n + 1)
                dve.wait_ge(psProd, HEAD + n - 1)
                dve.tensor_tensor(hg[u][:, :, 0:HALF], bsil[u][:].rearrange("p (s n) -> p s n", s=2),
                                  GU[u][:, INTER:2 * INTER].rearrange("p (s n) -> p s n", s=2), ALU.mult
                                  ).then_inc(hg_done, 1)

            product(0, 0)

            def body(n, r, left):
                half, u = r // 2, r % 2
                dve.wait_ge(psProd, HEAD + n + 1)
                dve.wait_ge(psOut, HEAD + n - 1)
                dve.tensor_copy(hgT[u][:], PROD[u][0:HPAD, 0:2 * P]).then_inc(hgT_done, 1)
                if left >= 1:
                    product(n + 1, 1 - u)
                dve.wait_ge(psOut, HEAD + n + 1)
                if u == 0:
                    dve.wait_ge(ob_out[half], DMA_HEAD + n * 4 - 4 * r)
                dve.tensor_copy(ob[half][:, u, :], OUT[u][:, 0:HID]).then_inc(ob_done, 1)

            blocks(dve, body)
            dve.wait_ge(z_evac, HEAD + 2 * CHUNKS)
            for t in range(TILES):
                dve.wait_ge(picked_in[t], 32)
                z, g = zsh[:, t, :], modb[:, t // TPB, 3, :]
                for choice in range(2):
                    dve.scalar_tensor_tensor(out=z, in0=picked[:, t, choice, :], scalar=wsel[:, choice, t:t + 1], in1=z,
                                             op0=ALU.mult, op1=ALU.add).then_inc(sum_step, 1)
                    dve.wait_ge(sum_step, 3 * t + 1 + choice)
                dve.tensor_tensor(z, z, g, ALU.mult).then_inc(sum_step, 1)
                dve.wait_ge(sum_step, 3 * t + 3)
                dve.tensor_tensor(x[:, t, :], x[:, t, :], z, ALU.add).then_inc(result_done, 1)

        @block.gpsimd
        def _(pool):
            pool.memset(ident[:], 0.0).then_inc(ident_step, 1)
            pool.wait_ge(ident_step, 1)
            pool.affine_select(out=ident[:], in_=ident[:], compare_op=ALU.not_equal, fill=1.0, base=0,
                               pattern=[[-1, P]], channel_multiplier=1).then_inc(const_done, 1)
            pool.memset(neghalf[:], -0.5).then_inc(const_done, 1)
            for i in range(2):
                pool.memset(qst[i][0:MROW].bitcast(F32), 0.0).then_inc(const_done, 1)
            pool.wait_ge(stat_step, 2 * TILES)
            pool.tensor_scalar(rstd[:], mv[:, :, 1], EPS, None, ALU.add).then_inc(rstd_done, 1)
            pool.wait_ge(rstd_done, 1)
            pool.wait_ge(const_done, CONSTS)
            pool.tensor_tensor(rstd[:], rstd[:], neghalf[:], ALU.pow).then_inc(rstd_done, 2)
            pool.wait_ge(modb_in, 16)

            def residual(b):
                pool.wait_ge(wo_evac, HEAD + b + 1)
                pool.tensor_tensor(att2[:], att[:], modb[:, ds(b, 1), 0, :].to_broadcast((P, TPB, HID)), ALU.mult
                                   ).then_inc(ga_done, 1)
                pool.wait_ge(ga_done, b + 1)
                tiles = x[:, ds(b * TPB, TPB), :]
                pool.tensor_tensor(tiles, att2[:], tiles, ALU.add).then_inc(x1_done, 1)

            def deviation2(b):
                tiles = slice(b * TPB, (b + 1) * TPB)
                pool.wait_ge(stat2_step, 4 * (b + 1))
                pool.tensor_scalar(rstd[:, tiles], mv[:, tiles, 1], EPS, None, ALU.add).then_inc(rstd2_done, 1)
                pool.wait_ge(rstd2_done, 2 * b + 1)
                pool.tensor_tensor(rstd[:, tiles], rstd[:, tiles], neghalf[:, tiles], ALU.pow).then_inc(rstd2_done, 1)

            def modulate2(b):
                tiles = h2[:, b * TPB:(b + 1) * TPB, :]
                pool.wait_ge(z2_done, TPB * (b + 1))
                pool.tensor_tensor(tiles, tiles, modb[:, b:b + 1, 2, :].to_broadcast((P, TPB, HID)), ALU.mult
                                   ).then_inc(h2_step, 1)
                pool.wait_ge(h2_step, b + 1)
                pool.tensor_tensor(tiles, tiles, modb[:, b:b + 1, 1, :].to_broadcast((P, TPB, HID)), ALU.add
                                   ).then_inc(h2_done, 1)

            def body(b, par, left, in_line):
                for done in second_norms(b, in_line):
                    deviation2(done)
                residual(b)
                for done in second_norms(b, in_line):
                    modulate2(done)

            batches(pool, body)
            deviation2(LAST)
            modulate2(LAST)

            pool.iota(iotai[:], pattern=[[-1, EXPERTS]], base=EXPERTS, channel_multiplier=0).then_inc(iota_step, 1)
            pool.iota(bnumi[:], pattern=[[1, BLOCKS]], base=0, channel_multiplier=0).then_inc(iota_step, 1)
            pool.memset(tri[:], 0.0).then_inc(tri_step, 1)
            pool.memset(ones[:], 1.0).then_inc(tri_step, 1)
            pool.wait_ge(iota_step, 2)
            pool.wait_ge(tri_step, 2)
            pool.tensor_copy(iotaf[:], iotai[:]).then_inc(iota_step, 1)
            pool.tensor_copy(bnum[:], bnumi[:]).then_inc(iota_step, 1)
            pool.affine_select(out=tri[:], in_=tri[:], compare_op=ALU.is_ge, fill=1.0, base=0,
                               pattern=[[-1, P]], channel_multiplier=1).then_inc(tri_step, 1)
            for c in range(2):
                for m, rows in enumerate(SHARED_ROWS):
                    gate_times_up(pool, c, m, rows)
            pool.wait_ge(slots_known, 1)
            pool.wait_ge(slots_zeroed, 16)
            for t in range(TILES):
                for choice in range(2):
                    pool.indirect_dma_start(slots_in, bass.IndirectOffsetOnAxis(ap=slot[:, choice, t:t + 1], axis=0),
                                            h2[:, t, :], None).then_inc(scattered, 16)
            pool.wait_ge(ob_out[0], DMA_HEAD + 16 * ((BLOCKS + 3) // 4))
            pool.wait_ge(ob_out[1], DMA_HEAD + 16 * ((BLOCKS + 1) // 4))
            for t in range(TILES):
                for choice in range(2):
                    pool.indirect_dma_start(picked[:, t, choice, :], None, slots_out,
                                            bass.IndirectOffsetOnAxis(ap=slot[:, choice, t:t + 1], axis=0)
                                            ).then_inc(picked_in[t], 16)


def kernel(**inputs):
    import concourse.bacc as bacc
    from concourse.bass_utils import run_bass_kernel_spmd

    a = {n.replace("L0_", ""): np.asarray(v) for n, v in inputs.items()}
    arrays = host_layout(a)
    nc = bacc.Bacc("TRN2", target_bir_lowering=False, num_devices=1)
    args = [nc.dram_tensor(n, v.shape, mybir.dt.from_np(v.dtype), kind="ExternalInput").ap() for n, v in arrays.items()]
    out = nc.dram_tensor("out", (T, HID), F32, kind="ExternalOutput").ap()
    adaln_block(nc, *args, out)
    result = run_bass_kernel_spmd(nc, [arrays], core_ids=[0])
    return result.results[0]["out"].reshape(BATCH, SEQ, HID)


def host_layout(a):
    c = np.ascontiguousarray
    return {
        "in_x": c(a["attn_X"].reshape(T, HID)),
        "in_bqk": c(np.concatenate([a["attn_bq"], a["attn_bk"]]).reshape(2 * KC, P).T),
        "in_wq": a["attn_Wq"], "in_wk": a["attn_Wk"],
        "in_wv": a["attn_Wv"], "in_bv": a["attn_bv"], "in_wo": a["attn_Wo"], "in_bo": a["attn_bo"],
        "in_route": c(np.concatenate([a["ffn_cls_w"], a["ffn_gate_w"]]).T),
        "in_escale": a["ffn_extra_scale"], "in_ebias": a["ffn_extra_bias"],
        "in_wgu": c(np.concatenate([a["ffn_wg"], a["ffn_wu"]], axis=1).transpose(2, 0, 1)),
        "in_wd": c(a["ffn_wd"].transpose(0, 2, 1)),
        "in_sgu": c(np.concatenate([a["ffn_sg"], a["ffn_su"]]).T),
        "in_sd": c(a["ffn_sd"].T),
        "in_ct": c(a["c"].T), "in_wmod": a["wmod"],
    }
```

```python
from contextlib import ExitStack

import concourse.bass as bass
import concourse.mybir as mybir
import numpy as np

F32, F32R, I32, U32 = mybir.dt.float32, mybir.dt.float32r, mybir.dt.int32, mybir.dt.uint32
ACT = mybir.ActivationFunctionType
ALU = mybir.AluOpType
AX = mybir.AxisListType
ds = bass.ds

P = 128
BATCH, SEQ, HID = 8, 256, 256
HEADS, HDIM = 16, 16
T = BATCH * SEQ
TILES = T // P
TPB = SEQ // P
KC = HID // P
EXPERTS, INTER, SHARED = 14, 176, 352
HALF = INTER // 2
HPAD = 96
BLOCKS = (2 * T + EXPERTS * (P - 1)) // P
SLOTS = BLOCKS * P
QUADS = 8
EARLY_SUMS = BATCH - 2
assert 4 + 4 * QUADS + 4 <= BLOCKS
CHUNK = 512
CT = CHUNK // P
CHUNKS = T // CHUNK
MROW = 96
STACK = MROW + 2
EPS = 1e-5
HEAD, DMA_HEAD = 4, 16
STACK_CONSTS = 6
NORMS = {5: (0, 1, 2), 6: (3, 4), 7: (5,)}
ROUTED = 6
SHARED_ROWS = [P, P, SHARED - 2 * P]
EARLY = 4
UNITS_BEFORE = [0, 2, 1, 1, 1, 2, 2, 2, 1, 0, 0, 0, 0, 0, 0, 0]
UNITS = 16
WEIGHED_AT = (5, 9, 12)
assert EARLY + sum(UNITS_BEFORE) == UNITS


def adaln_block(nc, x_d, bqk_d, wq_d, wk_d, wv_d, bv_d, wo_d, bo_d, route_d, escale_d, ebias_d,
                wgu_d, wd_d, sgu_d, sd_d, ct_d, wmod_d, out_d):
    mod_scr = nc.dram_tensor("mod_scr", (BATCH, 4 * HID), F32, kind="Internal").ap()
    scr = [nc.dram_tensor(f"stack_scr{i}", (2, 2, HEADS, HDIM, SEQ), F32, kind="Internal").ap() for i in range(2)]
    h2_rows = nc.dram_tensor("h2_rows", (T, HID), F32, kind="Internal").ap()
    chosen = nc.dram_tensor("chosen", (1 + 2 * T + SLOTS, HID), F32, kind="Internal").ap()

    ctx = ExitStack()
    phase1, phase2 = ExitStack(), ExitStack()

    def sb(name, shape, dt=F32, where=None):
        return (where or ctx).enter_context(nc.sbuf_tensor(name, shape, dt))

    def flag(name):
        return ctx.enter_context(nc.semaphore(name))

    with ctx:
        x = sb("x", [P, TILES, HID])
        with nc.sbuf_tensor("at_pos", [P, 2 * TILES, P], F32R) as at_pos:
            pass
        h2 = sb("h2", [P, TILES, HID])
        ident = sb("ident", [P, P])
        modb = sb("modb", [P, BATCH, 4, HID])
        stats = sb("stats", [P, TILES, 6])
        mv = sb("mv", [P, TILES, 2])
        rstd = sb("rstd", [P, TILES])
        neghalf = sb("neghalf", [P, TILES])
        route_w = sb("route_w", [P, KC, 2 * EXPERTS])
        sd = sb("sd", [P, 3, HID])
        with nc.sbuf_tensor("in_block", [P, 2 * TILES, BLOCKS + 1], F32R) as in_block:
            pass
        h2Ta = sb("h2Ta", [P, KC, T // 2])
        lg = sb("lg", [P, TILES, 2 * EXPERTS])
        escale = sb("escale", [P, EXPERTS])
        ebias = sb("ebias", [P, EXPERTS])

        def sb1(name, shape, dt=F32):
            return sb(name, shape, dt, phase1)

        stacks = [sb1(name, [P, HEADS, SEQ], F32R) for name in ("qst0", "kst0", "qst1", "kst1")]
        qst, kst = stacks[0::2], stacks[1::2]
        probs = sb1("probs", [P, 8, TPB, SEQ])
        vst = [sb1(f"vst{i}", [P, TPB, HEADS, 32]) for i in range(2)]
        wq, wk, wv, wo = (sb1(n, [P, KC, HID]) for n in ("wq", "wk", "wv", "wo"))
        wmod = probs[:].rearrange("p j t q -> p (j t q)")[:, 0:KC * 6 * HID].rearrange("p (k n) -> p k n", k=KC)
        ct = sb1("ct", [P, KC, BATCH])
        esc = sb1("esc", [P, KC, BATCH])
        rec = sb1("rec", [P, KC, BATCH])
        siluc = sb1("siluc", [P, KC, BATCH])
        sa = sb1("sa", [P, KC, BATCH])
        ca1 = sb1("ca1", [P, KC, BATCH])
        modr = h2[0:BATCH, 0:6, :].rearrange("b m d -> b (m d)")
        sgn = h2[0:BATCH, 6:8, :]
        minus = h2[0:BATCH, 8:10, :]
        bqk = sb1("bqk", [P, 4])
        bvb = sb1("bvb", [P, HID])
        bob = sb1("bob", [P, HID])
        z1 = sb1("z1", [P, TPB, HID])
        hT = sb1("hT", [P, KC, SEQ])
        qkf = sb1("qkf", [P, 4, SEQ])
        qks = sb1("qks", [P, 2, 4, SEQ], F32R)
        mx = sb1("mx", [P, TPB, HEADS])
        mneg = sb1("mneg", [HEADS, SEQ])
        mrow = sb1("mrow", [HEADS, 2, SEQ], F32R)
        OT = sb1("OT", [P, 4, SEQ])
        rs = sb1("rs", [P, TPB, HEADS])
        On = sb1("On", [P, TPB, HID])
        OnT = sb1("OnT", [P, KC, SEQ])
        att = sb1("att", [P, TPB, HID])
        phase1.close()

        def sb2(name, shape, dt=F32):
            return sb(name, shape, dt, phase2)

        sgT = [sb2(f"sgT{i}", [P, 3, CHUNK]) for i in range(2)]
        sup = [sb2(f"sup{i}", [P, CHUNK]) for i in range(2)]
        phase3 = ExitStack()
        h2Tb = sb("h2Tb", [P, KC, T // 2], F32, phase3)
        sgu = sb("sgu", [P, KC, 2 * SHARED], F32, phase3)
        phase3.close()
        hb = [sb2(f"hb{i}", [P, HID]) for i in range(4)]
        hbT = [sb2(f"hbT{i}", [P, KC, P]) for i in range(2)]
        bsil = [sb2(f"bsil{i}", [P, INTER]) for i in range(2)]
        hg = [sb2(f"hg{i}", [P, 2, HPAD]) for i in range(2)]
        hgT = [sb2(f"hgT{i}", [HPAD, 2, P]) for i in range(2)]
        ob = [sb2(f"ob{i}", [P, HID]) for i in range(4)]
        wgu = sb2("wgu", [P, KC, EXPERTS, 2 * INTER])
        wd = sb2("wd", [HPAD, 2, EXPERTS, HID])
        zsh = sb2("zsh", [P, TILES, HID])
        r3 = [sb2(f"r{i}", [P, TILES, EXPERTS]) for i in range(7)]
        c1 = [sb2(f"c{i}", [P, TILES]) for i in range(5)]
        iotaf = sb2("iotaf", [P, EXPERTS])
        masks = sb2("masks", [P, TILES + 1, EXPERTS], F32R)
        tri = sb2("tri", [P, P], F32R)
        ones = sb2("ones", [P, P], F32R)
        before = sb2("before", [P, EXPERTS + 1, EXPERTS])
        posn = sb2("posn", [P, P])
        destn = sb2("destn", [P, 2, TILES])
        padn = sb2("padn", [P, BLOCKS])
        destf = sb2("destf", [P, BLOCKS])
        blk = sb2("blk", [P, 4, EXPERTS])
        blki = sb2("blki", [P, EXPERTS], I32)
        cend = sb2("cend", [P, EXPERTS + 1])
        bnum = sb2("bnum", [P, BLOCKS + 1])
        bcmp = sb2("bcmp", [P, BLOCKS, EXPERTS])
        ends = bcmp[:, 0:EXPERTS + 1, :]
        eidf = sb2("eidf", [P, BLOCKS])
        eid = sb2("eid", [P, BLOCKS], I32)
        slotf = sb2("slotf", [P, 2, TILES])
        sloti = sb2("sloti", [P, 2, TILES], I32)
        slot_block = sb2("slot_block", [P, 2, TILES])
        slot_pos = sb2("slot_pos", [P, 2, TILES])
        tokf = sb2("tokf", [P, BLOCKS])
        tok = sb2("tok", [P, BLOCKS], U32)
        dest = sb2("dest", [P, BLOCKS], U32)
        wsel = sb2("wsel", [P, 2, TILES])
        picked = wgu[:].rearrange("p k e n -> p (k e n)")[:, 0:TILES * 2 * HID].rearrange("p (c t d) -> p c t d", t=TILES, c=2)
        phase2.close()

        bank = [ctx.enter_context(nc.psum_tensor(f"bank{i}", [P, 512], F32)) for i in range(8)]
        ST, SM, PV, MISC = bank[0:2], bank[2:4], bank[4:6], bank[6:8]
        MOD_ROWS = (bank[0], bank[1], bank[4])
        GATE_UP, DOWN, COUNTS, TABLE = (bank[0:2], bank[4:6]), bank[6:8], bank[2], bank[3]
        ROWS, GU, PROD, OUT = bank[0:2], bank[2:4], bank[4:6], bank[6:8]

        def h2T(k, tokens):
            half = (h2Ta, h2Tb)[tokens.start // (T // 2)]
            return half[:, k, tokens.start % (T // 2):(tokens.stop - 1) % (T // 2) + 1]

        x_in = [flag(f"x_in{q}") for q in range(4)]
        bias_in = flag("bias_in")
        ct_in, wmod_in, wmod_rows_in, bqk_in = flag("ct_in"), flag("wmod_in"), flag("wmod_rows_in"), flag("bqk_in")
        shared_w_in, sgu_in = flag("shared_w_in"), flag("sgu_in")
        attn_w_in = flag("attn_w_in")
        ffn_w_in = flag("ffn_w_in")
        ident_done, neghalf_set, stack_set = flag("ident_done"), flag("neghalf_set"), flag("stack_set")
        ident_step = flag("ident_step")
        tri_step = flag("tri_step")
        stat_step = flag("stat_step")
        rstd_done = flag("rstd_done")
        rstd_step = flag("rstd_step")
        esc_done = flag("esc_done")
        siluc_step = flag("siluc_step")
        ps_mod, ps_cols = flag("ps_mod"), flag("ps_cols")
        mod_raw, floor_step, modr_done, cols_done = flag("mod_raw"), flag("floor_step"), flag("modr_done"), flag("cols_done")
        mod_stored = flag("mod_stored")
        modb_in = [flag(f"modb_in{i}") for i in range(2)]
        z1_done = flag("z1_done")
        psT, psQ, psK, psV = flag("psT"), flag("psQ"), flag("psK"), flag("psV")
        hT_done = flag("hT_done")
        q_evac, k_evac, v_done = flag("q_evac"), flag("k_evac"), flag("v_done")
        split_hi, split_lo = flag("split_hi"), flag("split_lo")
        stored = flag("stored")
        loaded_q, loaded_k = ([[flag(f"loaded_{side}{i}_{half}") for half in range(2)] for i in range(2)] for side in "qk")
        first_keys_in = [flag(f"first_keys_in{half}") for half in range(2)]
        psMax, max_done = flag("psMax"), flag("max_done")
        psM, mT_evac, m_hi, m_lo = flag("psM"), flag("mT_evac"), flag("m_hi"), flag("m_lo")
        mrow_in = flag("mrow_in")
        psS, exp_done = flag("psS"), flag("exp_done")
        psPV, pv_evac = flag("psPV"), flag("pv_evac")
        psOT, rs_done, on_done = flag("psOT"), flag("rs_done"), flag("on_done")
        psOnT, onT_evac = flag("psOnT"), flag("onT_evac")
        psWo, wo_evac = flag("psWo"), flag("wo_evac")
        ga_done, x1_done = flag("ga_done"), flag("x1_done")
        stat2_step, rstd2_done, z2_done, h2_step = flag("stat2_step"), flag("rstd2_done"), flag("z2_done"), flag("h2_step")
        h2_done = flag("h2_done")
        psT2, h2T_done = flag("psT2"), flag("h2T_done")
        ps_r, r_evac = flag("ps_r"), flag("r_evac")
        ps_gu, gu_evac, sg_mul = flag("ps_gu"), flag("gu_evac"), flag("sg_mul")
        ps_dn, z_evac = flag("ps_dn"), flag("z_evac")
        route_step, route_silu, route_exp = flag("route_step"), flag("route_silu"), flag("route_exp")
        masks_done, ps_cnt, slots_known, iota_step = flag("masks_done"), flag("ps_cnt"), flag("slots_known"), flag("iota_step")
        tables_done, ps_table, rows_known, h2_out = flag("tables_done"), flag("ps_table"), flag("rows_known"), flag("h2_out")
        hb_in = [flag(f"hb_in{r}") for r in range(4)]
        ob_out = [flag(f"ob_out{r}") for r in range(4)]
        psRows, hbT_done, psGU, bsil_done = flag("psRows"), flag("hbT_done"), flag("psGU"), flag("bsil_done")
        hg_done, psProd, hgT_done, psOut, ob_done = flag("hg_done"), flag("psProd"), flag("hgT_done"), flag("psOut"), flag("ob_done")
        pads_done, wd_pads_done = flag("pads_done"), flag("wd_pads_done")
        picked_in = [flag(f"picked_in{q}") for q in range(4)]
        weighted, summed, gated = flag("weighted"), flag("summed"), flag("gated")
        sum_step, result_done, stored_out = flag("sum_step"), flag("result_done"), flag("stored_out")
        ahead = [split_hi, exp_done, gu_evac, hbT_done, hg_done, mT_evac, m_lo, ob_done, onT_evac, q_evac, psOut, psProd, hgT_done, psM, psOT, psOnT, psPV, psT, psGU, psV, psWo, ps_dn, pv_evac, split_lo, v_done, wo_evac, x1_done, z_evac]
        dma_ahead = [stored, mrow_in]

        block = ctx.enter_context(nc.Block())
        LAST = BATCH - 1

        def batches(eng, body):
            body(0, 0, LAST, True)
            with eng.Fori(0, (BATCH - 4) // 2) as pair:
                for i in range(2):
                    body(pair * 2 + 1 + i, (1 + i) % 2, 3, False)
            for b in range(BATCH - 3, BATCH):
                body(b, b % 2, LAST - b, True)

        def load_parts(eng, stack, par, side, order, half, loaded):
            heads = slice(8 * half, 8 * half + 8)
            for i, part in enumerate(order):
                eng.dma_start(stack[HDIM * i:HDIM * (i + 1), heads].bitcast(F32),
                              scr[par][part, side, heads].rearrange("h d t -> d h t")).then_inc(loaded, 16)

        def second_norms(b, in_line):
            return NORMS.get(b, ()) if in_line else ()

        def gate_times_up(eng, j):
            c, m = j // 3, j % 3
            rows = SHARED_ROWS[m]
            eng.wait_ge(gu_evac, HEAD + 2 * (j + 1))
            if j > 0:
                eng.wait_ge(sg_mul, j)
            eng.tensor_tensor(sgT[c % 2][0:rows, m, :], sgT[c % 2][0:rows, m, :], sup[j % 2][0:rows, :], ALU.mult
                              ).then_inc(sg_mul, 1)

        def blocks(eng, body):
            for n in range(4):
                body(n, n, BLOCKS - 1 - n, None)
            with eng.Fori(0, EARLY_SUMS) as quad:
                for r in range(4):
                    body(quad * 4 + 4 + r, r, 4, quad)
            with eng.Fori(EARLY_SUMS, QUADS) as quad:
                for r in range(4):
                    body(quad * 4 + 4 + r, r, 4, None)
            for n in range(4 * QUADS + 4, BLOCKS):
                body(n, n % 4, BLOCKS - 1 - n, None)

        @block.sync
        def _(sp):
            for f in ahead:
                sp.sem_inc(f, HEAD)
            for f in dma_ahead:
                sp.sem_inc(f, DMA_HEAD)
            sp.dma_start(ct[:], ct_d.rearrange("(k p) b -> p k b", p=P)).then_inc(ct_in, 16)
            wmod_src = wmod_d.rearrange("(k p) n -> p k n", p=P)

            def load_x(q):
                n = TILES // 4
                sp.dma_start(x[:, n * q:n * q + n, :], x_d[n * q * P:n * (q + 1) * P, :].rearrange(
                    "(t p) d -> p t d", p=P)).then_inc(x_in[q], 16)

            load_x(0)
            sp.dma_start(wmod[:, :, 0:2 * HID], wmod_src[:, :, 0:2 * HID]).then_inc(wmod_in, 16)
            sp.dma_start(bqk[:], bqk_d).then_inc(bqk_in, 16)
            for tile, src in ((wq, wq_d), (wk, wk_d), (wv, wv_d), (wo, wo_d)):
                sp.dma_start(tile[:], src.rearrange("(k p) n -> p k n", p=P)).then_inc(attn_w_in, 16)
            load_x(1)
            sp.dma_start(wmod[:, :, 2 * HID:6 * HID], wmod_src[:, :, 2 * HID:6 * HID]).then_inc(wmod_rows_in, 16)
            load_x(2)
            load_x(3)
            for tile, src, n in ((bvb, bv_d, HID), (bob, bo_d, HID), (escale, escale_d, EXPERTS), (ebias, ebias_d, EXPERTS)):
                sp.dma_start(tile[:], src.rearrange("(o n) -> o n", o=1).to_broadcast((P, n))).then_inc(bias_in, 16)

            def store_parts(b, par, first=False, in_prologue=False):
                b_is_2 = not first and in_prologue
                for part, done in ((0, split_hi), (1, split_lo)):
                    sp.wait_ge(done, HEAD + b + 1)
                    if not first:
                        for half in range(2):
                            sp.wait_ge(loaded_q[par][half], (b - 2 - par) * 24 + 48)
                            if b_is_2:
                                sp.wait_ge(first_keys_in[half], 48)
                            else:
                                sp.wait_ge(loaded_k[par][half], (b - 2 - par) * 24 + 48 * par)
                    sp.dma_start(scr[par][part].rearrange("s (c h) d t -> (h d) (s c) t", c=2),
                                 qks[:, part].bitcast(F32)).then_inc(stored, 16)

            def load_queries(b, par, half):
                sp.wait_ge(stored, DMA_HEAD + (b + 1) * 32)
                load_parts(sp, qst[par], par, 0, (1, 0, 0), half, loaded_q[par][half])

            def store_h2(b):
                sp.wait_ge(h2_done, b + 1)
                sp.dma_start(h2_rows[b * SEQ:(b + 1) * SEQ, :].rearrange("(t p) d -> p t d", p=P),
                             h2[:, b * TPB:(b + 1) * TPB, :]).then_inc(h2_out, 16)

            def place_maxima(b, par):
                sp.wait_ge(m_lo, HEAD + b + 1)
                for part in range(2):
                    sp.dma_start(qst[par][MROW + part:MROW + part + 1].bitcast(F32),
                                 mrow[:, part, :].bitcast(F32)).then_inc(mrow_in, 16)

            store_parts(0, 0, first=True)
            sp.wait_ge(stack_set, STACK_CONSTS)
            load_queries(0, 0, 0)
            load_queries(0, 0, 1)
            store_parts(1, 1, first=True)
            load_queries(1, 1, 0)
            place_maxima(0, 0)

            def body(b, par, left, in_line):
                if left == 0:
                    sp.wait_ge(psS, b * UNITS)
                    sp.dma_start(sgu[:], sgu_d.rearrange("(k p) n -> p k n", p=P)).then_inc(sgu_in, 16)
                    for done in range(LAST - 2):
                        store_h2(done)
                if left >= 1:
                    if not (in_line and b == 0):
                        sp.wait_ge(psS, b * UNITS)
                    load_queries(b + 1, 1 - par, 1)
                if left >= 2:
                    store_parts(b + 2, par, in_prologue=in_line and b == 0)
                    sp.wait_ge(psS, b * UNITS + UNITS // 2)
                    load_queries(b + 2, par, 0)
                if left >= 1:
                    place_maxima(b + 1, 1 - par)
                if in_line and b == 0:
                    sp.wait_ge(modr_done, 3)
                    sp.dma_start(mod_scr, modr[:, 2 * HID:6 * HID]).then_inc(mod_stored, 16)
                    sp.wait_ge(mod_stored, 16)
                    sp.dma_start(route_w[:], route_d.rearrange("(k p) n -> p k n", p=P)).then_inc(shared_w_in, 16)
                    for m, rows in enumerate(SHARED_ROWS):
                        sp.dma_start(sd[0:rows, m, :], sd_d[m * P:m * P + rows, :]).then_inc(shared_w_in, 16)

                if not (in_line and b < 2):
                    sp.wait_ge(x1_done, HEAD + b - 1)
                sp.dma_start(modb[:, ds(b, 1)].rearrange("p b m d -> p (b m d)"), mod_scr[ds(b, 1), :].to_broadcast(
                    (P, 4 * HID))).then_inc(modb_in[par], 16)

            batches(sp, body)
            store_h2(LAST - 2)
            sp.wait_ge(x1_done, HEAD + BATCH)
            sp.wait_ge(mrow_in, DMA_HEAD + 32 * BATCH)
            for k in range(KC):
                sp.dma_start(wgu[:, k], wgu_d[k * P:(k + 1) * P]).then_inc(ffn_w_in, 16)
            sp.wait_ge(wd_pads_done, 1)
            for s in range(2):
                sp.dma_start(wd[0:HALF, s], wd_d[:, s * HALF:(s + 1) * HALF, :].rearrange("e p n -> p e n")).then_inc(ffn_w_in, 16)
            for b in range(LAST - 1, BATCH):
                store_h2(b)
            for r in range(4):
                sp.wait_ge(ob_out[r], 16 * ((BLOCKS - r + 3) // 4))
            n = TILES // 4
            for q in range(4):
                for choice in range(2):
                    at = 1 + choice * T + q * n * P
                    sp.dma_start(picked[:, choice, q * n:(q + 1) * n, :],
                                 chosen[at:at + n * P, :].rearrange("(t p) d -> p t d", p=P)).then_inc(picked_in[q], 16)
            for t in range(0, TILES, 2):
                sp.wait_ge(result_done, t + 2)
                sp.dma_start(out_d[t * P:(t + 2) * P, :].rearrange("(t p) d -> p t d", p=P), x[:, t:t + 2, :]
                             ).then_inc(stored_out, 16)
            sp.wait_ge(stored_out, 8 * TILES)

        @block.tensor
        def _(pe):
            def modulation_columns():
                for n in range(2 * KC):
                    for k in range(KC):
                        mm = pe.matmul(bank[3][:, n * BATCH:(n + 1) * BATCH], wmod[:, k, n * P:(n + 1) * P], siluc[:, k, :],
                                       start=(k == 0), stop=(k == KC - 1))
                mm.then_inc(ps_cols, 1)

            def modulation_rows(n):
                for k in range(KC):
                    mm = pe.matmul(MOD_ROWS[n][0:BATCH, :], siluc[:, k, :], wmod[:, k, n * 512:n * 512 + 512],
                                   start=(k == 0), stop=(k == KC - 1))
                mm.then_inc(ps_mod, 1)

            def turn_tokens(b):
                pe.wait_ge(z1_done, (b + 1) * 2)
                pe.wait_ge(onT_evac, HEAD + b - 3)
                pe.wait_ge(q_evac, HEAD + b * 2)
                for t in range(TPB):
                    for k in range(KC):
                        mm = pe.transpose(MISC[0][:, k * SEQ + t * P:k * SEQ + t * P + P], z1[:, t, k * P:k * P + P], ident[:])
                mm.then_inc(psT, 1)

            def project(w, out, ready):
                for c in range(2):
                    for k in range(KC):
                        mm = pe.matmul(out[:, c * SEQ:(c + 1) * SEQ], w[:, k, c * P:c * P + P], hT[:, k, :],
                                       start=(k == 0), stop=(k == KC - 1))
                mm.then_inc(ready, 1)

            def project_q(b):
                pe.wait_ge(hT_done, (b + 1) * 2)
                project(wq, MISC[0], psQ)

            def project_k(b):
                pe.wait_ge(v_done, HEAD + b * 2)
                project(wk, MISC[1], psK)

            def project_v(b):
                pe.wait_ge(k_evac, (b + 1) * 2)
                pe.wait_ge(wo_evac, HEAD + b - 2)
                for t in range(TPB):
                    for k in range(KC):
                        mm = pe.matmul(MISC[1][:, t * HID:(t + 1) * HID], hT[:, k, t * P:t * P + P], wv[:, k, :],
                                       start=(k == 0), stop=(k == KC - 1))
                mm.then_inc(psV, 1)

            def max_unit(b, par, u, in_prologue=False):
                pair, qt = u // 2, u % 2
                if u % (UNITS // 2) == 0:
                    half = u // (UNITS // 2)
                    pe.wait_ge(loaded_q[par][half], b * 24 + 48 - 24 * par)
                    if in_prologue:
                        pe.wait_ge(first_keys_in[half], 48)
                    else:
                        pe.wait_ge(loaded_k[par][half], b * 24 + 24 * par)
                if u < 2:
                    pe.wait_ge(mT_evac, HEAD + b * 2 - 1 + u)
                else:
                    pe.wait_ge(max_done, b * UNITS + (u - 1))
                for i in range(2):
                    h = 2 * pair + i
                    mm = pe.matmul(SM[qt][:, i * SEQ:(i + 1) * SEQ], qst[par][0:MROW, h, qt * P:qt * P + P],
                                   kst[par][0:MROW, h, :], start=True, stop=True)
                mm.then_inc(psMax, 1)

            def turn_maxima(b):
                pe.wait_ge(max_done, (b + 1) * UNITS)
                for qt in range(TPB):
                    pe.transpose(SM[qt][0:HEADS, 0:P], mx[:, qt, :], ident[:]).then_inc(psM, 1)

            def scores(b, par, h):
                if h == 0:
                    pe.wait_ge(mrow_in, DMA_HEAD + (b + 1) * 32)
                pe.wait_ge(exp_done, HEAD + b * 16 + (h - 1))
                for kt in range(TPB):
                    mm = pe.matmul(ST[h % 2][:, kt * SEQ:(kt + 1) * SEQ], kst[par][0:STACK, h, kt * P:kt * P + P],
                                   qst[par][0:STACK, h, :], start=True, stop=True)
                mm.then_inc(psS, 1)

            def weigh(b, par, g):
                if g == 0:
                    pe.wait_ge(v_done, HEAD + (b + 1) * 2)
                if g % 2 == 0:
                    pe.wait_ge(pv_evac, HEAD + b * 2 + (g // 2 - 1))
                pe.wait_ge(exp_done, HEAD + b * 16 + (4 * g + 4))
                for kt in range(TPB):
                    for j in range(4):
                        mm = pe.matmul(PV[g // 2][32 * j:32 * j + 32, (g % 2) * SEQ:(g % 2 + 1) * SEQ],
                                       vst[par][:, kt, 4 * g + j, :], probs[:, (g % 2) * 4 + j, kt, :],
                                       start=(kt == 0), stop=(kt == TPB - 1))
                mm.then_inc(psPV, 1)

            def turn_output(b, left):
                pe.wait_ge(pv_evac, HEAD + (b + 1) * 2)
                if left >= 2:
                    pe.wait_ge(q_evac, HEAD + (b + 4) * 2)
                    pe.wait_ge(k_evac, (b + 4) * 2)
                else:
                    pe.wait_ge(onT_evac, HEAD + b)
                    pe.wait_ge(wo_evac, HEAD + b)
                    pe.wait_ge(v_done, HEAD + 2 * min(b + 3, BATCH))
                for qt in range(TPB):
                    for g in range(4):
                        mm = pe.transpose(MISC[qt][:, g * P:(g + 1) * P], OT[:, g, qt * P:qt * P + P], ident[:])
                    mm.then_inc(psOT, 1)

            def turn_back(b):
                pe.wait_ge(on_done, (b + 1) * 2)
                for t in range(TPB):
                    for k in range(KC):
                        mm = pe.transpose(MISC[0][:, k * SEQ + t * P:k * SEQ + t * P + P], On[:, t, k * P:k * P + P], ident[:])
                mm.then_inc(psOnT, 1)

            def project_out(b):
                pe.wait_ge(onT_evac, HEAD + b + 1)
                for t in range(TPB):
                    for k in range(KC):
                        mm = pe.matmul(MISC[1][:, t * HID:(t + 1) * HID], OnT[:, k, t * P:t * P + P], wo[:, k, :],
                                       start=(k == 0), stop=(k == KC - 1))
                mm.then_inc(psWo, 1)

            pe.wait_ge(siluc_step, 3)
            pe.wait_ge(wmod_in, 16)
            modulation_columns()
            pe.wait_ge(ident_done, 1)
            turn_tokens(0)
            pe.wait_ge(attn_w_in, 16 * 4)
            project_q(0)
            project_k(0)
            turn_tokens(1)
            project_v(0)
            project_q(1)
            project_k(1)
            project_v(1)
            turn_tokens(2)
            pe.wait_ge(cols_done, 3)
            pe.wait_ge(wmod_rows_in, 16)
            for u in range(UNITS):
                max_unit(0, 0, u, in_prologue=True)
                if u % 4 == 3 and u // 4 < 3:
                    modulation_rows(u // 4)
            turn_maxima(0)

            for u in range(EARLY):
                max_unit(1, 1, u)
            pe.wait_ge(mod_raw, 3)

            def turn_second(b):
                pe.wait_ge(h2_done, b + 1)
                if b == 0:
                    pe.wait_ge(mT_evac, HEAD + 2 * BATCH)
                else:
                    pe.wait_ge(h2T_done, b)
                for k in range(KC):
                    for t in range(TPB):
                        mm = pe.transpose(SM[0][:, k * SEQ + t * P:k * SEQ + t * P + P], h2[:, b * TPB + t, k * P:k * P + P], ident[:])
                mm.then_inc(psT2, 1)

            def router(b):
                pe.wait_ge(h2T_done, b + 1)
                if b > 0:
                    pe.wait_ge(r_evac, b)
                for t in range(TPB):
                    at = (b * TPB + t) * P
                    for k in range(KC):
                        mm = pe.matmul(SM[1][:, t * 2 * EXPERTS:(t + 1) * 2 * EXPERTS], h2T(k, slice(at, at + P)),
                                       route_w[:, k, :], start=(k == 0), stop=(k == KC - 1))
                mm.then_inc(ps_r, 1)

            def body(b, par, left, in_line):
                previous = not (in_line and b == 0)
                u = EARLY
                for h in range(HEADS):
                    if left == 0 and h == 0:
                        pe.wait_ge(shared_w_in, 16 * 4)
                    if left == 0 and h % 2 == 1 and h // 2 < ROUTED:
                        turn_second(h // 2)
                    if left == 0 and h % 2 == 0 and 0 < h // 2 <= ROUTED:
                        router(h // 2 - 1)
                    if left >= 1:
                        for _ in range(UNITS_BEFORE[h]):
                            max_unit(b + 1, 1 - par, u)
                            u += 1
                    scores(b, par, h)
                    if h == 0 and left >= 2:
                        project_q(b + 2)
                    if h == 1 and left >= 2:
                        project_k(b + 2)
                    if h in WEIGHED_AT:
                        weigh(b, par, WEIGHED_AT.index(h))
                    if h == 5 and previous:
                        turn_output(b - 1, left)
                    if h == 9 and left >= 1:
                        turn_maxima(b + 1)
                    if h == 10 and previous:
                        turn_back(b - 1)
                    if h == 13 and previous:
                        project_out(b - 1)
                if left >= 2:
                    project_v(b + 2)
                if left >= 3:
                    turn_tokens(b + 3)
                if left >= 2:
                    max_unit(b + 2, par, 0)
                    max_unit(b + 2, par, 1)
                weigh(b, par, 3)
                if left >= 2:
                    max_unit(b + 2, par, 2)
                    max_unit(b + 2, par, 3)

            batches(pe, body)

            def gate_up(j, sides=(0, 1)):
                c, m = j // 3, j % 3
                rows = SHARED_ROWS[m]
                pe.wait_ge(h2T_done, (c + 1) * CT // TPB)
                if sides == (1,):
                    pass
                elif j < 2:
                    pe.wait_ge((exp_done, pv_evac)[j], HEAD + BATCH * (HEADS, 2)[j])
                else:
                    pe.wait_ge(gu_evac, HEAD + 2 * (j - 1))
                for side in sides:
                    at = side * SHARED + m * P
                    for k in range(KC):
                        mm = pe.matmul(GATE_UP[j % 2][side][0:rows, :], sgu[:, k, at:at + rows],
                                       h2T(k, slice(c * CHUNK, (c + 1) * CHUNK)), start=(k == 0), stop=(k == KC - 1))
                if 1 in sides:
                    mm.then_inc(ps_gu, 1)

            def down(c):
                pe.wait_ge(sg_mul, 3 * (c + 1))
                if c == 0:
                    pe.wait_ge(wo_evac, HEAD + BATCH)
                for half in range(2):
                    pe.wait_ge(z_evac, HEAD + 2 * (c - 1) + half + 1)
                    for t in range(2):
                        tok = (2 * half + t) * P
                        for m, rows in enumerate(SHARED_ROWS):
                            mm = pe.matmul(DOWN[half][:, t * HID:(t + 1) * HID], sgT[c % 2][0:rows, m, tok:tok + P],
                                           sd[0:rows, m, :], start=(m == 0), stop=(m == 2))
                    mm.then_inc(ps_dn, 1)

            pe.wait_ge(sgu_in, 16)
            turn_output(LAST, -1)
            gate_up(0, sides=(0,))
            turn_back(LAST)
            project_out(LAST)
            gate_up(0, sides=(1,))
            turn_second(ROUTED)
            router(ROUTED)
            gate_up(1)
            turn_second(LAST)
            router(LAST)
            for j in range(2, 6):
                gate_up(j)
            down(0)
            gate_up(6)
            pe.wait_ge(masks_done, 2)
            pe.wait_ge(tri_step, 3)
            pe.matmul(COUNTS[:, 0:(TILES + 1) * EXPERTS], tri[:], masks[:].rearrange("p t e -> p (t e)"), start=True, stop=False)
            for t in range(TILES):
                mm = pe.matmul(COUNTS[:, (t + 1) * EXPERTS:(TILES + 1) * EXPERTS], ones[:],
                               masks[:, t:t + 1, :].to_broadcast((P, TILES - t, EXPERTS)), start=False, stop=(t == TILES - 1))
            mm.then_inc(ps_cnt, 1)
            gate_up(7)
            gate_up(8)
            down(1)
            for j in range(9, 12):
                gate_up(j)
            for i in range(2 * TILES):
                pe.wait_ge(tables_done, 2 * (i + 1))
                mm = pe.matmul(TABLE[:, 0:BLOCKS + 1], at_pos[:, i, :], in_block[:, i, :], start=(i == 0), stop=(i == 2 * TILES - 1))
            mm.then_inc(ps_table, 1)
            down(2)
            pe.wait_ge(z_evac, HEAD + 2 * (CHUNKS - 1))

            pe.wait_ge(ffn_w_in, 64)
            pe.wait_ge(pads_done, 2)
            pe.wait_ge(slots_known, 1)

            def turn_rows(n, r):
                u = r % 2
                pe.wait_ge(hb_in[r], n * 4 + 16 - 4 * r)
                pe.wait_ge(hbT_done, HEAD + n - 1)
                for k in range(KC):
                    mm = pe.transpose(ROWS[u][:, k * P:(k + 1) * P], hb[r][:, k * P:k * P + P], ident[:])
                mm.then_inc(psRows, 1)

            def expert(n):
                return pe.value_load(eid[0:1, ds(n, 1)], min_val=0, max_val=EXPERTS - 1)

            def expand(n, u, e):
                pe.wait_ge(hbT_done, HEAD + n + 1)
                pe.wait_ge(hg_done, HEAD + n - 1)
                for k in range(KC):
                    mm = pe.matmul(GU[u][:, 0:2 * INTER], hbT[u][:, k, :],
                                   wgu[:, k, ds(e, 1), :].rearrange("p o n -> p (o n)"), start=(k == 0), stop=(k == KC - 1))
                mm.then_inc(psGU, 1)

            def turn_product(n, u):
                pe.wait_ge(hg_done, HEAD + n + 1)
                pe.wait_ge(hgT_done, HEAD + n - 1)
                for s in range(2):
                    mm = pe.transpose(PROD[u][0:HPAD, s * P:(s + 1) * P], hg[u][:, s, :], ident[:])
                mm.then_inc(psProd, 1)

            def contract(n, u, e):
                pe.wait_ge(hgT_done, HEAD + n + 1)
                pe.wait_ge(ob_done, HEAD + n - 1)
                for s in range(2):
                    mm = pe.matmul(OUT[u][:, 0:HID], hgT[u][:, s, :],
                                   wd[:, s, ds(e, 1), :].rearrange("p o n -> p (o n)"), start=(s == 0), stop=(s == 1))
                mm.then_inc(psOut, 1)

            turn_rows(0, 0)
            turn_rows(1, 1)
            expand(0, 0, expert(0))

            def body(n, r, left, batch):
                u = r % 2
                if left >= 1:
                    e = expert(n + 1)
                if left >= 2:
                    turn_rows(n + 2, (r + 2) % 4)
                turn_product(n, u)
                if left >= 1:
                    expand(n + 1, 1 - u, e)
                contract(n, u, expert(n))

            blocks(pe, body)
            pe.wait_ge(ob_done, HEAD + BLOCKS)
            down(3)

        @block.scalar
        def _(act):
            act.wait_ge(ct_in, 16)
            act.activation(esc[:], ct[:], ACT.Exp, scale=-1.0).then_inc(esc_done, 1)
            act.wait_ge(cols_done, 3)

            def modulate(b):
                act.wait_ge(psT, HEAD + b + 1)
                act.wait_ge(psV, HEAD + b)
                for k in range(KC):
                    act.activation(hT[:, k, :], MISC[0][:, k * SEQ:(k + 1) * SEQ], ACT.Identity,
                                   bias=sa[:, k, ds(b, 1)], scale=ca1[:, k, ds(b, 1)]).then_inc(hT_done, 1)

            def keep_q(b):
                act.wait_ge(split_lo, HEAD + b)
                act.wait_ge(psQ, b + 1)
                for c in range(2):
                    act.activation(qkf[:, c, :], MISC[0][:, c * SEQ:(c + 1) * SEQ], ACT.Identity,
                                   bias=bqk[:, c:c + 1], scale=HDIM ** -0.5).then_inc(q_evac, 1)

            def keep_k(b):
                act.wait_ge(psK, b + 1)
                for c in range(2):
                    act.activation(qkf[:, 2 + c, :], MISC[1][:, c * SEQ:(c + 1) * SEQ], ACT.Identity,
                                   bias=bqk[:, 2 + c:3 + c]).then_inc(k_evac, 1)

            def negate_maxima(b):
                act.wait_ge(m_lo, HEAD + b)
                for qt in range(TPB):
                    act.wait_ge(psM, HEAD + b * 2 + (qt + 1))
                    act.activation(mneg[:, qt * P:qt * P + P], SM[qt][0:HEADS, 0:P], ACT.Copy, scale=-1.0).then_inc(mT_evac, 1)

            def exponential(b, h):
                g, j = h // 4, h % 4
                act.wait_ge(psS, b * 16 + (h + 1))
                if j == 0:
                    act.wait_ge(psPV, HEAD + b * 4 + (g - 1))
                act.activation(probs[:, (g % 2) * 4 + j], ST[h % 2][:], ACT.Exp).then_inc(exp_done, 1)

            def keep_weighed(b, half):
                act.wait_ge(psPV, HEAD + b * 4 + (2 * half + 2))
                act.wait_ge(psOT, HEAD + b * 2)
                act.activation(OT[:, 2 * half:2 * half + 2, :], PV[half][:], ACT.Copy).then_inc(pv_evac, 1)

            def keep_turned_output(b):
                act.wait_ge(psOnT, HEAD + b + 1)
                act.wait_ge(psWo, HEAD + b)
                act.activation(OnT[:], MISC[0][:], ACT.Copy).then_inc(onT_evac, 1)

            def load_keys(b, par, half):
                act.wait_ge(stored, DMA_HEAD + (b + 1) * 32)
                load_parts(act, kst[par], par, 1, (0, 0, 1), half, loaded_k[par][half])

            modulate(0)
            keep_q(0)
            keep_k(0)
            modulate(1)
            act.wait_ge(stack_set, STACK_CONSTS)
            act.wait_ge(stored, DMA_HEAD + 32)
            load_parts(act, kst[0], 0, 1, (0, 0, 1), 0, first_keys_in[0])
            keep_q(1)
            keep_k(1)
            modulate(2)
            load_keys(1, 1, 0)
            for n in range(3):
                act.wait_ge(ps_mod, n + 1)
                act.activation(modr[:, n * 512:(n + 1) * 512], MOD_ROWS[n][0:BATCH, :], ACT.Copy).then_inc(mod_raw, 1)
            negate_maxima(0)

            def body(b, par, left, in_line):
                previous = not (in_line and b == 0)
                if left >= 1:
                    load_keys(b + 1, 1 - par, 1)
                for h in range(HEADS):
                    exponential(b, h)
                    if h == 2 and left >= 2:
                        keep_q(b + 2)
                    if h == 3 and left >= 2:
                        keep_k(b + 2)
                    if h == 10 and left >= 1:
                        negate_maxima(b + 1)
                    if h == 12 and previous:
                        keep_turned_output(b - 1)
                    if h == 11:
                        keep_weighed(b, 0)
                    if h == 13 and left >= 2:
                        load_keys(b + 2, par, 0)
                if left >= 3:
                    modulate(b + 3)
                keep_weighed(b, 1)

            batches(act, body)

            def keep_gate_up(j):
                c, m = j // 3, j % 3
                rows = SHARED_ROWS[m]
                act.wait_ge(ps_gu, j + 1)
                if m == 0:
                    act.wait_ge(ps_dn, HEAD + 2 * (c - 1))
                act.activation(sgT[c % 2][0:rows, m, :], GATE_UP[j % 2][0][0:rows, :], ACT.Silu).then_inc(gu_evac, 1)
                if j >= 2:
                    act.wait_ge(sg_mul, j - 1)
                act.activation(sup[j % 2][0:rows, :], GATE_UP[j % 2][1][0:rows, :], ACT.Copy).then_inc(gu_evac, 1)

            def keep_down(c):
                for half in range(2):
                    act.wait_ge(ps_dn, HEAD + c * 2 + half + 1)
                    act.activation(zsh[:, c * CT + 2 * half:c * CT + 2 * half + 2, :], DOWN[half][:], ACT.Copy).then_inc(z_evac, 1)

            keep_turned_output(LAST)
            keep_gate_up(0)
            keep_gate_up(1)
            act.wait_ge(x1_done, HEAD + BATCH)
            act.wait_ge(r_evac, BATCH)
            act.activation(r3[0][:], lg[:, :, EXPERTS:], ACT.Silu).then_inc(route_silu, 1)
            keep_gate_up(2)
            act.wait_ge(route_step, 4)
            act.activation(r3[2][:], r3[1][:], ACT.Exp).then_inc(route_exp, 1)
            for j in range(3, 6):
                keep_gate_up(j)
            keep_down(0)
            for j in range(6, 9):
                keep_gate_up(j)
            keep_down(1)
            for j in range(9, 12):
                keep_gate_up(j)
            keep_down(2)
            def keep_rows(n, u):
                act.wait_ge(psRows, n + 1)
                act.wait_ge(psGU, HEAD + n - 1)
                act.activation(hbT[u][:], ROWS[u][:, 0:HID], ACT.Copy).then_inc(hbT_done, 1)

            keep_rows(0, 0)
            keep_rows(1, 1)

            def body(n, r, left, batch):
                u = r % 2
                act.wait_ge(psGU, HEAD + n + 1)
                act.wait_ge(hg_done, HEAD + n - 1)
                act.activation(bsil[u][:], GU[u][:, 0:INTER], ACT.Silu).then_inc(bsil_done, 1)
                if left >= 2:
                    keep_rows(n + 2, u)

            blocks(act, body)
            keep_down(3)
            for t in range(TILES):
                act.wait_ge(picked_in[t // 4], 32)
                act.activation(picked[:, 0, t, :], picked[:, 0, t, :], ACT.Copy, scale=wsel[:, 0, t:t + 1]).then_inc(weighted, 1)

        @block.vector
        def _(dve):
            dve.wait_ge(esc_done, 1)
            dve.wait_ge(ct_in, 16)
            dve.tensor_scalar(esc[:], esc[:], 1.0, None, ALU.add).then_inc(siluc_step, 1)
            dve.wait_ge(siluc_step, 1)
            dve.reciprocal(rec[:], esc[:]).then_inc(siluc_step, 1)
            dve.wait_ge(siluc_step, 2)
            dve.tensor_tensor(siluc[:], ct[:], rec[:], ALU.mult).then_inc(siluc_step, 1)

            def statistics(q):
                tiles = range(q * TILES // 4, (q + 1) * TILES // 4)
                dve.wait_ge(x_in[q], 16)
                for t in tiles:
                    dve.bn_stats(stats[:, t, :], x[:, t, :]).then_inc(stat_step, 1)
                for t in tiles:
                    dve.wait_ge(stat_step, q * TILES // 2 + TILES // 4)
                    dve.bn_aggr(mv[:, t, :], stats[:, t, :]).then_inc(stat_step, 1)

            statistics(0)

            def normalise(b):
                dve.wait_ge(psT, HEAD + b)
                for t in range(TPB):
                    at = b * TPB + t
                    dve.tensor_scalar(z1[:, t, :], x[:, ds(at, 1), :].rearrange("p o d -> p (o d)"),
                                      mv[:, ds(at, 1), 0:1].rearrange("p o i -> p (o i)"), rstd[:, ds(at, 1)],
                                      ALU.subtract, ALU.mult).then_inc(z1_done, 1)

            def modulation_columns():
                dve.wait_ge(ps_cols, 1)
                dve.tensor_copy(sa[:].rearrange("p k b -> p (k b)"), bank[3][:, 0:KC * BATCH]).then_inc(cols_done, 1)
                dve.tensor_scalar(ca1[:].rearrange("p k b -> p (k b)"), bank[3][:, KC * BATCH:2 * KC * BATCH], 1.0, None,
                                  ALU.add).then_inc(cols_done, 1)
                dve.wait_ge(bqk_in, 16)
                dve.tensor_scalar(bqk[:, 0:2], bqk[:, 0:2], HDIM ** -0.5, None, ALU.mult).then_inc(cols_done, 1)

            def modulation_rows():
                dve.wait_ge(mod_raw, 3)
                for n, at in enumerate((2 * HID, 5 * HID)):
                    g = modr[:, at:at + HID]
                    dve.tensor_scalar(sgn[:, n, :], g, 0.0, 2.0, ALU.is_ge, ALU.mult).then_inc(floor_step, 1)
                    dve.tensor_scalar(minus[:, n, :], g, -1.0, 0.25, ALU.mult, ALU.max).then_inc(floor_step, 1)
                    dve.wait_ge(floor_step, 3 * n + 2)
                    dve.tensor_tensor(g, g, minus[:, n, :], ALU.max).then_inc(floor_step, 1)
                    dve.wait_ge(floor_step, 3 * n + 3)
                    dve.scalar_tensor_tensor(out=g, in0=sgn[:, n, :], scalar=-1.0, in1=g, op0=ALU.add, op1=ALU.mult
                                             ).then_inc(modr_done, 1)
                dve.tensor_scalar(modr[:, 4 * HID:5 * HID], modr[:, 4 * HID:5 * HID], 1.0, None, ALU.add).then_inc(modr_done, 1)

            def split(b):
                dve.wait_ge(q_evac, HEAD + (b + 1) * 2)
                dve.wait_ge(k_evac, (b + 1) * 2)
                dve.wait_ge(stored, DMA_HEAD + b * 32)
                dve.tensor_copy(qks[:, 0], qkf[:]).then_inc(split_hi, 1)
                dve.wait_ge(split_hi, HEAD + b + 1)
                dve.tensor_tensor(qks[:, 1], qkf[:], qks[:, 0].bitcast(F32), ALU.subtract).then_inc(split_lo, 1)

            def keep_v(b, par, vst_used=True):
                dve.wait_ge(psV, HEAD + b + 1)
                dve.wait_ge(psPV, HEAD + (b - 1) * 4 if vst_used else HEAD)
                for t in range(TPB):
                    dve.tensor_tensor(vst[par][:, t, :, 0:HDIM], MISC[1][:, t * HID:(t + 1) * HID].rearrange(
                        "p (h d) -> p h d", h=HEADS), bvb[:].rearrange("p (h d) -> p h d", h=HEADS), ALU.add
                                      ).then_inc(v_done, 1)

            def max_unit(b, u):
                pair, qt = u // 2, u % 2
                if u == 0:
                    dve.wait_ge(psM, HEAD + b * 2)
                dve.wait_ge(psMax, b * UNITS + (u + 1))
                dve.tensor_reduce(mx[:, qt, 2 * pair:2 * pair + 2], SM[qt][:].rearrange("p (h k) -> p h k", h=2),
                                  AX.X, ALU.max).then_inc(max_done, 1)

            def split_maxima(b):
                dve.wait_ge(mT_evac, HEAD + (b + 1) * 2)
                dve.wait_ge(mrow_in, DMA_HEAD + b * 32)
                dve.tensor_copy(mrow[:, 0, :], mneg[:]).then_inc(m_hi, 1)
                dve.wait_ge(m_hi, b + 1)
                dve.tensor_tensor(mrow[:, 1, :], mneg[:], mrow[:, 0, :].bitcast(F32), ALU.subtract).then_inc(m_lo, 1)

            def statistics2(b):
                dve.wait_ge(x1_done, HEAD + b + 1)
                first, last = b * TPB, (b + 1) * TPB
                for t in range(first, last):
                    dve.bn_stats(stats[:, t, :], x[:, t, :]).then_inc(stat2_step, 1)
                for t in range(first, last):
                    dve.wait_ge(stat2_step, first + last)
                    dve.bn_aggr(mv[:, t, :], stats[:, t, :]).then_inc(stat2_step, 1)

            def normalise2(b):
                dve.wait_ge(rstd2_done, 2 * b + 2)
                for t in range(b * TPB, (b + 1) * TPB):
                    dve.tensor_scalar(h2[:, t, :], x[:, t, :], mv[:, t, 0:1], rstd[:, t:t + 1],
                                      ALU.subtract, ALU.mult).then_inc(z2_done, 1)

            def weighed_by_sum(b):
                for qt in range(TPB):
                    dve.wait_ge(psOT, HEAD + b * 2 + (qt + 1))
                    heads = MISC[qt][:].rearrange("p (h d) -> p h d", h=HEADS)
                    dve.reciprocal(rs[:, qt, :], heads[:, :, HDIM]).then_inc(rs_done, 1)
                    dve.wait_ge(rs_done, b * 2 + (qt + 1))
                    if qt == 0:
                        dve.wait_ge(psOnT, HEAD + b)
                    dve.tensor_tensor(On[:, qt, :].rearrange("p (h d) -> p h d", h=HEADS), heads[:, :, 0:HDIM],
                                      rs[:, qt, :].rearrange("p (h o) -> p h o", o=1).to_broadcast((P, HEADS, HDIM)),
                                      ALU.mult).then_inc(on_done, 1)

            def keep_attention(b):
                dve.wait_ge(psWo, HEAD + b + 1)
                dve.wait_ge(x1_done, HEAD + b)
                dve.tensor_tensor(att[:], MISC[1][:].rearrange("p (t d) -> p t d", t=TPB),
                                  bob[:].rearrange("p (o d) -> p o d", o=1).to_broadcast((P, TPB, HID)), ALU.add
                                  ).then_inc(wo_evac, 1)

            dve.wait_ge(rstd_done, 1)
            normalise(0)
            modulation_columns()
            normalise(1)
            dve.memset(kst[0][0:STACK].bitcast(F32), 1.0).then_inc(stack_set, 1)
            statistics(1)
            split(0)
            dve.wait_ge(bias_in, 16 * 4)
            dve.wait_ge(stack_set, STACK_CONSTS)
            keep_v(0, 0, vst_used=False)
            dve.wait_ge(rstd_done, 2)
            normalise(2)
            split(1)
            keep_v(1, 1, vst_used=False)
            for u in range(UNITS):
                max_unit(0, u)
            split_maxima(0)

            for u in range(EARLY):
                max_unit(1, u)

            def residual(b):
                dve.wait_ge(modb_in[b % 2], (b // 2 + 1) * 16)
                dve.wait_ge(wo_evac, HEAD + b + 1)
                dve.tensor_tensor(att[:], att[:], modb[:, b:b + 1, 0, :].to_broadcast((P, TPB, HID)), ALU.mult).then_inc(ga_done, 1)
                dve.wait_ge(ga_done, b + 1)
                tiles = x[:, b * TPB:(b + 1) * TPB, :]
                dve.tensor_tensor(tiles, att[:], tiles, ALU.add).then_inc(x1_done, 1)

            def modulate2(b):
                tiles = h2[:, b * TPB:(b + 1) * TPB, :]
                dve.wait_ge(z2_done, TPB * (b + 1))
                dve.wait_ge(h2_done, b)
                dve.tensor_tensor(tiles, tiles, modb[:, b:b + 1, 2, :].to_broadcast((P, TPB, HID)), ALU.mult).then_inc(h2_step, 1)
                dve.wait_ge(h2_step, b + 1)
                dve.tensor_tensor(tiles, tiles, modb[:, b:b + 1, 1, :].to_broadcast((P, TPB, HID)), ALU.add).then_inc(h2_done, 1)

            def keep_turned(b):
                dve.wait_ge(psT2, b + 1)
                dve.tensor_copy(h2T(slice(0, KC), slice(b * SEQ, (b + 1) * SEQ)), SM[0][:].rearrange("p (k t) -> p k t", k=KC)).then_inc(h2T_done, 1)

            def keep_logits(b):
                dve.wait_ge(ps_r, b + 1)
                dve.tensor_copy(lg[:, b * TPB:(b + 1) * TPB, :], SM[1][:, 0:TPB * 2 * EXPERTS].rearrange("p (t e) -> p t e", t=TPB)
                                ).then_inc(r_evac, 1)

            def body(b, par, left, in_line):
                previous = not (in_line and b == 0)
                u = EARLY
                for h in range(HEADS):
                    if left == 0 and h == 0:
                        statistics2(LAST - 2)
                    if left == 0 and h == 3:
                        normalise2(LAST - 2)
                        modulate2(LAST - 2)
                    if left == 0 and h % 2 == 1 and h // 2 < ROUTED:
                        keep_turned(h // 2)
                    if left == 0 and h % 2 == 0 and 0 < h // 2 <= ROUTED:
                        keep_logits(h // 2 - 1)
                    if left >= 1:
                        for _ in range(UNITS_BEFORE[h]):
                            max_unit(b + 1, u)
                            u += 1
                    if not previous and h == 8:
                        statistics(2)
                        statistics(3)
                    if not previous and h == 11:
                        modulation_rows()
                    if h == 5 and left >= 2:
                        split(b + 2)
                    if h == 8 and previous:
                        weighed_by_sum(b - 1)
                    if h == 9 and left >= 1:
                        split_maxima(b + 1)
                    if h == 15 and previous:
                        keep_attention(b - 1)
                    if h == 11 and left >= 3:
                        if not previous:
                            dve.wait_ge(rstd_done, 3)
                        normalise(b + 3)
                if left >= 2:
                    for u in range(EARLY):
                        max_unit(b + 2, u)
                    keep_v(b + 2, par)
                if left > 0:
                    for done in second_norms(b, in_line):
                        statistics2(done)
                    for done in second_norms(b, in_line):
                        normalise2(done)

            batches(dve, body)

            residual(LAST - 1)
            statistics2(LAST - 1)
            weighed_by_sum(LAST)
            normalise2(LAST - 1)
            modulate2(LAST - 1)
            keep_attention(LAST)
            residual(LAST)
            statistics2(LAST)
            keep_turned(ROUTED)
            keep_logits(ROUTED)
            normalise2(LAST)
            modulate2(LAST)
            keep_turned(LAST)
            keep_logits(LAST)

            steps = [0]

            def step(ins):
                steps[0] += 1
                ins.then_inc(route_step, 1)
                dve.wait_ge(route_step, steps[0])

            def rows(v):
                return v[:].rearrange("p (t o) -> p t o", o=1).to_broadcast((P, TILES, EXPERTS))

            def cols(v):
                return v.rearrange("p (o e) -> p o e", o=1).to_broadcast((P, TILES, EXPERTS))

            gate, logit, prob, weight, tie, first_of, second_of = (r[:] for r in r3)
            biased = gate
            dve.memset(masks[:, TILES, :].bitcast(F32), 0.0).then_inc(masks_done, 1)
            dve.wait_ge(route_silu, 1)
            step(dve.tensor_tensor(logit, lg[:, :, 0:EXPERTS], gate, ALU.mult))
            step(dve.scalar_tensor_tensor(out=logit, in0=logit, scalar=-1.0, in1=logit, op0=ALU.mult, op1=ALU.max))
            step(dve.tensor_reduce(c1[0][:], logit, AX.X, ALU.max))
            step(dve.tensor_tensor(logit, logit, rows(c1[0]), ALU.subtract))
            dve.wait_ge(route_exp, 1)
            step(dve.tensor_reduce(c1[1][:], prob, AX.X, ALU.add))
            step(dve.reciprocal(c1[2][:], c1[1][:]))
            step(dve.tensor_tensor(prob, prob, rows(c1[2]), ALU.mult))
            step(dve.tensor_tensor(biased, prob, cols(ebias[:]), ALU.add))
            step(dve.tensor_tensor(weight, prob, cols(escale[:]), ALU.mult))
            step(dve.tensor_scalar(weight, weight, 1.0, None, ALU.add))
            dve.wait_ge(iota_step, 10)
            for onehot in (first_of, second_of):
                step(dve.tensor_reduce(c1[3][:], biased, AX.X, ALU.max))
                step(dve.tensor_tensor(tie, biased, rows(c1[3]), ALU.is_equal))
                step(dve.tensor_tensor(tie, tie, cols(iotaf[:]), ALU.mult))
                step(dve.tensor_reduce(c1[4][:], tie, AX.X, ALU.max))
                step(dve.tensor_tensor(onehot, tie, rows(c1[4]), ALU.is_equal))
                if onehot is first_of:
                    step(dve.scalar_tensor_tensor(out=biased, in0=onehot, scalar=-1e30, in1=biased, op0=ALU.mult, op1=ALU.add))
            dve.tensor_tensor(masks[:, 0:TILES, :], first_of, second_of, ALU.add).then_inc(masks_done, 1)
            step(dve.tensor_tensor(before[:], bnum[:, 0:EXPERTS + 1].rearrange("p (e o) -> p e o", o=1).to_broadcast((P, EXPERTS + 1, EXPERTS)),
                                   bnum[:, 0:EXPERTS].rearrange("p (o e) -> p o e", o=1).to_broadcast((P, EXPERTS + 1, EXPERTS)), ALU.is_gt))
            dve.wait_ge(ps_cnt, 1)
            step(dve.tensor_scalar(blk[:, 0, :], COUNTS[:, TILES * EXPERTS:(TILES + 1) * EXPERTS], float(P - 1), None, ALU.add))
            step(dve.tensor_copy(blki[:], blk[:, 0, :]))
            step(dve.tensor_scalar(blki[:], blki[:], 7, None, ALU.logical_shift_right))
            step(dve.tensor_copy(blk[:, 1, :], blki[:]))
            step(dve.tensor_tensor(ends, before[:], blk[:, 1:2, :].to_broadcast((P, EXPERTS + 1, EXPERTS)), ALU.mult))
            step(dve.tensor_reduce(cend[:], ends, AX.X, ALU.add))
            step(dve.tensor_scalar(blk[:, 2, :], cend[:, 0:EXPERTS], float(P), None, ALU.mult))
            step(dve.tensor_tensor(prob, COUNTS[:, 0:TILES * EXPERTS].rearrange("p (t e) -> p t e", e=EXPERTS), cols(blk[:, 2, :]), ALU.add))
            for choice, onehot in enumerate((first_of, second_of)):
                step(dve.tensor_tensor(tie, onehot, prob, ALU.mult))
                step(dve.tensor_reduce(slotf[:, choice, :], tie, AX.X, ALU.add))
            step(dve.tensor_copy(sloti[:], slotf[:]))
            step(dve.tensor_scalar(sloti[:], sloti[:], 7, None, ALU.logical_shift_right))
            step(dve.tensor_copy(slot_block[:], sloti[:]))
            step(dve.scalar_tensor_tensor(out=slot_pos[:], in0=slot_block[:], scalar=-float(P), in1=slotf[:], op0=ALU.mult, op1=ALU.add))
            dve.wait_ge(h2_out, 16 * BATCH)
            dve.wait_ge(ps_gu, 6)
            dve.wait_ge(iota_step, 10)
            for i in range(2 * TILES):
                c, t = i // TILES, i % TILES
                dve.tensor_scalar(in_block[:, i, :], bnum[:], slot_block[:, c, t:t + 1], destn[:, c, t:t + 1],
                                  ALU.is_equal, ALU.mult).then_inc(tables_done, 1)
                dve.tensor_scalar(at_pos[:, i, :], posn[:], slot_pos[:, c, t:t + 1], None, ALU.is_equal).then_inc(tables_done, 1)
            step(dve.tensor_tensor(bcmp[:], cend[:, 1:EXPERTS + 1].rearrange("p (o e) -> p o e", o=1).to_broadcast((P, BLOCKS, EXPERTS)),
                                   bnum[:, 0:BLOCKS].rearrange("p (b o) -> p b o", o=1).to_broadcast((P, BLOCKS, EXPERTS)), ALU.is_le))
            step(dve.tensor_reduce(eidf[:], bcmp[:], AX.X, ALU.add))
            step(dve.tensor_scalar(eidf[:], eidf[:], float(EXPERTS - 1), None, ALU.min))
            dve.tensor_copy(eid[:], eidf[:]).then_inc(slots_known, 1)
            for choice, onehot in enumerate((first_of, second_of)):
                step(dve.tensor_tensor(tie, onehot, weight, ALU.mult))
                step(dve.tensor_reduce(wsel[:, choice, :], tie, AX.X, ALU.add))
            dve.wait_ge(ps_table, 1)
            step(dve.tensor_scalar(tokf[:], TABLE[:, 0:BLOCKS], -1.0, 0.0, ALU.add, ALU.max))
            step(dve.tensor_copy(tok[:], tokf[:]))
            step(dve.scalar_tensor_tensor(out=destf[:], in0=TABLE[:, 0:BLOCKS], scalar=0.0, in1=padn[:], op0=ALU.is_equal, op1=ALU.mult))
            step(dve.tensor_tensor(destf[:], destf[:], TABLE[:, 0:BLOCKS], ALU.add))
            dve.tensor_copy(dest[:], destf[:]).then_inc(rows_known, 1)
            dve.tensor_scalar(tok[:], tok[:], T - 1, None, ALU.bitwise_and).then_inc(rows_known, 1)
            dve.wait_ge(ps_gu, 3 * CHUNKS)
            for u in range(2):
                dve.memset(hg[u][:], 0.0).then_inc(pads_done, 1)
            dve.wait_ge(z_evac, HEAD + 2 * (CHUNKS - 1))

            def product(n, u):
                dve.wait_ge(bsil_done, n + 1)
                dve.wait_ge(psProd, HEAD + n - 1)
                dve.tensor_tensor(hg[u][:, :, 0:HALF], bsil[u][:].rearrange("p (s n) -> p s n", s=2),
                                  GU[u][:, INTER:2 * INTER].rearrange("p (s n) -> p s n", s=2), ALU.mult
                                  ).then_inc(hg_done, 1)

            def gate_shared(b):
                z = zsh[:, ds(b * TPB, TPB), :]
                dve.tensor_tensor(z, z, modb[:, ds(b, 1), 3, :].to_broadcast((P, TPB, HID)), ALU.mult).then_inc(sum_step, 1)

            def add_shared(b):
                tiles = x[:, ds(b * TPB, TPB), :]
                dve.wait_ge(sum_step, b * 2 + 1)
                dve.tensor_tensor(tiles, tiles, zsh[:, ds(b * TPB, TPB), :], ALU.add).then_inc(sum_step, 1)

            product(0, 0)

            def body(n, r, left, batch):
                u = r % 2
                dve.wait_ge(psProd, HEAD + n + 1)
                dve.wait_ge(psOut, HEAD + n - 1)
                dve.tensor_copy(hgT[u][:], PROD[u][0:HPAD, 0:2 * P]).then_inc(hgT_done, 1)
                if left >= 1:
                    product(n + 1, 1 - u)
                if batch is not None and r == 1:
                    gate_shared(batch)
                if batch is not None and r == 3:
                    add_shared(batch)
                dve.wait_ge(psOut, HEAD + n + 1)
                if not (isinstance(n, int) and n < 4):
                    dve.wait_ge(ob_out[r], n * 4 - 4 * r)
                dve.tensor_copy(ob[r][:], OUT[u][:, 0:HID]).then_inc(ob_done, 1)

            blocks(dve, body)
            def add(t):
                dve.wait_ge(gated, t + 1)
                dve.tensor_tensor(x[:, t, :], x[:, t, :], picked[:, 1, t, :], ALU.add).then_inc(result_done, 1)

            for b in range(EARLY_SUMS, BATCH):
                dve.wait_ge(z_evac, HEAD + b + 1)
                gate_shared(b)
                add_shared(b)
            for t in range(TILES):
                dve.wait_ge(weighted, t + 1)
                dve.scalar_tensor_tensor(out=picked[:, 1, t, :], in0=picked[:, 1, t, :], scalar=wsel[:, 1, t:t + 1],
                                         in1=picked[:, 0, t, :], op0=ALU.mult, op1=ALU.add).then_inc(summed, 1)
                if t >= 2:
                    add(t - 2)
            add(TILES - 2)
            add(TILES - 1)

        @block.gpsimd
        def _(pool):
            pool.memset(ident[:], 0.0).then_inc(ident_step, 1)
            pool.wait_ge(ident_step, 1)
            pool.affine_select(out=ident[:], in_=ident[:], compare_op=ALU.not_equal, fill=1.0, base=0,
                               pattern=[[-1, P]], channel_multiplier=1).then_inc(ident_done, 1)
            pool.memset(neghalf[:], -0.5).then_inc(neghalf_set, 1)
            pool.memset(qst[0][0:MROW].bitcast(F32), 0.0).then_inc(stack_set, 1)

            def deviation(part, first, last):
                pool.wait_ge(stat_step, last * TILES // 2)
                tiles = slice(first * TILES // 4, last * TILES // 4)
                pool.tensor_scalar(rstd[:, tiles], mv[:, tiles, 1], EPS, None, ALU.add).then_inc(rstd_step, 1)
                pool.wait_ge(rstd_step, part)
                pool.tensor_tensor(rstd[:, tiles], rstd[:, tiles], neghalf[:, tiles], ALU.pow).then_inc(rstd_done, 1)

            pool.wait_ge(neghalf_set, 1)
            deviation(1, 0, 1)
            pool.memset(kst[1][0:STACK].bitcast(F32), 1.0).then_inc(stack_set, 1)
            for i in range(2):
                pool.memset(vst[i][:], 1.0).then_inc(stack_set, 1)
            pool.memset(qst[1][0:MROW].bitcast(F32), 0.0).then_inc(stack_set, 1)
            deviation(2, 1, 2)
            pool.wait_ge(stack_set, STACK_CONSTS)
            pool.wait_ge(stored, DMA_HEAD + 32)
            load_parts(pool, kst[0], 0, 1, (0, 0, 1), 1, first_keys_in[1])
            deviation(3, 2, 4)

            def residual(b, par):
                pool.wait_ge(modb_in[par], b * 8 + 16 - 8 * par)
                pool.wait_ge(wo_evac, HEAD + b + 1)
                pool.tensor_tensor(att[:], att[:], modb[:, ds(b, 1), 0, :].to_broadcast((P, TPB, HID)), ALU.mult
                                   ).then_inc(ga_done, 1)
                pool.wait_ge(ga_done, b + 1)
                tiles = x[:, ds(b * TPB, TPB), :]
                pool.tensor_tensor(tiles, att[:], tiles, ALU.add).then_inc(x1_done, 1)

            def deviation2(b):
                tiles = slice(b * TPB, (b + 1) * TPB)
                pool.wait_ge(stat2_step, 4 * (b + 1))
                pool.tensor_scalar(rstd[:, tiles], mv[:, tiles, 1], EPS, None, ALU.add).then_inc(rstd2_done, 1)
                pool.wait_ge(rstd2_done, 2 * b + 1)
                pool.tensor_tensor(rstd[:, tiles], rstd[:, tiles], neghalf[:, tiles], ALU.pow).then_inc(rstd2_done, 1)

            def modulate2(b):
                tiles = h2[:, b * TPB:(b + 1) * TPB, :]
                pool.wait_ge(z2_done, TPB * (b + 1))
                pool.tensor_tensor(tiles, tiles, modb[:, b:b + 1, 2, :].to_broadcast((P, TPB, HID)), ALU.mult
                                   ).then_inc(h2_step, 1)
                pool.wait_ge(h2_step, b + 1)
                pool.tensor_tensor(tiles, tiles, modb[:, b:b + 1, 1, :].to_broadcast((P, TPB, HID)), ALU.add
                                   ).then_inc(h2_done, 1)

            def body(b, par, left, in_line):
                if not (in_line and b == 0) and left >= 1:
                    residual(b - 1, 1 - par)
                for done in second_norms(b, in_line):
                    deviation2(done)
                for done in second_norms(b, in_line):
                    if done < LAST - 2:
                        modulate2(done)

            batches(pool, body)
            deviation2(LAST - 1)
            deviation2(LAST)
            pool.wait_ge(psWo, HEAD + BATCH)
            pool.wait_ge(x1_done, HEAD + BATCH)
            pool.iota(iotaf[:].bitcast(I32), pattern=[[-1, EXPERTS]], base=EXPERTS, channel_multiplier=0).then_inc(iota_step, 1)
            pool.iota(bnum[:].bitcast(I32), pattern=[[1, BLOCKS + 1]], base=0, channel_multiplier=0).then_inc(iota_step, 1)
            pool.iota(posn[:].bitcast(I32), pattern=[[1, P]], base=0, channel_multiplier=0).then_inc(iota_step, 1)
            pool.iota(destn[:].bitcast(I32), pattern=[[T, 2], [P, TILES]], base=1, channel_multiplier=1).then_inc(iota_step, 1)
            pool.memset(tri[:].bitcast(F32), 0.0).then_inc(tri_step, 1)
            pool.memset(ones[:].bitcast(F32), 1.0).then_inc(tri_step, 1)
            pool.iota(padn[:].bitcast(I32), pattern=[[P, BLOCKS]], base=1 + 2 * T, channel_multiplier=1).then_inc(iota_step, 1)
            pool.wait_ge(iota_step, 5)
            pool.wait_ge(tri_step, 2)
            for number in (iotaf, bnum, posn, destn, padn):
                pool.tensor_copy(number[:], number[:].bitcast(I32)).then_inc(iota_step, 1)
            pool.affine_select(out=tri[:], in_=tri[:].bitcast(F32), compare_op=ALU.is_ge, fill=1.0, base=0,
                               pattern=[[-1, P]], channel_multiplier=1).then_inc(tri_step, 1)
            for j in range(6):
                gate_times_up(pool, j)
            pool.wait_ge(sg_mul, 6)
            pool.memset(wd[64:HPAD], 0.0).then_inc(wd_pads_done, 1)
            pool.wait_ge(wd_pads_done, 1)
            for j in range(6, 12):
                gate_times_up(pool, j)
            pool.wait_ge(ps_gu, 3 * CHUNKS)
            pool.wait_ge(rows_known, 2)

            def gather(n):
                pool.indirect_dma_start(hb[n % 4][:], None, h2_rows, bass.IndirectOffsetOnAxis(ap=tok[:, n:n + 1], axis=0)
                                        ).then_inc(hb_in[n % 4], 16)

            for n in range(4):
                gather(n)
            for n in range(BLOCKS):
                if n + 4 < BLOCKS:
                    pool.wait_ge(psRows, n + 1)
                    gather(n + 4)
                pool.wait_ge(ob_done, HEAD + n + 1)
                pool.indirect_dma_start(chosen, bass.IndirectOffsetOnAxis(ap=dest[:, n:n + 1], axis=0), ob[n % 4][:], None
                                        ).then_inc(ob_out[n % 4], 16)
            for t in range(TILES):
                pool.wait_ge(summed, t + 1)
                pool.tensor_tensor(picked[:, 1, t, :], picked[:, 1, t, :], modb[:, t // TPB, 3, :], ALU.mult).then_inc(gated, 1)


def kernel(**inputs):
    import concourse.bacc as bacc
    from concourse.bass_utils import run_bass_kernel_spmd

    a = {n.replace("L0_", ""): np.asarray(v) for n, v in inputs.items()}
    arrays = host_layout(a)
    nc = bacc.Bacc("TRN2", target_bir_lowering=False, num_devices=1)
    args = [nc.dram_tensor(n, v.shape, mybir.dt.from_np(v.dtype), kind="ExternalInput").ap() for n, v in arrays.items()]
    out = nc.dram_tensor("out", (T, HID), F32, kind="ExternalOutput").ap()
    adaln_block(nc, *args, out)
    result = run_bass_kernel_spmd(nc, [arrays], core_ids=[0])
    return result.results[0]["out"].reshape(BATCH, SEQ, HID)


def host_layout(a):
    c = np.ascontiguousarray
    return {
        "in_x": c(a["attn_X"].reshape(T, HID)),
        "in_bqk": c(np.concatenate([a["attn_bq"], a["attn_bk"]]).reshape(2 * KC, P).T),
        "in_wq": a["attn_Wq"], "in_wk": a["attn_Wk"],
        "in_wv": a["attn_Wv"], "in_bv": a["attn_bv"], "in_wo": a["attn_Wo"], "in_bo": a["attn_bo"],
        "in_route": c(np.concatenate([a["ffn_cls_w"], a["ffn_gate_w"]]).T),
        "in_escale": a["ffn_extra_scale"], "in_ebias": a["ffn_extra_bias"],
        "in_wgu": c(np.concatenate([a["ffn_wg"], a["ffn_wu"]], axis=1).transpose(2, 0, 1)),
        "in_wd": c(a["ffn_wd"].transpose(0, 2, 1)),
        "in_sgu": c(np.concatenate([a["ffn_sg"], a["ffn_su"]]).T),
        "in_sd": c(a["ffn_sd"].T),
        "in_ct": c(a["c"].T), "in_wmod": a["wmod"],
    }
```
